# Optimizing a Trainium2 kernel written in Bass

```python
import numpy as np
import jax
import jax.numpy as jnp

def _softmax(x, axis=-1):
    return jax.nn.softmax(x, axis=axis)

def _gelu(x):
    return jax.nn.gelu(x, approximate=True)

def _silu(x):
    return jax.nn.silu(x)

def _sigmoid(x):
    return jax.nn.sigmoid(x)

def _layernorm(x, axis=-1, eps=1e-05):
    m = jnp.mean(x, axis=axis, keepdims=True)
    v = jnp.var(x, axis=axis, keepdims=True)
    return (x - m) / jnp.sqrt(v + eps)

def _scatter_add(tgt, idx, src, axis=0):
    return tgt.at[idx].add(src)

def _segment_sum(src, seg, n):
    return jax.ops.segment_sum(src, seg, n)
kernel_name = 'mk_xattn_ffn_d4_seqx_r8_3d7530'

def setup_inputs(seed: int=0):
    np.random.seed(seed)
    _w = jnp.asarray

    def _rec_inputs():
        import jax
        import jax.numpy as jnp
        _rk = jax.random.key(seed)
        x = -0.0002928 + 1 * jax.random.normal(jax.random.fold_in(_rk, 1), (64, 64, 128), jnp.float32)
        _lenS = 64 - jax.random.randint(jax.random.fold_in(_rk, 7), (64,), 0, max(1, 64 // 4) + 1, jnp.int32)
        _lenS2 = 64 - jax.random.randint(jax.random.fold_in(_rk, 8), (64,), 0, max(1, 64 // 4) + 1, jnp.int32)
        _ctx_1024P = jax.random.normal(jax.random.fold_in(_rk, 11), (64, 16, 128), jnp.float32)
        _ctx_1024c = jax.random.dirichlet(jax.random.fold_in(_rk, 511), 0.3 * jnp.ones((16,), jnp.float32), (64, 64))
        _ctx_1024t = jnp.einsum('bsk,bkd->bsd', _ctx_1024c, _ctx_1024P)
        _ctx_1024t = _ctx_1024t * jax.lax.rsqrt(jnp.mean(jnp.square(_ctx_1024t)) + 1e-12) * 0.953939
        ctx_1024 = -1.39393e-06 + 0.999914 * (_ctx_1024t + 0.3 * jax.random.normal(jax.random.fold_in(_rk, 611), (64, 64, 128), jnp.float32))
        return (x, ctx_1024)
    x, ctx_1024 = _rec_inputs()

    def _L0_xattn_setup():
        import jax, jax.numpy as jnp
        import numpy as np
        D_MODEL = 128
        N_HEAD = 16

        def _split(x, n_head):
            B, S, D = x.shape
            return x.reshape(B, S, n_head, D // n_head).transpose(0, 2, 1, 3)
        key = jax.random.key(seed)
        ks = jax.random.split(key, 11)
        B, S, D = (2, 256, D_MODEL)
        s = 1.0 / np.sqrt(D)
        inp = {'q': jax.random.normal(ks[0], (B, S, D), jnp.float32), 'k': jax.random.normal(ks[1], (B, S, D), jnp.float32), 'v': jax.random.normal(ks[2], (B, S, D), jnp.float32), 'Wq': jax.random.normal(ks[3], (D, D), jnp.float32) * s, 'bq': jnp.zeros((D,), jnp.float32), 'Wk': jax.random.normal(ks[4], (D, D), jnp.float32) * s, 'bk': jnp.zeros((D,), jnp.float32), 'Wv': jax.random.normal(ks[5], (D, D), jnp.float32) * s, 'bv': jnp.zeros((D,), jnp.float32), 'Wo': jax.random.normal(ks[6], (D, D), jnp.float32) * s, 'bo': jnp.zeros((D,), jnp.float32)}
        return inp
    _L0_xattn_all = _L0_xattn_setup()
    _L0_xattn_in = {k: v for k, v in _L0_xattn_all.items() if k in ('Wq', 'bq', 'Wk', 'bk', 'Wv', 'bv', 'Wo', 'bo')}
    del _L0_xattn_all

    def _L0_ffn_setup():
        import jax, jax.numpy as jnp
        import numpy as np
        TOP_K = 2
        key = jax.random.key(seed)
        ks = jax.random.split(key, 5)
        B, N, C, FF, E = (2, 256, 128, 512, 8)
        x = jax.random.normal(ks[0], (B, N, C), dtype=jnp.float32)
        router_w = jax.random.normal(ks[1], (E, C), dtype=jnp.float32) * 0.02
        lim1 = np.sqrt(6.0 / (FF + C))
        expert_w1 = jax.random.uniform(ks[2], (E, FF, C), dtype=jnp.float32, minval=-lim1, maxval=lim1)
        expert_b1 = jnp.zeros((E, FF), dtype=jnp.float32)
        expert_w2 = jax.random.uniform(ks[3], (E, C, FF), dtype=jnp.float32, minval=-lim1, maxval=lim1)
        expert_b2 = jnp.zeros((E, C), dtype=jnp.float32)
        return {'x': x, 'router_w': router_w, 'expert_w1': expert_w1, 'expert_b1': expert_b1, 'expert_w2': expert_w2, 'expert_b2': expert_b2}
    _L0_ffn_all = _L0_ffn_setup()
    _L0_ffn_in = {k: v for k, v in _L0_ffn_all.items() if k in ('router_w', 'expert_w1', 'expert_b1', 'expert_w2', 'expert_b2')}
    del _L0_ffn_all

    def _L1_xattn_setup():
        import jax, jax.numpy as jnp
        import numpy as np
        C = 128
        B, SQ, SKV = (4, 256, 256)
        key = jax.random.key(seed)
        ks = jax.random.split(key, 10)
        s = 1.0 / np.sqrt(C)
        return {'x': jax.random.normal(ks[0], (B, SQ, C), jnp.float32), 'content_embeddings': jax.random.normal(ks[1], (B, SKV, C), jnp.float32), 'Wq': jax.random.normal(ks[2], (C, C), jnp.float32) * s, 'bq': jnp.zeros((C,), jnp.float32), 'Wk': jax.random.normal(ks[3], (C, C), jnp.float32) * s, 'bk': jnp.zeros((C,), jnp.float32), 'Wv': jax.random.normal(ks[4], (C, C), jnp.float32) * s, 'bv': jnp.zeros((C,), jnp.float32), 'Wo': jax.random.normal(ks[5], (C, C), jnp.float32) * s, 'bo': jnp.zeros((C,), jnp.float32)}
    _L1_xattn_all = _L1_xattn_setup()
    _L1_xattn_in = {k: v for k, v in _L1_xattn_all.items() if k in ('Wq', 'bq', 'Wk', 'bk', 'Wv', 'bv', 'Wo', 'bo')}
    del _L1_xattn_all

    def _L1_ffn_setup():
        import math
        import jax, jax.numpy as jnp
        import numpy as np
        NUM_EXPERTS = 16
        TOP_K = 2
        CAPACITY_FACTOR = 1.25
        key = jax.random.key(seed)
        k1, k2, k3, k4 = jax.random.split(key, 4)
        d, dff, E = (128, 512, NUM_EXPERTS)
        x = jax.random.normal(k1, (4, 256, d), dtype=jnp.float32)
        router_w = jax.random.normal(k2, (E, d), dtype=jnp.float32) * d ** (-0.5)
        router_b = jnp.zeros((E,), dtype=jnp.float32)
        w1 = jax.random.normal(k3, (E, d, dff), dtype=jnp.float32) * 0.02
        b1 = jnp.zeros((E, dff), dtype=jnp.float32)
        w2 = jax.random.normal(k4, (E, dff, d), dtype=jnp.float32) * 0.02
        b2 = jnp.zeros((E, d), dtype=jnp.float32)
        return {'x': x, 'router_w': router_w, 'router_b': router_b, 'w1': w1, 'b1': b1, 'w2': w2, 'b2': b2}
    _L1_ffn_all = _L1_ffn_setup()
    _L1_ffn_in = {k: v for k, v in _L1_ffn_all.items() if k in ('router_w', 'router_b', 'w1', 'b1', 'w2', 'b2')}
    del _L1_ffn_all

    def _L2_xattn_setup():
        import jax, jax.numpy as jnp
        import numpy as np
        B, S, E, NH = (1, 256, 128, 8)
        DH = E // NH
        EPS = 1e-06
        LN_EPS = 1e-05
        key = jax.random.key(seed)
        ks = jax.random.split(key, 8)
        q = jax.random.normal(ks[0], (B, S, E), dtype=jnp.float32)
        k = jax.random.normal(ks[1], (B, S, E), dtype=jnp.float32)
        v = jax.random.normal(ks[2], (B, S, E), dtype=jnp.float32)
        scale = 1.0 / np.sqrt(3 * E)
        igate_w = jax.random.normal(ks[3], (NH, 3 * E), dtype=jnp.float32) * scale
        igate_b = jax.random.normal(ks[4], (NH,), dtype=jnp.float32) * 0.1
        fgate_w = jax.random.normal(ks[5], (NH, 3 * E), dtype=jnp.float32) * scale
        fgate_b = jnp.linspace(3.0, 6.0, NH, dtype=jnp.float32)
        out_w = 1.0 + 0.1 * jax.random.normal(ks[6], (E,), dtype=jnp.float32)
        return {'q': q, 'k': k, 'v': v, 'igate_w': igate_w, 'igate_b': igate_b, 'fgate_w': fgate_w, 'fgate_b': fgate_b, 'out_w': out_w}
    _L2_xattn_all = _L2_xattn_setup()
    _L2_xattn_in = {k: v for k, v in _L2_xattn_all.items() if k in ('igate_w', 'igate_b', 'fgate_w', 'fgate_b', 'out_w')}
    del _L2_xattn_all

    def _L2_ffn_setup():
        import jax, jax.numpy as jnp
        import numpy as np
        E = 8
        TOP_K = 2
        CAP_FACTOR = 1.25
        MIN_CAP = 4
        SCORE_SCALE = 1.0

        def _ffn(x, w1, b1, w2, b2):
            return jax.nn.gelu(x @ w1 + b1, approximate=False) @ w2 + b2
        key = jax.random.key(seed)
        ks = jax.random.split(key, 6)
        B, S, D, I = (4, 256, 128, 512)
        std = 0.02
        return {'x': jax.random.normal(ks[0], (B, S, D), jnp.float32), 'Wr': jax.random.normal(ks[1], (E, D), jnp.float32) * std, 'W1': jax.random.normal(ks[2], (E, D, I), jnp.float32) * std, 'b1': jnp.zeros((E, I), jnp.float32), 'W2': jax.random.normal(ks[3], (E, I, D), jnp.float32) * std, 'b2': jnp.zeros((E, D), jnp.float32), 'fw1': jax.random.normal(ks[4], (D, I), jnp.float32) * std, 'fb1': jnp.zeros((I,), jnp.float32), 'fw2': jax.random.normal(ks[5], (I, D), jnp.float32) * std, 'fb2': jnp.zeros((D,), jnp.float32)}
    _L2_ffn_all = _L2_ffn_setup()
    _L2_ffn_in = {k: v for k, v in _L2_ffn_all.items() if k in ('Wr', 'W1', 'b1', 'W2', 'b2', 'fw1', 'fb1', 'fw2', 'fb2')}
    del _L2_ffn_all

    def _L3_xattn_setup():
        import jax, jax.numpy as jnp
        import numpy as np
        D_MODEL = 128
        N_HEADS = 16
        D_K = D_MODEL // N_HEADS
        SCALE = float(np.sqrt(D_K))
        key = jax.random.key(seed)
        ks = jax.random.split(key, 11)
        B, L, D = (2, 256, D_MODEL)
        s = 1.0 / np.sqrt(D)
        inp = {'q': jax.random.normal(ks[0], (B, L, D), dtype=jnp.float32), 'k': jax.random.normal(ks[1], (B, L, D), dtype=jnp.float32), 'v': jax.random.normal(ks[2], (B, L, D), dtype=jnp.float32), 'Wq': jax.random.normal(ks[3], (D, D), dtype=jnp.float32) * s, 'bq': jnp.zeros((D,), dtype=jnp.float32), 'Wk': jax.random.normal(ks[4], (D, D), dtype=jnp.float32) * s, 'bk': jnp.zeros((D,), dtype=jnp.float32), 'Wv': jax.random.normal(ks[5], (D, D), dtype=jnp.float32) * s, 'bv': jnp.zeros((D,), dtype=jnp.float32), 'Wo': jax.random.normal(ks[6], (D, D), dtype=jnp.float32) * s, 'bo': jnp.zeros((D,), dtype=jnp.float32)}
        return inp
    _L3_xattn_all = _L3_xattn_setup()
    _L3_xattn_in = {k: v for k, v in _L3_xattn_all.items() if k in ('Wq', 'bq', 'Wk', 'bk', 'Wv', 'bv', 'Wo', 'bo')}
    del _L3_xattn_all

    def _L3_ffn_setup():
        import jax, jax.numpy as jnp
        import numpy as np
        B, S, D_MODEL, D_HIDDEN = (4, 256, 128, 512)

        def act_quant(x):
            scale = 127.0 / jnp.clip(jnp.max(jnp.abs(x), axis=-1, keepdims=True), 1e-05)
            return jnp.clip(jnp.round(x * scale), -128, 127) / scale

        def weight_quant(w):
            scale = 1.0 / jnp.clip(jnp.mean(jnp.abs(w)), 1e-05)
            return jnp.clip(jnp.round(w * scale), -1, 1) / scale

        def bit_linear(x, w):
            xq = x + jax.lax.stop_gradient(act_quant(x) - x)
            wq = w + jax.lax.stop_gradient(weight_quant(w) - w)
            return jnp.einsum('bsd,hd->bsh', xq, wq)

        def depthwise_conv1d(x_bcl, w, b):
            y = jax.lax.conv_general_dilated(x_bcl, w, window_strides=(1,), padding=[(1, 1)], dimension_numbers=('NCH', 'OIH', 'NCH'), feature_group_count=x_bcl.shape[1])
            return y + b[None, :, None]
        key = jax.random.key(seed)
        ks = jax.random.split(key, 5)
        lim1 = 1.0 / np.sqrt(D_MODEL)
        lim2 = 1.0 / np.sqrt(D_HIDDEN)
        limc = 1.0 / np.sqrt(3.0)
        return {'x': jax.random.normal(ks[0], (B, S, D_MODEL), dtype=jnp.float32), 'w1': jax.random.uniform(ks[1], (D_HIDDEN, D_MODEL), jnp.float32, -lim1, lim1), 'conv_w': jax.random.uniform(ks[2], (D_HIDDEN, 1, 3), jnp.float32, -limc, limc), 'conv_b': jax.random.uniform(ks[3], (D_HIDDEN,), jnp.float32, -limc, limc), 'w2': jax.random.uniform(ks[4], (D_MODEL, D_HIDDEN), jnp.float32, -lim2, lim2)}
    _L3_ffn_all = _L3_ffn_setup()
    _L3_ffn_in = {k: v for k, v in _L3_ffn_all.items() if k in ('w1', 'conv_w', 'conv_b', 'w2')}
    del _L3_ffn_all
    return {'x': x, 'ctx_1024': ctx_1024, 'L0_xattn_Wq': _L0_xattn_in['Wq'], 'L0_xattn_bq': _L0_xattn_in['bq'], 'L0_xattn_Wk': _L0_xattn_in['Wk'], 'L0_xattn_bk': _L0_xattn_in['bk'], 'L0_xattn_Wv': _L0_xattn_in['Wv'], 'L0_xattn_bv': _L0_xattn_in['bv'], 'L0_xattn_Wo': _L0_xattn_in['Wo'], 'L0_xattn_bo': _L0_xattn_in['bo'], 'L0_ffn_router_w': _L0_ffn_in['router_w'], 'L0_ffn_expert_w1': _L0_ffn_in['expert_w1'], 'L0_ffn_expert_b1': _L0_ffn_in['expert_b1'], 'L0_ffn_expert_w2': _L0_ffn_in['expert_w2'], 'L0_ffn_expert_b2': _L0_ffn_in['expert_b2'], 'L1_xattn_Wq': _L1_xattn_in['Wq'], 'L1_xattn_bq': _L1_xattn_in['bq'], 'L1_xattn_Wk': _L1_xattn_in['Wk'], 'L1_xattn_bk': _L1_xattn_in['bk'], 'L1_xattn_Wv': _L1_xattn_in['Wv'], 'L1_xattn_bv': _L1_xattn_in['bv'], 'L1_xattn_Wo': _L1_xattn_in['Wo'], 'L1_xattn_bo': _L1_xattn_in['bo'], 'L1_ffn_router_w': _L1_ffn_in['router_w'], 'L1_ffn_router_b': _L1_ffn_in['router_b'], 'L1_ffn_w1': _L1_ffn_in['w1'], 'L1_ffn_b1': _L1_ffn_in['b1'], 'L1_ffn_w2': _L1_ffn_in['w2'], 'L1_ffn_b2': _L1_ffn_in['b2'], 'L2_xattn_igate_w': _L2_xattn_in['igate_w'], 'L2_xattn_igate_b': _L2_xattn_in['igate_b'], 'L2_xattn_fgate_w': _L2_xattn_in['fgate_w'], 'L2_xattn_fgate_b': _L2_xattn_in['fgate_b'], 'L2_xattn_out_w': _L2_xattn_in['out_w'], 'L2_ffn_Wr': _L2_ffn_in['Wr'], 'L2_ffn_W1': _L2_ffn_in['W1'], 'L2_ffn_b1': _L2_ffn_in['b1'], 'L2_ffn_W2': _L2_ffn_in['W2'], 'L2_ffn_b2': _L2_ffn_in['b2'], 'L2_ffn_fw1': _L2_ffn_in['fw1'], 'L2_ffn_fb1': _L2_ffn_in['fb1'], 'L2_ffn_fw2': _L2_ffn_in['fw2'], 'L2_ffn_fb2': _L2_ffn_in['fb2'], 'L3_xattn_Wq': _L3_xattn_in['Wq'], 'L3_xattn_bq': _L3_xattn_in['bq'], 'L3_xattn_Wk': _L3_xattn_in['Wk'], 'L3_xattn_bk': _L3_xattn_in['bk'], 'L3_xattn_Wv': _L3_xattn_in['Wv'], 'L3_xattn_bv': _L3_xattn_in['bv'], 'L3_xattn_Wo': _L3_xattn_in['Wo'], 'L3_xattn_bo': _L3_xattn_in['bo'], 'L3_ffn_w1': _L3_ffn_in['w1'], 'L3_ffn_conv_w': _L3_ffn_in['conv_w'], 'L3_ffn_conv_b': _L3_ffn_in['conv_b'], 'L3_ffn_w2': _L3_ffn_in['w2']}

def reference(x, ctx_1024, L0_xattn_Wq, L0_xattn_bq, L0_xattn_Wk, L0_xattn_bk, L0_xattn_Wv, L0_xattn_bv, L0_xattn_Wo, L0_xattn_bo, L0_ffn_router_w, L0_ffn_expert_w1, L0_ffn_expert_b1, L0_ffn_expert_w2, L0_ffn_expert_b2, L1_xattn_Wq, L1_xattn_bq, L1_xattn_Wk, L1_xattn_bk, L1_xattn_Wv, L1_xattn_bv, L1_xattn_Wo, L1_xattn_bo, L1_ffn_router_w, L1_ffn_router_b, L1_ffn_w1, L1_ffn_b1, L1_ffn_w2, L1_ffn_b2, L2_xattn_igate_w, L2_xattn_igate_b, L2_xattn_fgate_w, L2_xattn_fgate_b, L2_xattn_out_w, L2_ffn_Wr, L2_ffn_W1, L2_ffn_b1, L2_ffn_W2, L2_ffn_b2, L2_ffn_fw1, L2_ffn_fb1, L2_ffn_fw2, L2_ffn_fb2, L3_xattn_Wq, L3_xattn_bq, L3_xattn_Wk, L3_xattn_bk, L3_xattn_Wv, L3_xattn_bv, L3_xattn_Wo, L3_xattn_bo, L3_ffn_w1, L3_ffn_conv_w, L3_ffn_conv_b, L3_ffn_w2):
    import jax
    import jax.numpy as jnp

    def _L0_xattn_ref(q, k, v, Wq, bq, Wk, bk, Wv, bv, Wo, bo):
        import jax, jax.numpy as jnp
        import numpy as np
        D_MODEL = 128
        N_HEAD = 16

        def _split(x, n_head):
            B, S, D = x.shape
            return x.reshape(B, S, n_head, D // n_head).transpose(0, 2, 1, 3)
        qh = _split(q @ Wq.T + bq, N_HEAD)
        kh = _split(k @ Wk.T + bk, N_HEAD)
        vh = _split(v @ Wv.T + bv, N_HEAD)
        d_tensor = qh.shape[-1]
        score = jnp.einsum('bhqd,bhkd->bhqk', qh, kh) / jnp.sqrt(jnp.float32(d_tensor))
        attn = jax.nn.softmax(score, axis=-1)
        out = jnp.einsum('bhqk,bhkd->bhqd', attn, vh)
        B, H, S, dh = out.shape
        out = out.transpose(0, 2, 1, 3).reshape(B, S, H * dh)
        return out @ Wo.T + bo

    def _L0_ffn_ref(x, router_w, expert_w1, expert_b1, expert_w2, expert_b2):
        import jax, jax.numpy as jnp
        import numpy as np
        TOP_K = 2
        router_logits = jnp.einsum('bnc,ec->bne', x, router_w)
        router_probs = jax.nn.softmax(router_logits, axis=-1)
        expert_weights, expert_idx = jax.lax.top_k(router_probs, TOP_K)
        expert_weights = expert_weights / (expert_weights.sum(axis=-1, keepdims=True) + 1e-09)
        h = jnp.einsum('bnc,efc->bnef', x, expert_w1) + expert_b1
        h = jax.nn.gelu(h, approximate=False)
        out_all = jnp.einsum('bnef,ecf->bnec', h, expert_w2) + expert_b2
        out_k = jnp.take_along_axis(out_all, expert_idx[..., None], axis=2)
        return (out_k * expert_weights[..., None]).sum(axis=2)

    def _L1_xattn_ref(x, content_embeddings, Wq, bq, Wk, bk, Wv, bv, Wo, bo):
        import jax, jax.numpy as jnp
        import numpy as np
        C = 128
        B, SQ, SKV = (4, 256, 256)
        queries = x @ Wq.T + bq
        keys = content_embeddings @ Wk.T + bk
        values = content_embeddings @ Wv.T + bv
        scale = 1.0 / jnp.sqrt(jnp.asarray(C, x.dtype))
        scores = jnp.einsum('bqc,bkc->bqk', queries, keys) * scale
        attn = jax.nn.softmax(scores, axis=-1)
        attended = jnp.einsum('bqk,bkc->bqc', attn, values)
        out = x + attended
        return out @ Wo.T + bo

    def _L1_ffn_ref(x, router_w, router_b, w1, b1, w2, b2):
        import math
        import jax, jax.numpy as jnp
        import numpy as np
        NUM_EXPERTS = 16
        TOP_K = 2
        CAPACITY_FACTOR = 1.25
        E, k = (NUM_EXPERTS, TOP_K)
        B, S, d = x.shape
        tokens = B * S
        capacity = max(1, int(math.ceil(CAPACITY_FACTOR * tokens * k / E)))
        x2d = x.reshape(tokens, d)
        logits = x2d @ router_w.T + router_b
        vals, idx = jax.lax.top_k(logits, k)
        gates = jax.nn.softmax(vals, axis=-1)
        flat_e = idx.reshape(-1)
        oh = (flat_e[:, None] == jnp.arange(E)[None, :]).astype(jnp.int32)
        pos = jnp.take_along_axis(jnp.cumsum(oh, axis=0) - 1, flat_e[:, None], axis=1)[:, 0]
        kept = pos < capacity
        kept2 = kept.reshape(tokens, k)
        denom = jnp.sum(gates * kept2, axis=-1, keepdims=True)
        gates = jnp.where(kept2, gates / (denom + 1e-09), 0.0)
        slot = flat_e * capacity + pos
        slot_safe = jnp.where(kept, slot, E * capacity)
        x_rep = jnp.repeat(x2d, k, axis=0)
        buf = jnp.zeros((E * capacity + 1, d), x.dtype).at[slot_safe].set(x_rep)
        packed = buf[:E * capacity].reshape(E, capacity, d)
        h = jax.nn.gelu(jnp.einsum('ecd,edf->ecf', packed, w1) + b1[:, None, :], approximate=False)
        expert_out = jnp.einsum('ecf,efd->ecd', h, w2) + b2[:, None, :]
        eflat = expert_out.reshape(E * capacity, d)
        gathered = eflat[jnp.clip(slot, 0, E * capacity - 1)]
        w = (gates.reshape(-1) * kept.astype(x.dtype))[:, None]
        out = (gathered * w).reshape(tokens, k, d).sum(axis=1)
        return out.reshape(B, S, d)

    def _L2_xattn_ref(q, k, v, igate_w, igate_b, fgate_w, fgate_b, out_w):
        import jax, jax.numpy as jnp
        import numpy as np
        B, S, E, NH = (1, 256, 128, 8)
        DH = E // NH
        EPS = 1e-06
        LN_EPS = 1e-05
        Bq, Sq, Eq = q.shape
        nh = igate_b.shape[0]
        dh = Eq // nh
        gi = jnp.concatenate([q, k, v], axis=-1)
        ig = (gi @ igate_w.T + igate_b).transpose(0, 2, 1)
        fg = (gi @ fgate_w.T + fgate_b).transpose(0, 2, 1)
        qh = q.reshape(Bq, Sq, nh, dh).transpose(0, 2, 1, 3)
        kh = k.reshape(Bq, Sq, nh, dh).transpose(0, 2, 1, 3)
        vh = v.reshape(Bq, Sq, nh, dh).transpose(0, 2, 1, 3)
        log_f = jax.nn.log_sigmoid(fg)
        cs = jnp.cumsum(log_f, axis=-1)
        diff = cs[..., :, None] - cs[..., None, :]
        mask = jnp.tril(jnp.ones((Sq, Sq), dtype=bool))
        log_fg_mat = jnp.where(mask, diff, -jnp.inf)
        log_D = log_fg_mat + ig[..., None, :]
        max_log_D = jnp.max(log_D, axis=-1, keepdims=True)
        D = jnp.exp(log_D - max_log_D)
        qk = jnp.einsum('bhsd,bhtd->bhst', qh, kh) / jnp.sqrt(jnp.float32(dh))
        C = qk * D
        normalizer = jnp.maximum(jnp.abs(C.sum(-1, keepdims=True)), jnp.exp(-max_log_D))
        h = jnp.einsum('bhst,bhtd->bhsd', C / (normalizer + EPS), vh)
        mean = h.mean(-1, keepdims=True)
        var = ((h - mean) ** 2).mean(-1, keepdims=True)
        hn = (h - mean) / jnp.sqrt(var + LN_EPS)
        hn = hn * out_w.reshape(nh, dh)[None, :, None, :]
        return hn.transpose(0, 2, 1, 3).reshape(Bq, Sq, Eq)

    def _L2_ffn_ref(x, Wr, W1, b1, W2, b2, fw1, fb1, fw2, fb2):
        import jax, jax.numpy as jnp
        import numpy as np
        E = 8
        TOP_K = 2
        CAP_FACTOR = 1.25
        MIN_CAP = 4
        SCORE_SCALE = 1.0

        def _ffn(x, w1, b1, w2, b2):
            return jax.nn.gelu(x @ w1 + b1, approximate=False) @ w2 + b2
        B, S, D = x.shape
        T = B * S
        x_flat = x.reshape(T, D)
        logits = x_flat @ Wr.T * SCORE_SCALE
        probs = jax.nn.softmax(logits, axis=-1)
        topk_scores, topk_experts = jax.lax.top_k(probs, TOP_K)
        topk_scores = topk_scores / jnp.clip(topk_scores.sum(-1, keepdims=True), 1e-09, None)
        cap = max(int(CAP_FACTOR * (T * TOP_K / E)), MIN_CAP)
        y_fb = _ffn(x_flat, fw1, fb1, fw2, fb2)
        y_flat = jnp.zeros_like(x_flat)
        fallback = jnp.zeros((T,), bool)
        tok_ids = jnp.arange(T, dtype=jnp.int32)
        for e in range(E):
            match = topk_experts == e
            elig = match.any(-1) & ~fallback
            pos = jnp.cumsum(elig) - 1
            kept = elig & (pos < cap)
            overflow = elig & (pos >= cap)
            slot = jnp.where(kept, pos, cap)
            buf = jnp.zeros((cap + 1,), jnp.int32).at[slot].set(tok_ids)
            vmask = jnp.zeros((cap + 1,), bool).at[slot].set(kept)
            idx = buf[:cap]
            valid = vmask[:cap]
            x_e = x_flat[idx]
            y_e = _ffn(x_e, W1[e], b1[e], W2[e], b2[e])
            w_tok = (topk_scores * match).sum(-1)
            w = jnp.where(valid, w_tok[idx], 0.0)
            y_flat = y_flat.at[idx].add(y_e * w[:, None])
            y_flat = jnp.where(overflow[:, None], y_fb, y_flat)
            fallback = fallback | overflow
        return y_flat.reshape(B, S, D)

    def _L3_xattn_ref(q, k, v, Wq, bq, Wk, bk, Wv, bv, Wo, bo):
        import jax, jax.numpy as jnp
        import numpy as np
        D_MODEL = 128
        N_HEADS = 16
        D_K = D_MODEL // N_HEADS
        SCALE = float(np.sqrt(D_K))
        B, L, D = q.shape
        H, Dk = (N_HEADS, D_K)

        def proj(x, W, b):
            y = x @ W + b
            return y.reshape(B, -1, H, Dk).transpose(0, 2, 1, 3)
        qh = proj(q, Wq, bq)
        kh = proj(k, Wk, bk)
        vh = proj(v, Wv, bv)
        scores = jnp.einsum('bhqd,bhkd->bhqk', qh, kh) / SCALE
        attn = jax.nn.softmax(scores, axis=-1)
        out = jnp.einsum('bhqk,bhkd->bhqd', attn, vh)
        out = out.transpose(0, 2, 1, 3).reshape(B, -1, D)
        return out @ Wo + bo

    def _L3_ffn_ref(x, w1, conv_w, conv_b, w2):
        import jax, jax.numpy as jnp
        import numpy as np
        B, S, D_MODEL, D_HIDDEN = (4, 256, 128, 512)

        def act_quant(x):
            scale = 127.0 / jnp.clip(jnp.max(jnp.abs(x), axis=-1, keepdims=True), 1e-05)
            return jnp.clip(jnp.round(x * scale), -128, 127) / scale

        def weight_quant(w):
            scale = 1.0 / jnp.clip(jnp.mean(jnp.abs(w)), 1e-05)
            return jnp.clip(jnp.round(w * scale), -1, 1) / scale

        def bit_linear(x, w):
            xq = x + jax.lax.stop_gradient(act_quant(x) - x)
            wq = w + jax.lax.stop_gradient(weight_quant(w) - w)
            return jnp.einsum('bsd,hd->bsh', xq, wq)

        def depthwise_conv1d(x_bcl, w, b):
            y = jax.lax.conv_general_dilated(x_bcl, w, window_strides=(1,), padding=[(1, 1)], dimension_numbers=('NCH', 'OIH', 'NCH'), feature_group_count=x_bcl.shape[1])
            return y + b[None, :, None]
        h = bit_linear(x, w1)
        h = depthwise_conv1d(h.transpose(0, 2, 1), conv_w, conv_b)
        h = h.transpose(0, 2, 1)
        h = jax.nn.silu(h)
        return bit_linear(h, w2)
    x = x + _L0_xattn_ref(_layernorm(x, axis=-1), ctx_1024, ctx_1024, L0_xattn_Wq, L0_xattn_bq, L0_xattn_Wk, L0_xattn_bk, L0_xattn_Wv, L0_xattn_bv, L0_xattn_Wo, L0_xattn_bo)
    x = x + _L0_ffn_ref(_layernorm(x, axis=-1), L0_ffn_router_w, L0_ffn_expert_w1, L0_ffn_expert_b1, L0_ffn_expert_w2, L0_ffn_expert_b2)
    x = x + _L1_xattn_ref(_layernorm(x, axis=-1), ctx_1024, L1_xattn_Wq, L1_xattn_bq, L1_xattn_Wk, L1_xattn_bk, L1_xattn_Wv, L1_xattn_bv, L1_xattn_Wo, L1_xattn_bo)
    x = x + _L1_ffn_ref(_layernorm(x, axis=-1), L1_ffn_router_w, L1_ffn_router_b, L1_ffn_w1, L1_ffn_b1, L1_ffn_w2, L1_ffn_b2)
    x = x + _L2_xattn_ref(_layernorm(x, axis=-1), ctx_1024, ctx_1024, L2_xattn_igate_w, L2_xattn_igate_b, L2_xattn_fgate_w, L2_xattn_fgate_b, L2_xattn_out_w)
    x = x + _L2_ffn_ref(_layernorm(x, axis=-1), L2_ffn_Wr, L2_ffn_W1, L2_ffn_b1, L2_ffn_W2, L2_ffn_b2, L2_ffn_fw1, L2_ffn_fb1, L2_ffn_fw2, L2_ffn_fb2)
    x = x + _L3_xattn_ref(_layernorm(x, axis=-1), ctx_1024, ctx_1024, L3_xattn_Wq, L3_xattn_bq, L3_xattn_Wk, L3_xattn_bk, L3_xattn_Wv, L3_xattn_bv, L3_xattn_Wo, L3_xattn_bo)
    x = x + _L3_ffn_ref(_layernorm(x, axis=-1), L3_ffn_w1, L3_ffn_conv_w, L3_ffn_conv_b, L3_ffn_w2)
    return x

_drawn_inputs = setup_inputs


def setup_inputs(seed=0):
    import zlib

    import numpy as np

    out = dict(_drawn_inputs(seed))
    spreads = {'L0_xattn_bq': (0.0, 0.1),
     'L0_xattn_bk': (0.0, 2.0),
     'L0_xattn_bv': (0.0, 0.1),
     'L0_xattn_bo': (0.0, 0.1),
     'L0_ffn_expert_b1': (0.0, 0.1),
     'L0_ffn_expert_b2': (0.0, 0.1),
     'L1_xattn_bq': (0.0, 0.406),
     'L1_xattn_bk': (0.0, 2.0),
     'L1_xattn_bv': (0.0, 0.1),
     'L1_xattn_bo': (0.0, 0.1),
     'L1_ffn_router_b': (0.0, 0.369),
     'L1_ffn_b1': (0.0, 0.611),
     'L1_ffn_b2': (0.0, 0.1),
     'L2_ffn_b1': (0.0, 0.8),
     'L2_ffn_b2': (0.0, 0.27),
     'L2_ffn_fb1': (0.0, 0.8),
     'L2_ffn_fb2': (0.0, 0.8),
     'L3_xattn_bq': (0.0, 0.761),
     'L3_xattn_bk': (0.0, 2.0),
     'L3_xattn_bv': (0.0, 0.1),
     'L3_xattn_bo': (0.0, 0.1)}
    factors = {'L2_xattn_igate_b': 64.0,
     'L2_ffn_W1': 3.715,
     'L2_ffn_W2': 3.391,
     'L2_ffn_fw1': 8.0,
     'L2_ffn_fw2': 8.0,
     'L3_ffn_w1': 2.673}
    for name, (base, spread) in spreads.items():
        noise = np.random.default_rng([zlib.crc32(name.encode()), seed]).standard_normal(out[name].shape)
        drawn = base * np.exp(spread * noise) if base else spread * noise
        out[name] = jnp.asarray(drawn.astype(out[name].dtype))
    for name, factor in factors.items():
        out[name] = (out[name] * factor).astype(out[name].dtype)
    return out
```

```python
import numpy as np
from contextlib import ExitStack
import concourse.bass as bass
from concourse import mybir

FP32 = mybir.dt.float32
BF16 = mybir.dt.bfloat16
I32 = mybir.dt.int32
U32 = mybir.dt.uint32
ALU = mybir.AluOpType
ACT = mybir.ActivationFunctionType
AX = mybir.AxisListType

B, S, C = 64, 64, 128
TOK = B * S
P = 128
TILES = TOK // P
GT = 4
GROUP = GT * P
NG = TILES // GT
PAIRS = GT
LN_EPS = 1e-5
FF = 512
FK = FF // P
MAX_E = 16
TOP_K = 2
SLOTS = (TOK * TOP_K // P + MAX_E + 2) * P


class Chain:

    def __init__(self, engine, sem, per=0):
        self.engine, self.sem, self.per, self.base, self.n = engine, sem, per, 0, 0

    def start(self, i):
        assert self.n in (0, self.per), (self.n, self.per)
        self.base, self.n = i * self.per, 0

    def done(self, instruction):
        self.n += 1
        instruction.then_inc(self.sem, 1)

    def sync(self):
        self.engine.wait_ge(self.sem, self.base + self.n)

    def step(self, instruction):
        self.done(instruction)
        self.sync()


class Kit:

    def __init__(self, nc, A, ctx):
        self.nc, self.A = nc, A
        sb = lambda name, shape, dt=FP32: ctx.enter_context(nc.sbuf_tensor(name, shape, dt))
        self.X = sb("residual", [P, TILES, C])
        self.XN = sb("normed", [P, TILES, C])
        self.W1 = sb("expert_w1", [C, MAX_E, FF])
        self.W2 = sb("expert_w2", [P, MAX_E, FK, C])
        self.B1 = sb("expert_b1", [P, MAX_E, FF])
        self.B2 = sb("expert_b2", [P, MAX_E, C])
        self.experts_in = ctx.enter_context(nc.semaphore("experts_in"))
        self.experts_loaded = 0
        self.packed = nc.dram_tensor("packed_rows", (SLOTS, C), FP32, kind="Internal").ap()
        self.expert_out = nc.dram_tensor("expert_rows", (SLOTS, C), FP32, kind="Internal").ap()
        self.marks = ctx.enter_context(nc.semaphore("marks"))
        self.minus_half = sb("minus_half", [P, GT])
        self.ident = sb("identity", [P, P])


    def passed(self, engine):
        engine.sem_inc(self.marks, 1)


def scoped(nc, stack, tag):
    sb = lambda name, shape, dt=FP32: stack.enter_context(nc.sbuf_tensor(f"{tag}_{name}", shape, dt))
    ps = lambda name, shape, dt=FP32: stack.enter_context(nc.psum_tensor(f"{tag}_{name}", shape, dt))
    taken = []

    def clear():
        if taken:
            nc.clear_and_free_semaphores(taken)
            nc.all_engine_barrier()

    stack.callback(clear)

    def sem(name):
        taken.append(nc.alloc_semaphore(name=f"{tag}_{name}"))
        return taken[-1]
    return sb, ps, sem



LN_STEPS = 2 * GT


def layernorm(nc, v, chain, x_group, xn, stats, mv, var, var_ready, rstd, rstd_ready, turn, passed):
    for j in range(GT):
        chain.done(nc.vector.bn_stats(stats[:, j, :], x_group(j)))
    chain.sync()
    passed(v)
    for j in range(GT):
        chain.done(nc.vector.bn_aggr(mv[:, j, :], stats[:, j, :]))
    chain.sync()
    nc.vector.tensor_scalar(var[:, :], mv[:, :, 1], LN_EPS, None, ALU.add).then_inc(var_ready, 1)
    v.wait_ge(rstd_ready, turn + 1)
    for j in range(GT):
        ins = nc.vector.tensor_scalar(xn[:, j, :], x_group(j), mv[:, j, 0:1], rstd[:, j:j + 1], ALU.subtract, ALU.mult)
    return ins


def inverse_root(nc, pool, var, var_ready, rstd, rstd_ready, minus_half, turn):
    pool.wait_ge(var_ready, turn + 1)
    nc.gpsimd.tensor_tensor(rstd[:, :], var[:, :], minus_half[:, :], ALU.pow).then_inc(rstd_ready, 1)


def load_x(kit):
    nc, A = kit.nc, kit.A
    with ExitStack() as st:
        _, _, sem = scoped(nc, st, "load")
        loaded = sem("loaded")
        block = st.enter_context(nc.Block())

        @block.vector
        def _(v):
            nc.vector.memset(kit.minus_half[:, :], -0.5)

        @block.sync
        def _(sp):
            sp.dma_start(kit.X[:, :, :], A["x"].rearrange("(t p) c -> p t c", p=P)).then_inc(loaded, 16)
            sp.dma_start(kit.ident[:, :], A["ident"]).then_inc(loaded, 16)
            sp.wait_ge(loaded, 32)


def store_x(kit, out):
    nc = kit.nc
    with ExitStack() as st:
        _, _, sem = scoped(nc, st, "store")
        stored = sem("stored")
        block = st.enter_context(nc.Block())

        @block.sync
        def _(sp):
            sp.dma_start(out.rearrange("(t p) c -> p t c", p=P), kit.X[:, :, :]).then_inc(stored, 16)
            sp.wait_ge(stored, 16)


def mha(kit, tag):
    nc, A = kit.nc, kit.A
    H, DH = 16, C // 16
    HH = H // 2
    SCALE = DH ** -0.5
    VW = 2 * 2 * DH + 2
    with ExitStack() as st:
        sb, ps, sem = scoped(nc, st, tag)
        w = {n: sb(n, [C, C]) for n in ("Wq", "Wk", "Wv", "Wo")}
        bias = {n: sb(n, [C, 1]) for n in ("bq", "bk", "bv")}
        bo = sb("bo", [P, C])
        head_mask = sb("head_mask", [P, HH])
        half_mask = sb("half_mask", [P, C])
        cT = sb("cT", [C, GROUP // S, 2, S])
        stats, mv, var, rstd = sb("stats", [P, GT, 6]), sb("mv", [P, GT, 2]), sb("var", [P, GT]), sb("rstd", [P, GT])
        xn, xnT = sb("xn", [P, GT, C]), sb("xnT", [C, GROUP])
        QT, KT = sb("QT", [C, GROUP // S, 2, S]), sb("KT", [C, GROUP])
        fold = sb("fold", [P, S])
        Km = sb("Km", [C, 2, 2, HH, S])
        V2 = sb("V2", [P, PAIRS, 2 * HH // 2, VW])
        Pm = sb("Pm", [P, 2, H * S])
        mx = sb("mx", [P, 2, H])
        PT = sb("PT", [P, H * S])
        rs = sb("rs", [P, 2, H])
        O = sb("O", [P, PAIRS, 2, 2, C // 2])
        OT = sb("OT", [C, GROUP])
        p_misc = ps("p_misc", [P, GROUP])
        p_s = [ps(f"p_s{i}", [P, H * S]) for i in range(2)]
        p_t = [ps(f"p_t{i}", [P, H * S // 2]) for i in range(2)]
        p_o = ps("p_o", [P, 512])

        weights, ctx_in = sem("weights"), sem("ctx_in")
        xn_ready, xT_ps, xnT_ready = sem("xn_ready"), sem("xT_ps"), sem("xnT_ready")
        q_ps, k_ps, v_ps = sem("q_ps"), sem("k_ps"), sem("v_ps")
        qT_ready, kT_ready, v_ready, km_ready = sem("qT_ready"), sem("kT_ready"), sem("v_ready"), sem("km_ready")
        s_ps, d_ready, p_ready, t_ps, pT_ready = sem("s_ps"), sem("d_ready"), sem("p_ready"), sem("t_ps"), sem("pT_ready")
        o_ps, o_ready, oT_ps, oT_ready, y_ps = sem("o_ps"), sem("o_ready"), sem("oT_ps"), sem("oT_ready"), sem("y_ps")
        var_ready, rstd_ready = sem("var_ready"), sem("rstd_ready")
        bo_added, ones_set, dve = sem("bo_added"), sem("ones_set"), sem("dve")
        X = kit.X
        block = st.enter_context(nc.Block())

        @block.sync
        def _(sp):
            for n in w:
                sp.dma_start(w[n][:, :], A[f"{tag}_{n}"]).then_inc(weights, 16)
            for n in bias:
                sp.dma_start(bias[n][:, :], A[f"{tag}_{n}"].rearrange("(c a) -> c a", a=1)).then_inc(weights, 16)
            sp.dma_start(bo[:, :], A[f"{tag}_bo"].rearrange("(a c) -> a c", a=1).to_broadcast([P, C])).then_inc(weights, 16)
            sp.dma_start(head_mask[:, :], A["head_mask"]).then_inc(weights, 16)
            sp.dma_start(half_mask[:, :], A["half_mask8"]).then_inc(weights, 16)
            sp.dma_start(fold[:, :], A["fold"]).then_inc(weights, 16)
            with sp.Fori(0, NG) as g:
                sp.wait_ge(v_ps, 2 * g)
                for twice in range(2):
                    sp.dma_start(cT[:, :, twice, :],
                                 A["ctxT"][:, bass.ds(g * GROUP, GROUP)].rearrange("c (b s) -> c b s", s=S)).then_inc(ctx_in, 16)
        N_WEIGHTS = 16 * 11

        @block.gpsimd
        def _(pool):
            pool.wait_ge(weights, N_WEIGHTS)
            with pool.Fori(0, NG) as g:
                xg = X[:, bass.ds(g * GT, GT), :]
                inverse_root(nc, pool, var, var_ready, rstd, rstd_ready, kit.minus_half, g)
                pool.wait_ge(xn_ready, g + 1)
                nc.gpsimd.tensor_tensor(xg, xg, bo[:, :].unsqueeze(1).to_broadcast([P, GT, C]), ALU.add).then_inc(bo_added, 1)
                pool.wait_ge(kT_ready, g + 1)
                for j in range(PAIRS):
                    if j >= 2:
                        pool.wait_ge(s_ps, PAIRS * g + j - 1)
                    kt = KT[:, j * P:(j + 1) * P].rearrange("c (b s) -> c b s", s=S)
                    for b in range(2):
                        ins = nc.gpsimd.tensor_tensor(
                            Km[:, j % 2, b], kt[:, b].unsqueeze(1).to_broadcast([P, HH, S]),
                            head_mask[:, :].unsqueeze(2).to_broadcast([P, HH, S]), ALU.mult)
                    ins.then_inc(km_ready, 1)

        @block.scalar
        def _(act):
            act.wait_ge(weights, N_WEIGHTS)
            act.wait_ge(ones_set, 5)
            with act.Fori(0, NG) as g:
                act.wait_ge(xT_ps, g + 1)
                nc.scalar.activation(xnT[:, :], p_misc[:, :], ACT.Copy).then_inc(xnT_ready, 1)
                act.wait_ge(q_ps, g + 1)
                for h in range(2):
                    rows = slice(64 * h, 64 * h + 64)
                    ins = nc.scalar.activation(QT[rows, :, h, :], p_s[0][rows, 0:512].rearrange("c (b s) -> c b s", s=S),
                                               ACT.Identity, bias=bias["bq"][rows, :])
                ins.then_inc(qT_ready, 1)

                def evacuate(j):
                    act.wait_ge(o_ps, PAIRS * g + j)
                    for h in range(2):
                        act.wait_ge(t_ps, 2 * PAIRS * g + 2 * j + h + 1)
                        nc.scalar.activation(PT[:, h * 512:(h + 1) * 512], p_t[h][:, :], ACT.Copy).then_inc(pT_ready, 1)

                for j in range(PAIRS):
                    act.wait_ge(d_ready, PAIRS * g + j + 1)
                    nc.scalar.activation(Pm[:, j % 2, :], Pm[:, j % 2, :], ACT.Exp, scale=SCALE).then_inc(p_ready, 1)
                    if j >= 1:
                        evacuate(j - 1)
                evacuate(PAIRS - 1)
                act.wait_ge(oT_ps, g + 1)
                nc.scalar.activation(OT[:, :], p_misc[:, :], ACT.Identity, bias=bias["bv"][:, :]).then_inc(oT_ready, 1)

        @block.vector
        def _(v):
            c = Chain(v, dve, LN_STEPS + 2 * PAIRS + 1)
            nc.vector.memset(V2[:, :, :, 4 * DH:VW], 0.0).then_inc(ones_set, 1)
            v.wait_ge(ones_set, 1)
            nc.vector.memset(V2[0:S, :, :, 4 * DH:4 * DH + 1], 1.0).then_inc(ones_set, 1)
            nc.vector.memset(V2[S:P, :, :, 4 * DH + 1:VW], 1.0).then_inc(ones_set, 1)
            nc.vector.memset(QT[:, :, :, :], 0.0).then_inc(ones_set, 1)
            nc.vector.memset(O[:, :, :, :, :], 0.0).then_inc(ones_set, 1)
            v.wait_ge(ones_set, 5)
            v.wait_ge(weights, N_WEIGHTS)
            with v.Fori(0, NG) as g:
                c.start(g)
                layernorm(nc, v, c, lambda j: X[:, bass.ds(g * GT + j, 1), :].squeeze(1), xn, stats, mv, var, var_ready,
                          rstd, rstd_ready, g, kit.passed).then_inc(xn_ready, 1)
                v.wait_ge(k_ps, g + 1)
                nc.vector.tensor_scalar(KT[:, :], p_s[0][:, 512:1024], bias["bk"][:, :], None, ALU.add).then_inc(kT_ready, 1)
                for j in range(PAIRS):
                    v.wait_ge(v_ps, 2 * g + j // 2 + 1)
                    hm = half_mask[:, :].rearrange("p (f i c) -> p i f c", f=2, c=2 * DH)
                    for b in range(2):
                        vin = p_s[1][:, 256 * j + C * b:256 * j + C * b + C].rearrange("p (f i c) -> p i f c", f=2, c=2 * DH)
                        vout = V2[:, j, 4 * b:4 * b + 4, 0:4 * DH].rearrange("p i (f c) -> p i f c", f=2)
                        ins = nc.vector.tensor_tensor(vout, vin, hm, ALU.mult)
                ins.then_inc(v_ready, 1)

                def normalise(j):
                    v.wait_ge(o_ps, PAIRS * g + j + 1)
                    po = p_o[:, 0:H // 2 * VW].rearrange("p (h c) -> p h c", c=VW)
                    r = rs[:, j % 2, :]
                    c.step(nc.vector.reciprocal(r.rearrange("p (h c) -> p h c", c=2), po[:, :, 4 * DH:VW]))
                    for f in range(2):
                        q = slice(f * S, (f + 1) * S)
                        ins = nc.vector.tensor_tensor(
                            O[q, j, :, f, :].rearrange("p b (i a c) -> p b i a c", a=2, c=DH),
                            po[q, :, f * 2 * DH:(f + 1) * 2 * DH].rearrange("p (b i) (a c) -> p b i a c", b=2, c=DH),
                            r[q].rearrange("p (b i a) -> p b i a", b=2, a=2).unsqueeze(4).to_broadcast([S, 2, HH // 2, 2, DH]),
                            ALU.mult)
                    ins.then_inc(o_ready, 1)

                for j in range(PAIRS):
                    v.wait_ge(s_ps, PAIRS * g + j + 1)
                    s3 = p_s[j % 2][:, :].rearrange("p (h k) -> p h k", k=S)
                    c.step(nc.vector.tensor_reduce(mx[:, j % 2, :], s3, AX.X, ALU.max))
                    nc.vector.tensor_tensor(Pm[:, j % 2, :].rearrange("p (h k) -> p h k", k=S), s3,
                                            mx[:, j % 2, :].unsqueeze(2).to_broadcast([P, H, S]), ALU.subtract).then_inc(d_ready, 1)
                    if j >= 1:
                        normalise(j - 1)
                normalise(PAIRS - 1)
                v.wait_ge(y_ps, g + 1)
                v.wait_ge(bo_added, g + 1)
                xg = X[:, bass.ds(g * GT, GT), :]
                c.done(nc.vector.tensor_tensor(xg, xg, p_misc[:, :].rearrange("p (t c) -> p t c", c=C), ALU.add))
                c.sync()

        @block.tensor
        def _(pe):
            pe.wait_ge(weights, N_WEIGHTS)
            pe.wait_ge(ones_set, 5)
            with pe.Fori(0, NG) as g:
                pe.wait_ge(xn_ready, g + 1)
                for j in range(GT):
                    ins = nc.tensor.transpose(p_misc[:, j * P:(j + 1) * P], xn[:, j, :], kit.ident[:, :])
                ins.then_inc(xT_ps, 1)
                pe.wait_ge(ctx_in, 32 * g + 32)
                nc.tensor.matmul(p_s[0][:, 512:1024], w["Wk"][:, :], cT[:, :, 0, :], start=True, stop=True).then_inc(k_ps, 1)
                for half in range(2):
                    for b in range(4):
                        ins = nc.tensor.matmul(p_s[1][:, half * 512 + b * C:half * 512 + (b + 1) * C],
                                               cT[:, half * 4 + b], w["Wv"][:, :], start=True, stop=True)
                    ins.then_inc(v_ps, 1)
                pe.wait_ge(xnT_ready, g + 1)
                nc.tensor.matmul(p_s[0][:, 0:512], w["Wq"][:, :], xnT[:, :], start=True, stop=True).then_inc(q_ps, 1)

                def scores(j):
                    if j == 0:
                        pe.wait_ge(qT_ready, g + 1)
                        pe.wait_ge(kT_ready, g + 1)
                    elif j == 1:
                        pe.wait_ge(v_ready, g + 1)
                    else:
                        pe.wait_ge(d_ready, PAIRS * g + j - 1)
                    pe.wait_ge(km_ready, PAIRS * g + j + 1)
                    for b in range(2):
                        ins = nc.tensor.matmul(p_s[j % 2][:, b * 512:(b + 1) * 512], QT[:, 2 * j + b], Km[:, j % 2, b],
                                               start=True, stop=True)
                    ins.then_inc(s_ps, 1)

                def values(j):
                    pe.wait_ge(p_ready, PAIRS * g + j + 1)
                    for h in range(2):
                        if j >= 1:
                            pe.wait_ge(pT_ready, 2 * PAIRS * g + 2 * (j - 1) + h + 1)
                        for i in range(4):
                            ins = nc.tensor.transpose(p_t[h][:, i * P:(i + 1) * P],
                                                      Pm[:, j % 2, (4 * h + i) * P:(4 * h + i + 1) * P], kit.ident[:, :])
                        ins.then_inc(t_ps, 1)
                    pe.wait_ge(o_ready, PAIRS * g + j)
                    if j == 0:
                        pe.wait_ge(v_ready, g + 1)
                    for h in range(2):
                        pe.wait_ge(pT_ready, 2 * PAIRS * g + 2 * j + h + 1)
                        for i in range(4 * h, 4 * h + 4):
                            ins = nc.tensor.matmul(p_o[:, i * VW:(i + 1) * VW], PT[:, i * P:(i + 1) * P], V2[:, j, i, :],
                                                   start=True, stop=True)
                    ins.then_inc(o_ps, 1)

                def back(j):
                    pe.wait_ge(o_ready, PAIRS * g + j + 1)
                    for b in range(2):
                        ins = nc.tensor.matmul(p_misc[:, j * P + b * S:j * P + (b + 1) * S], O[:, j, b, :, :], fold[:, :],
                                               start=True, stop=True)
                    if j == PAIRS - 1:
                        ins.then_inc(oT_ps, 1)

                scores(0)
                scores(1)
                for j in range(PAIRS):
                    values(j)
                    if j + 2 < PAIRS:
                        scores(j + 2)
                    if j >= 1:
                        back(j - 1)
                back(PAIRS - 1)
                pe.wait_ge(oT_ready, g + 1)
                for j in range(GT):
                    ins = nc.tensor.matmul(p_misc[:, j * C:(j + 1) * C], OT[:, j * P:(j + 1) * P], w["Wo"][:, :],
                                           start=True, stop=True)
                ins.then_inc(y_ps, 1)


class Moe:

    def __init__(self, routed, cap, fallback, gates):
        self.routed, self.cap, self.fallback, self.gates = routed, cap, fallback, gates
        self.experts = routed + fallback
        most = TOK * TOP_K // P + self.experts - 1
        self.tiles = most + most % 2


MOES = {
    "L0_ffn": Moe(8, None, 0, "probs_sum"),
    "L1_ffn": Moe(16, -(-5 * TOK * TOP_K // (4 * 16)), 0, "kept_softmax"),
    "L2_ffn": Moe(8, int(1.25 * (TOK * TOP_K / 8)), 1, "probs_clip"),
}


def load_experts(kit, sp, tag):
    A, E = kit.A, MOES[tag].experts
    sp.dma_start(kit.W1[:, 0:E, :], A[f"{tag}_w1"]).then_inc(kit.experts_in, 16)
    sp.dma_start(kit.W2[:, 0:E, :, :], A[f"{tag}_w2"]).then_inc(kit.experts_in, 16)
    sp.dma_start(kit.B1[:, 0:E, :], A[f"{tag}_b1"].unsqueeze(0).to_broadcast([P, E, FF])).then_inc(kit.experts_in, 16)
    sp.dma_start(kit.B2[:, 0:E, :], A[f"{tag}_b2"].unsqueeze(0).to_broadcast([P, E, C])).then_inc(kit.experts_in, 16)
    kit.experts_loaded += 64


def load_now(kit, tag):
    with ExitStack() as st:
        block = st.enter_context(kit.nc.Block())

        @block.sync
        def _(sp):
            load_experts(kit, sp, tag)


def moe(kit, tag):
    nc = kit.nc
    with ExitStack() as st:
        sb, _, _ = scoped(nc, st, tag)
        r = Route()
        r.values = sb("values", [P, TILES, TOP_K])
        r.chosen = sb("chosen", [P, TILES, TOP_K])
        r.logits = sb("logits", [P, TILES, MOES[tag].routed])
        r.gate = sb("gate", [P, TOP_K, TILES])
        r.slot_out = sb("slot_out", [P, TILES, TOP_K], I32)
        r.slot_back = sb("slot_back", [P, TILES, TOP_K], I32)
        r.tile_expert = sb("tile_expert", [1, MOES[tag].tiles], I32)
        load_now(kit, tag)
        router(kit, tag, r)
        plan(kit, tag, r)
        dispatch(kit, tag, r)
        run_experts(kit, tag, r)
        combine(kit, tag, r)


class Route:
    pass


def router(kit, tag, r):
    nc, A, m = kit.nc, kit.A, MOES[tag]
    E = m.routed
    with ExitStack() as st:
        sb, ps, sem = scoped(nc, st, tag + "_r")
        wr = sb("wr", [C, E])
        br = sb("br", [P, E])
        stats, mv, var, rstd = sb("stats", [P, GT, 6]), sb("mv", [P, GT, 2]), sb("var", [P, GT]), sb("rstd", [P, GT])
        xn, xnT = sb("xn", [P, GT, C]), sb("xnT", [C, GROUP])
        lg = sb("lg", [P, GT, E])
        top, top_i = sb("top", [P, GT, 8]), sb("top_i", [P, GT, 8], U32)
        p_x, p_l = ps("p_x", [P, GROUP]), ps("p_l", [P, 512])
        weights, var_ready, rstd_ready, xn_ready = sem("weights"), sem("var_ready"), sem("rstd_ready"), sem("xn_ready")
        xT_ps, xnT_ready, logits_ps, kept, dve = sem("xT_ps"), sem("xnT_ready"), sem("logits_ps"), sem("kept"), sem("dve")
        N_WEIGHTS = 32
        X = kit.X
        block = st.enter_context(nc.Block())

        @block.sync
        def _(sp):
            sp.dma_start(wr[:, :], A[f"{tag}_router_w"]).then_inc(weights, 16)
            sp.dma_start(br[:, :], A[f"{tag}_router_b"].rearrange("(a c) -> a c", a=1).to_broadcast([P, E])).then_inc(weights, 16)

        @block.gpsimd
        def _(pool):
            with pool.Fori(0, NG) as g:
                inverse_root(nc, pool, var, var_ready, rstd, rstd_ready, kit.minus_half, g)

        @block.tensor
        def _(pe):
            pe.wait_ge(weights, N_WEIGHTS)
            with pe.Fori(0, NG) as g:
                pe.wait_ge(xn_ready, g + 1)
                for j in range(GT):
                    ins = nc.tensor.transpose(p_x[:, j * P:(j + 1) * P], xn[:, j, :], kit.ident[:, :])
                ins.then_inc(xT_ps, 1)
                pe.wait_ge(xnT_ready, g + 1)
                for j in range(GT):
                    ins = nc.tensor.matmul(p_l[:, j * E:(j + 1) * E], xnT[:, j * P:(j + 1) * P], wr[:, :], start=True, stop=True)
                ins.then_inc(logits_ps, 1)

        @block.scalar
        def _(act):
            with act.Fori(0, NG) as g:
                act.wait_ge(xT_ps, g + 1)
                nc.scalar.activation(xnT[:, :], p_x[:, :], ACT.Copy).then_inc(xnT_ready, 1)
                act.wait_ge(xn_ready, g + 1)
                nc.scalar.activation(kit.XN[:, bass.ds(g * GT, GT), :], xn[:, :, :], ACT.Copy).then_inc(kept, 1)

        @block.vector
        def _(v):
            c = Chain(v, dve, LN_STEPS + 2 * GT + 4)
            v.wait_ge(weights, N_WEIGHTS)
            with v.Fori(0, NG) as g:
                c.start(g)
                v.wait_ge(kept, g)
                layernorm(nc, v, c, lambda j: X[:, bass.ds(g * GT + j, 1), :].squeeze(1), xn, stats, mv, var, var_ready,
                          rstd, rstd_ready, g, kit.passed).then_inc(xn_ready, 1)
                v.wait_ge(logits_ps, g + 1)
                c.done(nc.vector.tensor_tensor(lg[:, :, :], p_l[:, 0:GT * E].rearrange("p (t e) -> p t e", e=E),
                                               br[:, :].unsqueeze(1).to_broadcast([P, GT, E]), ALU.add))
                c.sync()
                kit.passed(v)
                for j in range(GT):
                    c.done(nc.vector.max(top[:, j, :], lg[:, j, :]))
                c.sync()
                kit.passed(v)
                for j in range(GT):
                    c.done(nc.vector.max_index(top_i[:, j, :], top[:, j, :], lg[:, j, :]))
                c.sync()
                tiles = bass.ds(g * GT, GT)
                c.done(nc.vector.tensor_copy(r.values[:, tiles, :], top[:, :, 0:TOP_K]))
                c.done(nc.vector.tensor_copy(r.chosen[:, tiles, :], top_i[:, :, 0:TOP_K]))
                c.done(nc.vector.tensor_copy(r.logits[:, tiles, :], lg[:, :, :]))
                c.sync()


def plan(kit, tag, r):
    nc, A, m = kit.nc, kit.A, MOES[tag]
    E, R, T = m.experts, m.routed, TILES
    with ExitStack() as st:
        sb, ps, sem = scoped(nc, st, tag + "_p")
        earlier, ones = sb("earlier", [P, P]), sb("ones", [P, P])
        iota = sb("iota", [P, 128])
        restart = sb("restart", [P, E, T])
        M = [sb("M0", [P, E, T]), sb("M1", [P, E, T])]
        both, pos, tot, inc, row = (sb(n, [P, E, T]) for n in ("both", "pos", "tot", "inc", "row"))
        ex = sb("ex", [P, T, R])
        es, pr, den, kp, sl = sb("es", [P, T]), sb("pr", [P, 2, T]), sb("den", [P, T]), sb("kp", [P, 2, T]), sb("sl", [P, 2, T])
        open_, over = sb("open", [P, T]), sb("over", [P, T])
        cnt, cnt_i, nt, cum, base = sb("cnt", [P, E]), sb("cnt_i", [P, E], I32), sb("nt", [P, E]), sb("cum", [P, E]), sb("base", [P, E])
        ones_e = sb("ones_e", [P, E])
        le = sb("le", [1, m.tiles, E])
        te = sb("te", [1, m.tiles])
        p_in, p_tot = ps("p_in", [P, 512]), ps("p_tot", [P, 512])
        consts, dve, counted, exps, asked, ready = sem("consts"), sem("dve"), sem("counted"), sem("exps"), sem("asked"), sem("ready")
        block = st.enter_context(nc.Block())
        ROUNDS = 1 if not m.fallback else E

        @block.sync
        def _(sp):
            sp.dma_start(earlier[:, :], A["earlier"]).then_inc(consts, 16)
            sp.dma_start(ones[:, :], A["ones"]).then_inc(consts, 16)
            sp.dma_start(iota[:, :], A["iota"].to_broadcast([P, 128])).then_inc(consts, 16)

        @block.scalar
        def _(act):
            act.wait_ge(exps, 1)
            nc.scalar.activation(ex[:, :, :], ex[:, :, :], ACT.Exp)
            nc.scalar.activation(pr[:, :, :], pr[:, :, :], ACT.Exp).then_inc(exps, 1)

        @block.tensor
        def _(pe):
            pe.wait_ge(consts, 48)
            for n in range(ROUNDS):
                pe.wait_ge(asked, n + 1)
                src = both[:, n, :] if m.fallback else both[:, :, :]
                width = T if m.fallback else E * T
                nc.tensor.matmul(p_in[:, 0:width], earlier[:, :], src, start=True, stop=True)
                nc.tensor.matmul(p_tot[:, 0:width], ones[:, :], src, start=True, stop=True).then_inc(counted, 1)

        @block.vector
        def _(v):
            c = Chain(v, dve)
            tt, ts = nc.vector.tensor_tensor, nc.vector.tensor_scalar
            v.wait_ge(consts, 48)
            c.done(nc.vector.memset(restart[:, :, :], 1.0))
            c.done(nc.vector.memset(ones_e[:, :], 1.0))
            c.done(nc.vector.memset(open_[:, :], 1.0))
            c.done(nc.vector.memset(M[0][:, :, :], 0.0))
            c.done(nc.vector.memset(M[1][:, :, :], 0.0))
            top = r.values[:, :, 0]
            c.done(tt(ex[:, :, :], r.logits[:, :, :], top.unsqueeze(2).to_broadcast([P, T, R]), ALU.subtract))
            for k in range(TOP_K):
                last = tt(pr[:, k, :], r.values[:, :, k], top, ALU.subtract)
                if k == 0:
                    c.done(last)
                else:
                    last.then_inc(exps, 1)
            c.sync()
            c.done(nc.vector.memset(restart[:, :, 0], 0.0))
            for k in range(TOP_K):
                c.done(tt(M[k][:, 0:R, :], r.chosen[:, :, k].unsqueeze(1).to_broadcast([P, R, T]),
                          iota[:, 0:R].unsqueeze(2).to_broadcast([P, R, T]), ALU.is_equal))
            c.sync()
            if not m.fallback:
                tt(both[:, :, :], M[0][:, :, :], M[1][:, :, :], ALU.add).then_inc(asked, 1)
                v.wait_ge(counted, 1)
                c.step(nc.vector.tensor_copy(tot[:, :, :], p_tot[:, 0:E * T].rearrange("p (e t) -> p e t", t=T)))
                c.step(nc.vector.tensor_tensor_scan(inc[:, :, :].rearrange("p e t -> p (e t)"), restart[:, :, :].rearrange("p e t -> p (e t)"),
                                                    tot[:, :, :].rearrange("p e t -> p (e t)"), 0.0, ALU.mult, ALU.add))
                c.step(tt(pos[:, :, :], inc[:, :, :], tot[:, :, :], ALU.subtract))
                c.step(tt(pos[:, :, :], pos[:, :, :], p_in[:, 0:E * T].rearrange("p (e t) -> p e t", t=T), ALU.add))
                if m.cap:
                    c.step(ts(row[:, :, :], pos[:, :, :], float(m.cap), None, ALU.is_lt))
                    for k in range(TOP_K):
                        c.done(tt(M[k][:, :, :], M[k][:, :, :], row[:, :, :], ALU.mult))
                c.step(ts(cnt[:, :], inc[:, :, T - 1], float(m.cap or TOK * TOP_K), None, ALU.min))
            else:
                c.step(tt(row[:, 0:R, :], M[0][:, 0:R, :], M[1][:, 0:R, :], ALU.add))
                for e in range(E):
                    if e < R:
                        tt(both[:, e, :], row[:, e, :], open_[:, :], ALU.mult).then_inc(asked, 1)
                    else:
                        ts(both[:, e, :], open_[:, :], -1.0, 1.0, ALU.mult, ALU.add).then_inc(asked, 1)
                    v.wait_ge(counted, e + 1)
                    c.step(nc.vector.tensor_copy(tot[:, e, :], p_tot[:, 0:T]))
                    c.step(nc.vector.tensor_tensor_scan(inc[:, e, :], restart[:, e, :], tot[:, e, :], 0.0, ALU.mult, ALU.add))
                    c.step(tt(pos[:, e, :], inc[:, e, :], tot[:, e, :], ALU.subtract))
                    c.step(tt(pos[:, e, :], pos[:, e, :], p_in[:, 0:T], ALU.add))
                    if e < R:
                        c.step(nc.vector.scalar_tensor_tensor(over[:, :], pos[:, e, :], float(m.cap), both[:, e, :], ALU.is_ge, ALU.mult))
                        c.step(tt(open_[:, :], open_[:, :], over[:, :], ALU.subtract))
                for k in range(TOP_K):
                    c.done(tt(M[k][:, 0:R, :], M[k][:, 0:R, :], open_[:, :].unsqueeze(1).to_broadcast([P, R, T]), ALU.mult))
                c.done(nc.vector.tensor_copy(M[0][:, R, :], both[:, R, :]))
                c.done(ts(cnt[:, 0:R], inc[:, 0:R, T - 1], float(m.cap), None, ALU.min))
                c.done(nc.vector.tensor_copy(cnt[:, R:E], inc[:, R:E, T - 1]))
                c.sync()
            c.step(ts(cnt_i[:, :], cnt[:, :], float(P - 1), None, ALU.add))
            c.step(ts(cnt_i[:, :], cnt_i[:, :], P.bit_length() - 1, None, ALU.logical_shift_right))
            c.step(nc.vector.tensor_copy(nt[:, :], cnt_i[:, :]))
            c.step(nc.vector.tensor_tensor_scan(cum[:, :], ones_e[:, :], nt[:, :], 0.0, ALU.mult, ALU.add))
            c.step(tt(base[:, :], cum[:, :], nt[:, :], ALU.subtract))
            c.step(ts(base[:, :], base[:, :], float(P), None, ALU.mult))
            c.step(tt(row[:, :, :], pos[:, :, :], base[:, :].unsqueeze(2).to_broadcast([P, E, T]), ALU.add))
            n = m.tiles
            c.step(tt(le[:, :, :], cum[0:1, :].unsqueeze(1).to_broadcast([1, n, E]), iota[0:1, 0:n].unsqueeze(2).to_broadcast([1, n, E]), ALU.is_le))
            c.step(nc.vector.tensor_reduce(te[:, :], le[:, :, :], AX.X, ALU.add))
            c.done(ts(r.tile_expert[:, :], te[:, :], float(E - 1), None, ALU.min))
            for k in range(TOP_K):
                c.step(nc.vector.tensor_reduce(kp[:, k, :], M[k][:, :, :].rearrange("p e t -> p t e"), AX.X, ALU.add))
                c.step(tt(pos[:, :, :], M[k][:, :, :], row[:, :, :], ALU.mult))
                c.step(nc.vector.tensor_reduce(sl[:, k, :], pos[:, :, :].rearrange("p e t -> p t e"), AX.X, ALU.add))
                c.step(nc.vector.tensor_copy(r.slot_back[:, :, k], sl[:, k, :]))
                c.step(ts(over[:, :], kp[:, k, :], float(-NOWHERE), float(NOWHERE), ALU.mult, ALU.add))
                c.step(tt(r.slot_out[:, :, k], sl[:, k, :], over[:, :], ALU.add))
            v.wait_ge(exps, 2)
            if m.gates == "kept_softmax":
                c.step(tt(den[:, :], pr[:, 0, :], pr[:, 1, :], ALU.add))
                c.step(nc.vector.reciprocal(den[:, :], den[:, :]))
                for k in range(TOP_K):
                    c.step(tt(pr[:, k, :], pr[:, k, :], den[:, :], ALU.mult))
                    c.step(tt(pr[:, k, :], pr[:, k, :], kp[:, k, :], ALU.mult))
                c.step(tt(den[:, :], pr[:, 0, :], pr[:, 1, :], ALU.add))
                c.step(ts(den[:, :], den[:, :], 1e-9, None, ALU.add))
            else:
                c.step(nc.vector.tensor_reduce(es[:, :], ex[:, :, :], AX.X, ALU.add))
                c.step(nc.vector.reciprocal(es[:, :], es[:, :]))
                for k in range(TOP_K):
                    c.step(tt(pr[:, k, :], pr[:, k, :], es[:, :], ALU.mult))
                c.step(tt(den[:, :], pr[:, 0, :], pr[:, 1, :], ALU.add))
                c.step(ts(den[:, :], den[:, :], 1e-9, None, ALU.max if m.gates == "probs_clip" else ALU.add))
            c.step(nc.vector.reciprocal(den[:, :], den[:, :]))
            for k in range(TOP_K):
                c.done(tt(r.gate[:, k, :], pr[:, k, :], den[:, :], ALU.mult))
            c.sync()
            if m.fallback:
                for k in range(TOP_K):
                    c.done(tt(r.gate[:, k, :], r.gate[:, k, :], open_[:, :], ALU.mult))
                    c.done(tt(kp[:, k, :], kp[:, k, :], open_[:, :], ALU.mult))
                c.sync()
                c.step(tt(r.gate[:, 0, :], r.gate[:, 0, :], M[0][:, R, :], ALU.add))


NOWHERE = 1 << 20


def dispatch(kit, tag, r):
    nc = kit.nc
    with ExitStack() as st:
        sb, _, sem = scoped(nc, st, tag + "_d")
        rows, where = sb("rows", [P, GT, C]), sb("where", [P, GT, TOP_K], I32)
        staged = [sem(f"staged{j}") for j in range(GT)]
        sent = [sem(f"sent{j}") for j in range(GT)]
        block = st.enter_context(nc.Block())

        @block.vector
        def _(v):
            with v.Fori(0, NG) as g:
                for j in range(GT):
                    v.wait_ge(sent[j], 32 * g)
                    nc.vector.tensor_copy(rows[:, j, :], kit.XN[:, bass.ds(g * GT + j, 1), :].squeeze(1))
                    nc.vector.tensor_copy(where[:, j, :], r.slot_out[:, bass.ds(g * GT + j, 1), :].squeeze(1)).then_inc(staged[j], 1)

        @block.gpsimd
        def _(pool):
            with pool.Fori(0, NG) as g:
                for j in range(GT):
                    pool.wait_ge(staged[j], g + 1)
                    kit.passed(pool)
                    for k in range(TOP_K):
                        nc.gpsimd.indirect_dma_start(
                            out=kit.packed[:, :], out_offset=bass.IndirectOffsetOnAxis(ap=where[:, j, k:k + 1], axis=0),
                            in_=rows[:, j, :], in_offset=None, bounds_check=SLOTS - 1, oob_is_err=False).then_inc(sent[j], 16)
            for j in range(GT):
                pool.wait_ge(sent[j], 32 * NG)


def run_experts(kit, tag, r):
    nc, m = kit.nc, MOES[tag]
    T = m.tiles
    with ExitStack() as st:
        sb, ps, sem = scoped(nc, st, tag + "_e")
        xin, xT = sb("xin", [P, 2, C]), sb("xT", [C, 2, P])
        hb, hT, y = sb("hb", [P, 2, FF]), sb("hT", [P, 2, FK, P]), sb("y", [P, 2, C])
        p_x, p_h, p_t, p_y = ([ps(f"{n}{i}", [P, 512]) for i in range(2)] for n in ("p_x", "p_h", "p_t", "p_y"))
        in_done, out_done = [sem(f"in_done{i}") for i in range(2)], [sem(f"out_done{i}") for i in range(2)]
        x_ps, xT_ready, h_ps, hb_ready, hT_ps, g_ready, y_ps, y_ready = (
            sem(n) for n in ("x_ps", "xT_ready", "h_ps", "hb_ready", "hT_ps", "g_ready", "y_ps", "y_ready"))
        experts = (kit.experts_in, kit.experts_loaded)
        block = st.enter_context(nc.Block())

        def expert(engine, i):
            return engine.value_load(r.tile_expert[0:1, bass.ds(i, 1)], min_val=0, max_val=m.experts - 1)

        def two_steps(engine, body):
            with engine.Fori(0, (T - 2) // 2) as n:
                for s in range(2):
                    body(n * 2 + (2 + s), s, n + 1)

        @block.sync
        def _(sp):
            def load(i, s, half):
                if not isinstance(i, int) or i >= 2:
                    sp.wait_ge(x_ps, i - 1)
                sp.dma_start(xin[:, s, :], kit.packed[bass.ds(i * P, P), :]).then_inc(in_done[s], 16)
            load(0, 0, 0)
            load(1, 1, 0)
            two_steps(sp, load)
            load(T, 0, T // 2)

        @block.gpsimd
        def _(pool):
            with pool.Fori(0, T // 2) as n:
                for s in range(2):
                    pool.wait_ge(y_ready, n * 2 + s + 1)
                    pool.dma_start(kit.expert_out[bass.ds((n * 2 + s) * P, P), :], y[:, s, :]).then_inc(out_done[s], 16)
            for s in range(2):
                pool.wait_ge(out_done[s], 16 * (T // 2))

        @block.scalar
        def _(act):
            def rows(i, s, first=False):
                act.wait_ge(x_ps, i + 1)
                if not first:
                    act.wait_ge(h_ps, i - 1)
                nc.scalar.activation(xT[:, s, :], p_x[s][:, 0:P], ACT.Copy).then_inc(xT_ready, 1)

            def gelu(i, s, first=False):
                act.wait_ge(hT_ps, i + 1)
                if not first:
                    act.wait_ge(y_ps, i - 1)
                nc.scalar.activation(hT[:, s].rearrange("p k t -> p (k t)"), p_t[s][:, :], ACT.Gelu).then_inc(g_ready, 1)

            def step(i, s, half):
                rows(i + 1, 1 - s)
                gelu(i - 1, 1 - s, first=False)
            rows(0, 0, True)
            rows(1, 1, True)
            rows(2, 0)
            gelu(0, 0, True)
            rows(3, 1)
            gelu(1, 1, True)
            with act.Fori(0, (T - 4) // 2) as n:
                step(n * 2 + 3, 1, 0)
                step(n * 2 + 4, 0, 0)
            step(T - 1, 1, 0)
            gelu(T - 1, 1)

        @block.vector
        def _(v):
            def add_b1(i, s, first=False):
                e = expert(v, i)
                v.wait_ge(h_ps, i + 1)
                if not first:
                    v.wait_ge(hT_ps, i - 1)
                nc.vector.tensor_tensor(hb[:, s, :], p_h[s][:, :], kit.B1[:, bass.ds(e, 1), :].squeeze(1), ALU.add).then_inc(hb_ready, 1)

            def add_b2(i, s, half):
                e = expert(v, i)
                v.wait_ge(y_ps, i + 1)
                v.wait_ge(out_done[s], half * 16)
                nc.vector.tensor_tensor(y[:, s, :], p_y[s][:, 0:C], kit.B2[:, bass.ds(e, 1), :].squeeze(1), ALU.add).then_inc(y_ready, 1)

            def step(i, s, half):
                add_b1(i, s)
                add_b2(i - 2, s, half - 1)
            v.wait_ge(*experts)
            add_b1(0, 0, True)
            add_b1(1, 1, True)
            two_steps(v, step)
            add_b2(T - 2, 0, T // 2 - 1)
            add_b2(T - 1, 1, T // 2 - 1)

        @block.tensor
        def _(pe):
            def rows(i, s, half, first=False):
                pe.wait_ge(in_done[s], 16 * half + 16)
                if not first:
                    pe.wait_ge(xT_ready, i - 1)
                nc.tensor.transpose(p_x[s][:, 0:P], xin[:, s, :], kit.ident[:, :]).then_inc(x_ps, 1)

            def up(i, s, first=False):
                e = expert(pe, i)
                pe.wait_ge(xT_ready, i + 1)
                if not first:
                    pe.wait_ge(hb_ready, i - 1)
                nc.tensor.matmul(p_h[s][:, :], xT[:, s, :], kit.W1[:, bass.ds(e, 1), :].squeeze(1), start=True, stop=True).then_inc(h_ps, 1)

            def turn(i, s, first=False):
                pe.wait_ge(hb_ready, i + 1)
                if not first:
                    pe.wait_ge(g_ready, i - 1)
                for k in range(FK):
                    ins = nc.tensor.transpose(p_t[s][:, k * P:(k + 1) * P], hb[:, s, k * P:(k + 1) * P], kit.ident[:, :])
                ins.then_inc(hT_ps, 1)

            def down(i, s, first=False):
                e = expert(pe, i)
                pe.wait_ge(g_ready, i + 1)
                if not first:
                    pe.wait_ge(y_ready, i - 1)
                for k in range(FK):
                    ins = nc.tensor.matmul(p_y[s][:, 0:C], hT[:, s, k, :], kit.W2[:, bass.ds(e, 1), k, :].squeeze(1),
                                           start=(k == 0), stop=(k == FK - 1))
                ins.then_inc(y_ps, 1)

            def step(i, s, half, first=False):
                rows(i + 1, 1 - s, half + s)
                up(i, s)
                turn(i - 1, 1 - s, first=first and s == 0)
                down(i - 2, s, first)
            pe.wait_ge(*experts)
            rows(0, 0, 0, True)
            rows(1, 1, 0, True)
            up(0, 0, True)
            rows(2, 0, 1)
            up(1, 1, True)
            turn(0, 0, True)
            step(2, 0, 1, True)
            step(3, 1, 1, True)
            with pe.Fori(0, (T - 4) // 2) as n:
                for s in range(2):
                    step(n * 2 + 4 + s, s, n + 2)
            turn(T - 1, 1)
            down(T - 2, 0)
            down(T - 1, 1)


def combine(kit, tag, r):
    nc = kit.nc
    with ExitStack() as st:
        sb, _, sem = scoped(nc, st, tag + "_c")
        rows, where = sb("rows", [P, GT, TOP_K, C]), sb("where", [P, GT, TOP_K], I32)
        staged, used, dve = sem("staged"), [sem(f"used{j}") for j in range(GT)], sem("dve")
        here = [sem(f"here{j}") for j in range(GT)]
        block = st.enter_context(nc.Block())

        @block.vector
        def _(v):
            c = Chain(v, dve, GT)
            with v.Fori(0, NG) as g:
                c.start(g)
                nc.vector.tensor_copy(where[:, :, :], r.slot_back[:, bass.ds(g * GT, GT), :]).then_inc(staged, 1)
                for j in range(GT):
                    t = bass.ds(g * GT + j, 1)
                    x = kit.X[:, t, :].squeeze(1)
                    v.wait_ge(here[j], 32 * g + 32)
                    c.step(nc.vector.scalar_tensor_tensor(x, rows[:, j, 0, :], r.gate[:, 0, t], x, ALU.mult, ALU.add))
                    nc.vector.scalar_tensor_tensor(x, rows[:, j, 1, :], r.gate[:, 1, t], x, ALU.mult, ALU.add).then_inc(used[j], 1)

        @block.gpsimd
        def _(pool):
            with pool.Fori(0, NG) as g:
                pool.wait_ge(staged, g + 1)
                for j in range(GT):
                    pool.wait_ge(used[j], g)
                    kit.passed(pool)
                    for k in range(TOP_K):
                        nc.gpsimd.indirect_dma_start(
                            out=rows[:, j, k, :], out_offset=None, in_=kit.expert_out[0:MOES[tag].tiles * P, :],
                            in_offset=bass.IndirectOffsetOnAxis(ap=where[:, j, k:k + 1], axis=0)).then_inc(here[j], 16)


def attention(kit, tag):
    nc, A = kit.nc, kit.A
    SCALE = C ** -0.5
    NB = GROUP // S
    with ExitStack() as st:
        sb, ps, sem = scoped(nc, st, tag)
        w = {n: sb(n, [C, C]) for n in ("Wq", "Wk", "Wv", "Wo")}
        bias = {n: sb(n, [C, 1]) for n in ("bq", "bk", "bv")}
        bo = sb("bo", [P, C])
        cT = sb("cT", [C, GROUP])
        stats, mv, var, rstd = sb("stats", [P, GT, 6]), sb("mv", [P, GT, 2]), sb("var", [P, GT]), sb("rstd", [P, GT])
        xn, xnT = sb("xn", [P, GT, C]), sb("xnT", [C, GROUP])
        QT, KT, V = sb("QT", [C, GROUP]), sb("KT", [C, GROUP]), sb("V", [S, NB, C])
        Pm, mx, su = sb("Pm", [P, PAIRS, S]), sb("mx", [P, PAIRS]), sb("su", [P, PAIRS])
        PT, aT = sb("PT", [S, GROUP]), sb("aT", [C, GROUP])
        p_x, p_q, p_k, p_s, p_t, p_a = (ps(n, [P, 512]) for n in ("p_x", "p_q", "p_k", "p_s", "p_t", "p_a"))
        p_v = ps("p_v", [P, 1024])
        weights, ctx_in, var_ready, rstd_ready = (sem(n) for n in ("weights", "ctx_in", "var_ready", "rstd_ready"))
        xn_ready, xT_ps, xnT_ready, q_ps, k_ps, v_ps = (sem(n) for n in ("xn_ready", "xT_ps", "xnT_ready", "q_ps", "k_ps", "v_ps"))
        qT_ready, kT_ready, v_ready, s_ps, d_ready, e_ready = (sem(n) for n in ("qT_ready", "kT_ready", "v_ready", "s_ps", "d_ready", "e_ready"))
        p_ready, t_ps, pT_ready, a_ps, a_ready, y_ps, bo_added, dve = (
            sem(n) for n in ("p_ready", "t_ps", "pT_ready", "a_ps", "a_ready", "y_ps", "bo_added", "dve"))
        N_WEIGHTS = 16 * 8
        X = kit.X
        block = st.enter_context(nc.Block())

        @block.sync
        def _(sp):
            for n in w:
                sp.dma_start(w[n][:, :], A[f"{tag}_{n}"]).then_inc(weights, 16)
            for n in bias:
                sp.dma_start(bias[n][:, :], A[f"{tag}_{n}"].rearrange("(c a) -> c a", a=1)).then_inc(weights, 16)
            sp.dma_start(bo[:, :], A[f"{tag}_bo"].rearrange("(a c) -> a c", a=1).to_broadcast([P, C])).then_inc(weights, 16)
            with sp.Fori(0, NG) as g:
                sp.wait_ge(v_ps, g)
                sp.dma_start(cT[:, :], A["ctxT"][:, bass.ds(g * GROUP, GROUP)]).then_inc(ctx_in, 16)

        @block.gpsimd
        def _(pool):
            pool.wait_ge(weights, N_WEIGHTS)
            with pool.Fori(0, NG) as g:
                xg = X[:, bass.ds(g * GT, GT), :]
                inverse_root(nc, pool, var, var_ready, rstd, rstd_ready, kit.minus_half, g)
                pool.wait_ge(xn_ready, g + 1)
                nc.gpsimd.tensor_tensor(xg, xg, bo[:, :].unsqueeze(1).to_broadcast([P, GT, C]), ALU.add).then_inc(bo_added, 1)

        @block.scalar
        def _(act):
            act.wait_ge(weights, N_WEIGHTS)
            with act.Fori(0, NG) as g:
                act.wait_ge(v_ps, g + 1)
                nc.scalar.activation(V[:, :, :].rearrange("k b c -> k (b c)"), p_v[0:S, :], ACT.Copy).then_inc(v_ready, 1)
                act.wait_ge(xT_ps, g + 1)
                nc.scalar.activation(xnT[:, :], p_x[:, :], ACT.Copy).then_inc(xnT_ready, 1)
                act.wait_ge(q_ps, g + 1)
                nc.scalar.activation(QT[:, :], p_q[:, :], ACT.Identity, bias=bias["bq"][:, :]).then_inc(qT_ready, 1)
                act.wait_ge(d_ready, g + 1)
                nc.scalar.activation(Pm[:, :, :], Pm[:, :, :], ACT.Exp, scale=SCALE).then_inc(e_ready, 1)
                act.wait_ge(t_ps, g + 1)
                nc.scalar.activation(PT[:, :], p_t[0:S, :], ACT.Copy).then_inc(pT_ready, 1)

        @block.vector
        def _(v):
            c = Chain(v, dve, LN_STEPS + 4)
            v.wait_ge(weights, N_WEIGHTS)
            with v.Fori(0, NG) as g:
                c.start(g)
                layernorm(nc, v, c, lambda j: X[:, bass.ds(g * GT + j, 1), :].squeeze(1), xn, stats, mv, var, var_ready,
                          rstd, rstd_ready, g, kit.passed).then_inc(xn_ready, 1)
                v.wait_ge(k_ps, g + 1)
                nc.vector.tensor_scalar(KT[:, :], p_k[:, :], bias["bk"][:, :], None, ALU.add).then_inc(kT_ready, 1)
                v.wait_ge(s_ps, g + 1)
                s3 = p_s[:, 0:PAIRS * S].rearrange("p (j k) -> p j k", k=S)
                c.step(nc.vector.tensor_reduce(mx[:, :], s3, AX.X, ALU.max))
                nc.vector.tensor_tensor(Pm[:, :, :], s3, mx[:, :].unsqueeze(2).to_broadcast([P, PAIRS, S]), ALU.subtract).then_inc(d_ready, 1)
                v.wait_ge(e_ready, g + 1)
                c.step(nc.vector.tensor_reduce(su[:, :], Pm[:, :, :], AX.X, ALU.add))
                c.step(nc.vector.reciprocal(su[:, :], su[:, :]))
                nc.vector.tensor_tensor(Pm[:, :, :], Pm[:, :, :], su[:, :].unsqueeze(2).to_broadcast([P, PAIRS, S]), ALU.mult).then_inc(p_ready, 1)
                v.wait_ge(a_ps, g + 1)
                nc.vector.scalar_tensor_tensor(aT[:, :], p_a[:, :], bias["bv"][:, :], xnT[:, :], ALU.add, ALU.add).then_inc(a_ready, 1)
                v.wait_ge(y_ps, g + 1)
                v.wait_ge(bo_added, g + 1)
                xg = X[:, bass.ds(g * GT, GT), :]
                c.step(nc.vector.tensor_tensor(xg, xg, p_x[:, :].rearrange("p (t c) -> p t c", c=C), ALU.add))

        @block.tensor
        def _(pe):
            pe.wait_ge(weights, N_WEIGHTS)
            with pe.Fori(0, NG) as g:
                pe.wait_ge(ctx_in, 16 * g + 16)
                nc.tensor.matmul(p_k[:, :], w["Wk"][:, :], cT[:, :], start=True, stop=True).then_inc(k_ps, 1)
                for b in range(NB):
                    ins = nc.tensor.matmul(p_v[0:S, b * C:(b + 1) * C], cT[:, b * S:(b + 1) * S], w["Wv"][:, :], start=True, stop=True)
                ins.then_inc(v_ps, 1)
                pe.wait_ge(xn_ready, g + 1)
                for j in range(GT):
                    ins = nc.tensor.transpose(p_x[:, j * P:(j + 1) * P], xn[:, j, :], kit.ident[:, :])
                ins.then_inc(xT_ps, 1)
                pe.wait_ge(xnT_ready, g + 1)
                nc.tensor.matmul(p_q[:, :], w["Wq"][:, :], xnT[:, :], start=True, stop=True).then_inc(q_ps, 1)
                pe.wait_ge(kT_ready, g + 1)
                pe.wait_ge(qT_ready, g + 1)
                kit.passed(pe)
                for b in range(NB):
                    t = slice(b * S, (b + 1) * S)
                    ins = nc.tensor.matmul(p_s[b % 2 * S:(b % 2 + 1) * S, b // 2 * S:(b // 2 + 1) * S], QT[:, t], KT[:, t],
                                           start=True, stop=True)
                ins.then_inc(s_ps, 1)
                pe.wait_ge(p_ready, g + 1)
                kit.passed(pe)
                for j in range(PAIRS):
                    ins = nc.tensor.transpose(p_t[0:S, j * P:(j + 1) * P], Pm[:, j, :], kit.ident[:, :])
                ins.then_inc(t_ps, 1)
                pe.wait_ge(v_ready, g + 1)
                pe.wait_ge(pT_ready, g + 1)
                kit.passed(pe)
                for b in range(NB):
                    ins = nc.tensor.matmul(p_a[:, b * S:(b + 1) * S], V[:, b, :], PT[:, b * S:(b + 1) * S], start=True, stop=True)
                ins.then_inc(a_ps, 1)
                pe.wait_ge(a_ready, g + 1)
                for j in range(GT):
                    ins = nc.tensor.matmul(p_x[:, j * C:(j + 1) * C], aT[:, j * P:(j + 1) * P], w["Wo"][:, :], start=True, stop=True)
                ins.then_inc(y_ps, 1)


def mlstm(kit, tag):
    nc, A = kit.nc, kit.A
    H, DH = 8, 16
    HH = H // 2
    NB = GROUP // S
    VW = 2 * 2 * DH + 2
    EPS = 1e-6
    FAR = -1e30
    with ExitStack() as st:
        sb, ps, sem = scoped(nc, st, tag)
        gate_w = sb("gate_w", [C, 3, 40])
        ib, fb = sb("ib", [H, 1]), sb("fb", [H, 1])
        out_w = sb("out_w", [P, C // 2])
        head_mask, half_mask, fold = sb("head_mask", [P, HH]), sb("half_mask", [P, C]), sb("fold", [P, S])
        pick = sb("pick", [P, 2, S])
        hoh, foh = sb("hoh", [H, HH]), sb("foh", [H, 2])
        later32, later = sb("later32", [S, S]), sb("later", [S, 2 * HH, S], BF16)
        ident2 = sb("ident2", [S, 2, S], BF16)
        cT, c2 = sb("cT", [C, GROUP]), sb("c2", [P, NB, C])
        stats, mv, var, rstd = sb("stats", [P, GT, 6]), sb("mv", [P, GT, 2]), sb("var", [P, GT]), sb("rstd", [P, GT])
        xn, xnT = sb("xn", [P, GT, C]), sb("xnT", [C, GROUP])
        QT = sb("QT", [C, NB, 2, S])
        Km = sb("Km", [C, 2, 2, HH, S])
        V2 = sb("V2", [P, NB, 2, VW])
        i_, f_, na, lf, cs, gm, M = (sb(n, [H, GROUP]) for n in ("i_", "f_", "na", "lf", "cs", "gm", "M"))
        restart, drop = sb("restart", [H, GROUP]), sb("drop", [H, GROUP])
        left = sb("left", [P, NB, 2, S])
        right = sb("right", [P, 2, 2, HH, S])
        nm = sb("nm", [H, NB, 2, S])
        D, Cm = sb("D", [P, 2, GROUP]), sb("Cm", [P, 2, GROUP])
        CT = sb("CT", [P, GROUP])
        en = sb("en", [P, PAIRS, 2 * HH])
        nrm = sb("nrm", [P, 2, 2 * HH])
        hh = sb("hh", [P, PAIRS * 2 * HH, DH])
        sq = sb("sq", [P, PAIRS * 2 * HH, DH])
        mean, hv, hr = (sb(n, [P, PAIRS * 2 * HH]) for n in ("mean", "hv", "hr"))
        minus_half = sb("minus_half", [P, PAIRS * 2 * HH])
        p_x, p_g, p_q, p_t, p_o = (ps(n, [P, 512]) for n in ("p_x", "p_g", "p_q", "p_t", "p_o"))
        p_d = [ps(f"p_d{i}", [P, 512]) for i in range(2)]
        names = ("weights set_up ctx_in ctx2_in var_ready rstd_ready xn_ready xT_ps xnT_ready qT_ready g_ps na_ready "
                 "l_ready m_ready km_ready right_ready d_ps q_ps e_ready v_ready c_ready t_ps cT_ready o_ps n_ps en_ready "
                 "h_ready hv_ready hr_ready hn_ready y_ps dve act_set")
        s_ = {n: sem(n) for n in names.split()}
        N_WEIGHTS = 16 * 12
        X = kit.X
        SET_UP = 16
        block = st.enter_context(nc.Block())

        @block.sync
        def _(sp):
            row = lambda name, parts, n: A[name].rearrange("(a c) -> a c", a=1).to_broadcast([parts, n])
            col = lambda name: A[name].rearrange("(c a) -> c a", a=1)
            for dst, src in ((gate_w[:, :, :], A[f"{tag}_gate_w"]), (ib[:, :], col(f"{tag}_igate_b")), (fb[:, :], col(f"{tag}_fgate_b")),
                             (head_mask[:, :], A["head_mask16"]), (half_mask[:, :], A["half_mask16"]), (fold[:, :], A["fold"]),
                             (pick[:, :, :].rearrange("p f s -> p (f s)"), A["ident"]), (hoh[:, :], A["head_of_half"]),
                             (foh[:, :], A["half_of_head"]), (later32[:, :], A["later"])):
                sp.dma_start(dst, src).then_inc(s_["weights"], 16)
            for f in range(2):
                half = A[f"{tag}_out_w"][f * 64:f * 64 + 64]
                sp.dma_start(out_w[f * S:(f + 1) * S, :], half.rearrange("(a c) -> a c", a=1).to_broadcast([S, C // 2])).then_inc(s_["weights"], 16)
            with sp.Fori(0, NG) as g:
                sp.wait_ge(s_["g_ps"], g)
                kit.passed(sp)
                sp.wait_ge(s_["km_ready"], PAIRS * g)
                kit.passed(sp)
                sp.dma_start(cT[:, :], A["ctxT"][:, bass.ds(g * GROUP, GROUP)]).then_inc(s_["ctx_in"], 16)
                sp.wait_ge(s_["v_ready"], g)
                kit.passed(sp)
                for twice in range(2):
                    sp.dma_start(c2[twice * S:(twice + 1) * S, :, :],
                                 A["ctx"][bass.ds(g * GROUP, GROUP), :].rearrange("(b s) c -> s b c", s=S)).then_inc(s_["ctx2_in"], 16)

        @block.gpsimd
        def _(pool):
            pool.wait_ge(s_["weights"], N_WEIGHTS)
            pool.wait_ge(s_["set_up"], SET_UP)
            with pool.Fori(0, NG) as g:
                inverse_root(nc, pool, var, s_["var_ready"], rstd, s_["rstd_ready"], kit.minus_half, g)
                pool.wait_ge(s_["ctx_in"], 16 * g + 16)
                for j in range(PAIRS):
                    if j >= 2:
                        pool.wait_ge(s_["q_ps"], PAIRS * g + j - 1)
                    for b in range(2):
                        t = slice(j * P + b * S, j * P + (b + 1) * S)
                        ins = nc.gpsimd.tensor_tensor(Km[:, j % 2, b], cT[:, t].unsqueeze(1).to_broadcast([C, HH, S]),
                                                      head_mask[:, :].unsqueeze(2).to_broadcast([C, HH, S]), ALU.mult)
                    ins.then_inc(s_["km_ready"], 1)
                    if j == 0:
                        pool.wait_ge(s_["m_ready"], g + 1)
                    if j >= 2:
                        pool.wait_ge(s_["d_ps"], PAIRS * g + j - 1)
                    for b in range(2):
                        t = slice(j * P + b * S, j * P + (b + 1) * S)
                        ins = nc.gpsimd.tensor_tensor(right[0:H, j % 2, b], gm[:, t].unsqueeze(1).to_broadcast([H, HH, S]),
                                                      hoh[:, :].unsqueeze(2).to_broadcast([H, HH, S]), ALU.mult)
                    ins.then_inc(s_["right_ready"], 1)
                pool.wait_ge(s_["hv_ready"], g + 1)
                nc.gpsimd.tensor_tensor(hr[:, :], hv[:, :], minus_half[:, :], ALU.pow).then_inc(s_["hr_ready"], 1)

        @block.scalar
        def _(act):
            act.wait_ge(s_["weights"], N_WEIGHTS)
            act.wait_ge(s_["set_up"], SET_UP)
            with act.Fori(0, NG) as g:
                act.wait_ge(s_["xT_ps"], g + 1)
                nc.scalar.activation(xnT[:, :], p_x[:, :], ACT.Copy).then_inc(s_["xnT_ready"], 1)
                for f in range(2):
                    rows = slice(64 * f, 64 * f + 64)
                    ins = nc.scalar.activation(QT[rows, :, f, :], p_x[rows, :].rearrange("c (b s) -> c b s", s=S), ACT.Copy)
                ins.then_inc(s_["qT_ready"], 1)
                act.wait_ge(s_["na_ready"], g + 1)
                nc.scalar.activation(na[:, :], na[:, :], ACT.Exp).then_inc(s_["act_set"], 1)
                act.wait_ge(s_["act_set"], g + 1)
                nc.scalar.activation(na[:, :], na[:, :], ACT.Ln, bias=1.0).then_inc(s_["l_ready"], 1)

                def exponent(j):
                    act.wait_ge(s_["d_ps"], PAIRS * g + j + 1)
                    nc.scalar.activation(D[:, j % 2, :], p_d[j % 2][:, :], ACT.Exp).then_inc(s_["e_ready"], 1)

                def turned(j):
                    act.wait_ge(s_["t_ps"], PAIRS * g + j + 1)
                    nc.scalar.activation(CT[:, :], p_t[:, :], ACT.Copy).then_inc(s_["cT_ready"], 1)

                act.wait_ge(s_["n_ps"], g + 1)
                nc.scalar.activation(en[:, :, :].rearrange("p j h -> p (j h)"), p_g[:, 0:PAIRS * 2 * HH], ACT.Exp).then_inc(s_["en_ready"], 1)
                exponent(0)
                for j in range(PAIRS):
                    if j + 1 < PAIRS:
                        exponent(j + 1)
                    turned(j)

        @block.vector
        def _(v):
            tt, ts, stt = nc.vector.tensor_tensor, nc.vector.tensor_scalar, nc.vector.scalar_tensor_tensor
            up, at = s_["set_up"], 0

            def setup(ins):
                nonlocal at
                at += 1
                ins.then_inc(up, 1)
                v.wait_ge(up, at)

            v.wait_ge(s_["weights"], N_WEIGHTS)
            setup(nc.vector.memset(left[:, :, :, :], 0.0))
            setup(nc.vector.memset(right[:, :, :, :, :], 0.0))
            setup(tt(left[0:H].rearrange("h b f s -> h b f s"), left[0:H], foh[:, :].unsqueeze(1).unsqueeze(3).to_broadcast([H, NB, 2, S]), ALU.add))
            for n in range(2):
                setup(tt(right[32:40, n], right[32:40, n], hoh[:, :].unsqueeze(1).unsqueeze(3).to_broadcast([H, 2, HH, S]), ALU.add))
            setup(nc.vector.memset(restart[:, :], 1.0))
            setup(nc.vector.memset(restart[:, :].rearrange("h (b s) -> h b s", s=S)[:, :, 0], 0.0))
            setup(nc.vector.memset(drop[:, :], 0.0))
            setup(nc.vector.memset(drop[:, :].rearrange("h (b s) -> h b s", s=S)[:, :, 0], FAR))
            setup(nc.vector.memset(V2[:, :, :, 4 * DH:VW], 0.0))
            setup(nc.vector.memset(V2[0:S, :, :, 4 * DH:4 * DH + 1], 1.0))
            setup(nc.vector.memset(V2[S:P, :, :, 4 * DH + 1:VW], 1.0))
            setup(nc.vector.memset(QT[:, :, :, :], 0.0))
            setup(nc.vector.memset(minus_half[:, :], -0.5))
            setup(nc.vector.tensor_copy(ident2[:, :, :], pick[0:S, 0, :].unsqueeze(1).to_broadcast([S, 2, S])))
            setup(nc.vector.tensor_copy(later[:, :, :], later32[:, :].unsqueeze(1).to_broadcast([S, 2 * HH, S])))
            assert at == SET_UP
            c = Chain(v, s_["dve"], LN_STEPS + 9 + 4 * PAIRS + 6 + 1)
            with v.Fori(0, NG) as g:
                c.start(g)
                layernorm(nc, v, c, lambda j: X[:, bass.ds(g * GT + j, 1), :].squeeze(1), xn, stats, mv, var, s_["var_ready"],
                          rstd, s_["rstd_ready"], g, kit.passed).then_inc(s_["xn_ready"], 1)
                v.wait_ge(s_["ctx2_in"], 32 * g + 32)
                hm = half_mask[:, :].rearrange("p (f i c) -> p i f c", f=2, c=2 * DH)
                for b in range(NB):
                    ins = tt(V2[:, b, :, 0:4 * DH].rearrange("p i (f c) -> p i f c", f=2),
                             c2[:, b, :].rearrange("p (f i c) -> p i f c", f=2, c=2 * DH), hm, ALU.mult)
                ins.then_inc(s_["v_ready"], 1)
                v.wait_ge(s_["g_ps"], g + 1)
                c.done(ts(f_[:, :], p_g[32:40, :], fb[:, :], None, ALU.add))
                c.done(ts(i_[:, :], p_g[0:H, :], ib[:, :], None, ALU.add))
                c.sync()
                stt(na[:, :], f_[:, :], -1.0, f_[:, :], ALU.mult, ALU.min).then_inc(s_["na_ready"], 1)
                v.wait_ge(s_["l_ready"], g + 1)
                c.step(stt(lf[:, :], f_[:, :], 0.0, na[:, :], ALU.min, ALU.subtract))
                c.step(nc.vector.tensor_tensor_scan(cs[:, :], restart[:, :], lf[:, :], 0.0, ALU.mult, ALU.add))
                c.step(tt(gm[:, :], i_[:, :], cs[:, :], ALU.subtract))
                c.step(nc.vector.tensor_tensor_scan(M[:, :], drop[:, :], gm[:, :], FAR, ALU.add, ALU.max))
                both = foh[:, :].unsqueeze(1).unsqueeze(3).to_broadcast([H, NB, 2, S])
                v3 = lambda t: t[:, :].rearrange("h (b s) -> h b s", s=S).unsqueeze(2).to_broadcast([H, NB, 2, S])
                c.step(stt(lf[:, :], cs[:, :], -1.0, M[:, :], ALU.mult, ALU.subtract))
                c.step(ts(M[:, :], M[:, :], -1.0, None, ALU.mult))
                c.done(tt(left[32:40], v3(M), both, ALU.mult))
                tt(nm[:, :, :, :], v3(lf), both, ALU.mult).then_inc(s_["m_ready"], 1)

                def product(j):
                    v.wait_ge(s_["e_ready"], PAIRS * g + j + 1)
                    v.wait_ge(s_["q_ps"], PAIRS * g + j + 1)
                    stt(Cm[:, j % 2, :], p_q[:, :], DH ** -0.5, D[:, j % 2, :], ALU.mult, ALU.mult).then_inc(s_["c_ready"], 1)

                def normalise(j):
                    v.wait_ge(s_["o_ps"], PAIRS * g + j + 1)
                    po = p_o[:, 0:4 * VW].rearrange("p (h c) -> p h c", c=VW)
                    n = nrm[:, j % 2, :]
                    if j == 0:
                        v.wait_ge(s_["en_ready"], g + 1)
                    c.step(nc.vector.tensor_copy(n.rearrange("p (h c) -> p h c", c=2), po[:, :, 4 * DH:VW]))
                    c.step(stt(n, n, -1.0, n, ALU.mult, ALU.max))
                    c.step(tt(n, n, en[:, j, :], ALU.max))
                    c.step(ts(n, n, EPS, None, ALU.add))
                    nc.vector.reciprocal(n, n).then_inc(s_["h_ready"], 1)
                    v.wait_ge(s_["h_ready"], 2 * (PAIRS * g + j) + 1)
                    for f in range(2):
                        q = slice(f * S, (f + 1) * S)
                        ins = tt(hh[q, j * 2 * HH:(j + 1) * 2 * HH, :].rearrange("p (h a) c -> p h a c", a=2),
                                 po[q, :, f * 2 * DH:(f + 1) * 2 * DH].rearrange("p h (a c) -> p h a c", c=DH),
                                 n[q].rearrange("p (h a) -> p h a", a=2).unsqueeze(3).to_broadcast([S, HH, 2, DH]), ALU.mult)
                    ins.then_inc(s_["h_ready"], 1)

                product(0)
                for j in range(PAIRS):
                    if j + 1 < PAIRS:
                        product(j + 1)
                    normalise(j)
                v.wait_ge(s_["h_ready"], 2 * PAIRS * (g + 1))
                N = PAIRS * 2 * HH
                wide = lambda t: t[:, :].unsqueeze(2).to_broadcast([P, N, DH])
                c.step(nc.vector.tensor_reduce(mean[:, :], hh[:, :, :], AX.X, ALU.add))
                c.step(ts(mean[:, :], mean[:, :], 1.0 / DH, None, ALU.mult))
                c.step(tt(hh[:, :, :], hh[:, :, :], wide(mean), ALU.subtract))
                c.step(tt(sq[:, :, :], hh[:, :, :], hh[:, :, :], ALU.mult))
                c.step(nc.vector.tensor_reduce(hv[:, :], sq[:, :, :], AX.X, ALU.add))
                ts(hv[:, :], hv[:, :], 1.0 / DH, LN_EPS, ALU.mult, ALU.add).then_inc(s_["hv_ready"], 1)
                v.wait_ge(s_["hr_ready"], g + 1)
                c.step(tt(hh[:, :, :], hh[:, :, :], wide(hr), ALU.mult))
                tt(hh[:, :, :].rearrange("p (j h) c -> p j (h c)", h=HH), hh[:, :, :].rearrange("p (j h) c -> p j (h c)", h=HH),
                   out_w[:, :].unsqueeze(1).to_broadcast([P, NB, C // 2]), ALU.mult).then_inc(s_["hn_ready"], 1)
                v.wait_ge(s_["y_ps"], g + 1)
                xg = X[:, bass.ds(g * GT, GT), :]
                c.step(tt(xg, xg, p_x[:, :].rearrange("p (t c) -> p t c", c=C), ALU.add))

        @block.tensor
        def _(pe):
            pe.wait_ge(s_["weights"], N_WEIGHTS)
            pe.wait_ge(s_["set_up"], SET_UP)
            with pe.Fori(0, NG) as g:
                pe.wait_ge(s_["xn_ready"], g + 1)
                for j in range(GT):
                    ins = nc.tensor.transpose(p_x[:, j * P:(j + 1) * P], xn[:, j, :], kit.ident[:, :])
                ins.then_inc(s_["xT_ps"], 1)
                pe.wait_ge(s_["ctx_in"], 16 * g + 16)
                kit.passed(pe)
                nc.tensor.matmul(p_g[0:40, :], gate_w[:, 1, :], cT[:, :], start=True, stop=False)
                nc.tensor.matmul(p_g[0:40, :], gate_w[:, 2, :], cT[:, :], start=False, stop=False)
                pe.wait_ge(s_["xnT_ready"], g + 1)
                kit.passed(pe)
                nc.tensor.matmul(p_g[0:40, :], gate_w[:, 0, :], xnT[:, :], start=False, stop=True).then_inc(s_["g_ps"], 1)

                def decays(j):
                    if j >= 2:
                        pe.wait_ge(s_["e_ready"], PAIRS * g + j - 1)
                    pe.wait_ge(s_["right_ready"], PAIRS * g + j + 1)
                    kit.passed(pe)
                    for b in range(2):
                        nc.tensor.matmul(p_d[j % 2][:, b * 256:(b + 1) * 256], left[:, 2 * j + b], right[:, j % 2, b], start=(b == 0),
                                         stop=False, skip_group_check=True)
                    nc.tensor.matmul(p_d[j % 2][:, :], ident2[:, :, :], later[:, :, :], start=False, stop=True,
                                     skip_group_check=True).then_inc(s_["d_ps"], 1)

                def products(j):
                    if j == 0:
                        pe.wait_ge(s_["qT_ready"], g + 1)
                    pe.wait_ge(s_["km_ready"], PAIRS * g + j + 1)
                    pe.wait_ge(s_["c_ready"], PAIRS * g + j)
                    for b in range(2):
                        ins = nc.tensor.matmul(p_q[:, b * 256:(b + 1) * 256], QT[:, 2 * j + b], Km[:, j % 2, b], start=True, stop=True)
                    ins.then_inc(s_["q_ps"], 1)

                def values(j):
                    pe.wait_ge(s_["c_ready"], PAIRS * g + j + 1)
                    if j >= 1:
                        pe.wait_ge(s_["cT_ready"], PAIRS * g + j)
                    for i in range(4):
                        ins = nc.tensor.transpose(p_t[:, i * P:(i + 1) * P], Cm[:, j % 2, i * P:(i + 1) * P], kit.ident[:, :])
                    ins.then_inc(s_["t_ps"], 1)

                def sums(j):
                    if j == 0:
                        pe.wait_ge(s_["v_ready"], g + 1)
                    pe.wait_ge(s_["h_ready"], 2 * (PAIRS * g + j))
                    pe.wait_ge(s_["cT_ready"], PAIRS * g + j + 1)
                    for i in range(4):
                        ins = nc.tensor.matmul(p_o[:, i * VW:(i + 1) * VW], CT[:, i * P:(i + 1) * P], V2[:, 2 * j + i // 2, i % 2, :],
                                               start=True, stop=True)
                    ins.then_inc(s_["o_ps"], 1)

                pe.wait_ge(s_["m_ready"], g + 1)
                kit.passed(pe)
                for b in range(NB):
                    ins = nc.tensor.matmul(p_g[:, b * HH:(b + 1) * HH], nm[:, b], hoh[:, :], start=True, stop=True)
                ins.then_inc(s_["n_ps"], 1)
                decays(0)
                products(0)
                for j in range(PAIRS):
                    if j + 1 < PAIRS:
                        decays(j + 1)
                    values(j)
                    if j + 1 < PAIRS:
                        products(j + 1)
                    sums(j)
                pe.wait_ge(s_["hn_ready"], g + 1)
                kit.passed(pe)
                for j in range(PAIRS):
                    for b in range(2):
                        for f in range(2):
                            at = (2 * j + b) * HH
                            ins = nc.tensor.matmul(p_x[b * S:(b + 1) * S, j * C + f * 64:j * C + f * 64 + 64], pick[:, f, :],
                                                   hh[:, at:at + HH, :], start=True, stop=True)
                ins.then_inc(s_["y_ps"], 1)


def quantised_ffn(kit, tag):
    nc, A = kit.nc, kit.A
    TAPS = 3
    NB = 2
    ROUND = 1.5 * 2.0 ** 23
    with ExitStack() as st:
        sb, ps, sem = scoped(nc, st, tag)
        w1, w2 = sb("w1", [C, FF]), sb("w2", [P, FK, C])
        taps, conv_b = sb("taps", [P, TAPS, FF]), sb("conv_b", [P, FF])
        w1t, w2q = sb("w1t", [C, TAPS, FF]), sb("w2q", [P, FK, C], BF16)
        ones, identb = sb("ones", [P, P]), sb("identb", [P, P], BF16)
        wsum, wmean, wscale = sb("wsum", [P, 2]), sb("wmean", [P, 2]), sb("wscale", [P, 2])
        wq = sb("wq", [P, FF])
        stats, mv, var, rstd = sb("stats", [P, GT, 6]), sb("mv", [P, GT, 2]), sb("var", [P, GT]), sb("rstd", [P, GT])
        xn = sb("xn", [P, GT, C])
        amax, ascale, aback = sb("amax", [P, GT]), sb("ascale", [P, GT]), sb("aback", [P, GT])
        xT = sb("xT", [C, TAPS, GROUP])
        h = sb("h", [P, 2, FF])
        hmax, hscale, hback = sb("hmax", [P, 2]), sb("hscale", [P, 2]), sb("hback", [P, 2])
        hq, hT = sb("hq", [P, 2, FF], BF16), sb("hT", [P, 2, FF], BF16)
        p_x, p_w = ps("p_x", [P, 512]), ps("p_w", [P, 512])
        p_h = [ps(f"p_h{i}", [P, FF]) for i in range(2)]
        p_t = [ps(f"p_t{i}", [P, 2 * FF], BF16) for i in range(2)]
        p_y = [ps(f"p_y{i}", [P, 512]) for i in range(2)]
        weights, set_up, w_ps, var_ready, rstd_ready = (sem(n) for n in ("weights", "set_up", "w_ps", "var_ready", "rstd_ready"))
        xn_ready, xT_ps, xT_ready, h_ps, hb_ready, s_ready, hq_ready, hT_ps, hT_ready, y_ps, y_done, dve = (
            sem(n) for n in "xn_ready xT_ps xT_ready h_ps hb_ready s_ready hq_ready hT_ps hT_ready y_ps y_done dve".split())
        N_WEIGHTS = 16 * 8
        X = kit.X
        block = st.enter_context(nc.Block())

        @block.sync
        def _(sp):
            for dst, src in ((w1[:, :], A[f"{tag}_w1"]), (w2[:, :, :], A[f"{tag}_w2"]), (ones[:, :], A["ones"])):
                sp.dma_start(dst, src).then_inc(weights, 16)
            for k in range(TAPS):
                sp.dma_start(taps[:, k, :], A[f"{tag}_conv_w"][k:k + 1, :].to_broadcast([P, FF])).then_inc(weights, 16)
            sp.dma_start(conv_b[:, :], A[f"{tag}_conv_b"].rearrange("(a c) -> a c", a=1).to_broadcast([P, FF])).then_inc(weights, 16)
            sp.dma_start(wq[:, 0:P], A["ident"]).then_inc(weights, 16)

        @block.gpsimd
        def _(pool):
            with pool.Fori(0, NG) as g:
                inverse_root(nc, pool, var, var_ready, rstd, rstd_ready, kit.minus_half, g)

        @block.vector
        def _(v):
            tt, ts, stt = nc.vector.tensor_tensor, nc.vector.tensor_scalar, nc.vector.scalar_tensor_tensor
            at = 0

            def setup(ins):
                nonlocal at
                at += 1
                ins.then_inc(set_up, 1)
                v.wait_ge(set_up, at)

            v.wait_ge(weights, N_WEIGHTS)
            setup(nc.vector.tensor_copy(identb[:, :], wq[:, 0:P]))
            setup(nc.vector.memset(xT[:, :, :], 0.0))
            both = (w1[:, :], w2[:, :, :].rearrange("p k c -> p (k c)"))
            for n in range(2):
                setup(nc.vector.tensor_reduce(wsum[:, n:n + 1], both[n], AX.X, ALU.add, apply_absolute_value=True))
            v.wait_ge(w_ps, 1)
            setup(ts(wmean[:, :], p_w[:, 0:2], 1.0 / (C * FF), 1e-5, ALU.mult, ALU.max))
            setup(nc.vector.reciprocal(wscale[:, :], wmean[:, :]))

            def ternary(n):
                setup(ts(wq[:, :], both[n], wscale[:, n:n + 1], ROUND, ALU.mult, ALU.add))
                setup(ts(wq[:, :], wq[:, :], ROUND, None, ALU.subtract))
                setup(ts(wq[:, :], wq[:, :], -1.0, 1.0, ALU.max, ALU.min))

            ternary(1)
            setup(nc.vector.tensor_copy(w2q[:, :, :].rearrange("p k c -> p (k c)"), wq[:, :]))
            ternary(0)
            setup(ts(wq[:, :], wq[:, :], wmean[:, 0:1], None, ALU.mult))
            for k in range(TAPS):
                setup(tt(w1t[:, k, :], wq[:, :], taps[:, k, :], ALU.mult))
            c = Chain(v, dve, LN_STEPS + 6 + 5 * GT)
            with v.Fori(0, NG) as g:
                c.start(g)
                ins = layernorm(nc, v, c, lambda j: X[:, bass.ds(g * GT + j, 1), :].squeeze(1), xn, stats, mv, var, var_ready,
                                rstd, rstd_ready, g, kit.passed)
                c.done(ins)
                c.sync()
                c.step(nc.vector.tensor_reduce(amax[:, :], xn[:, :, :], AX.X, ALU.max, apply_absolute_value=True))
                c.step(ts(aback[:, :], amax[:, :], 1e-5, 1.0 / 127.0, ALU.max, ALU.mult))
                c.step(nc.vector.reciprocal(ascale[:, :], aback[:, :]))
                wide = lambda t: t[:, :].unsqueeze(2).to_broadcast([P, GT, C])
                c.step(tt(xn[:, :, :], xn[:, :, :], wide(ascale), ALU.mult))
                c.step(ts(xn[:, :, :], xn[:, :, :], ROUND, ROUND, ALU.add, ALU.subtract))
                tt(xn[:, :, :], xn[:, :, :], wide(aback), ALU.mult).then_inc(xn_ready, 1)

                def first(j):
                    p = j % 2
                    v.wait_ge(h_ps, GT * g + j + 1)
                    tt(h[:, p, :], p_h[p][:, :], conv_b[:, :], ALU.add).then_inc(hb_ready, 1)

                def second(j):
                    p = j % 2
                    v.wait_ge(s_ready, GT * g + j + 1)
                    one = lambda t: t[:, p:p + 1]
                    c.step(nc.vector.tensor_reduce(one(hmax), h[:, p, :], AX.X, ALU.max, apply_absolute_value=True))
                    c.step(ts(one(hback), one(hmax), 1e-5, 1.0 / 127.0, ALU.max, ALU.mult))
                    c.step(nc.vector.reciprocal(one(hscale), one(hback)))
                    c.step(ts(one(hback), one(hback), wmean[:, 1:2], None, ALU.mult))
                    c.step(ts(h[:, p, :], h[:, p, :], one(hscale), ROUND, ALU.mult, ALU.add))
                    ts(hq[:, p, :], h[:, p, :], ROUND, None, ALU.subtract).then_inc(hq_ready, 1)

                def third(j):
                    p = j % 2
                    v.wait_ge(y_ps, GT * g + j + 1)
                    x = X[:, bass.ds(g * GT + j, 1), :].squeeze(1)
                    stt(x, p_y[p][:, 0:C], hback[:, p:p + 1], x, ALU.mult, ALU.add).then_inc(y_done, 1)

                first(0)
                for j in range(GT):
                    if j + 1 < GT:
                        first(j + 1)
                    second(j)
                    if j >= 1:
                        third(j - 1)
                third(GT - 1)
                v.wait_ge(y_done, GT * (g + 1))

        @block.scalar
        def _(act):
            act.wait_ge(set_up, 2)
            with act.Fori(0, NG) as g:
                act.wait_ge(xT_ps, g + 1)
                t3 = lambda t: t.rearrange("c (b s) -> c b s", s=S)
                nc.scalar.activation(xT[:, 1, :], p_x[:, :], ACT.Copy)
                nc.scalar.activation(t3(xT[:, 0, :])[:, :, 1:S], t3(p_x[:, :])[:, :, 0:S - 1], ACT.Copy)
                nc.scalar.activation(t3(xT[:, 2, :])[:, :, 0:S - 1], t3(p_x[:, :])[:, :, 1:S], ACT.Copy).then_inc(xT_ready, 1)

                def turned(j):
                    act.wait_ge(hT_ps, GT * g + j + 1)
                    nc.scalar.activation(hT[:, j % 2, :], p_t[j % 2][:, 0:FF], ACT.Copy).then_inc(hT_ready, 1)

                for j in range(GT):
                    act.wait_ge(hb_ready, GT * g + j + 1)
                    nc.scalar.activation(h[:, j % 2, :], h[:, j % 2, :], ACT.Silu).then_inc(s_ready, 1)
                    if j >= 1:
                        turned(j - 1)
                turned(GT - 1)

        @block.tensor
        def _(pe):
            pe.wait_ge(set_up, 4)
            nc.tensor.matmul(p_w[:, 0:2], ones[:, :], wsum[:, :], start=True, stop=True).then_inc(w_ps, 1)
            pe.wait_ge(set_up, 6 + 7 + 1 + 3)
            with pe.Fori(0, NG) as g:
                pe.wait_ge(xn_ready, g + 1)
                for j in range(GT):
                    ins = nc.tensor.transpose(p_x[:, j * P:(j + 1) * P], xn[:, j, :], kit.ident[:, :])
                ins.then_inc(xT_ps, 1)
                pe.wait_ge(xT_ready, g + 1)

                def up(j):
                    if j >= 2:
                        pe.wait_ge(hb_ready, GT * g + j - 1)
                    for k in range(TAPS):
                        ins = nc.tensor.matmul(p_h[j % 2][:, :], xT[:, k, j * P:(j + 1) * P], w1t[:, k, :], start=(k == 0), stop=(k == TAPS - 1))
                    ins.then_inc(h_ps, 1)

                def turn(j):
                    pe.wait_ge(hq_ready, GT * g + j + 1)
                    if j >= 2:
                        pe.wait_ge(hT_ready, GT * g + j - 1)
                    for k in range(FK):
                        ins = nc.tensor.transpose(p_t[j % 2][:, k * P:(k + 1) * P], hq[:, j % 2, k * P:(k + 1) * P], identb[:, :])
                    ins.then_inc(hT_ps, 1)

                def down(j):
                    pe.wait_ge(hT_ready, GT * g + j + 1)
                    if j >= 2:
                        pe.wait_ge(y_done, GT * g + j - 1)
                    for k in range(FK):
                        ins = nc.tensor.matmul(p_y[j % 2][:, 0:C], hT[:, j % 2, k * P:(k + 1) * P], w2q[:, k, :], start=(k == 0), stop=(k == FK - 1))
                    ins.then_inc(y_ps, 1)

                up(0)
                for j in range(GT):
                    if j + 1 < GT:
                        up(j + 1)
                    turn(j)
                    down(j)


def clear_lists(kit):
    nc = kit.nc
    with ExitStack() as st:
        sb, _, sem = scoped(nc, st, "clear")
        zeros = sb("zeros", [P, SLOTS // P * C // 2])
        zeroed, cleared = sem("zeroed"), sem("cleared")
        block = st.enter_context(nc.Block())

        @block.vector
        def _(v):
            nc.vector.memset(zeros[:, :], 0.0).then_inc(zeroed, 1)

        @block.sync
        def _(sp):
            sp.wait_ge(zeroed, 1)
            half = SLOTS // 2
            for h in range(2):
                sp.dma_start(kit.packed[h * half:(h + 1) * half, :].rearrange("(p n) c -> p (n c)", p=P), zeros[:, :]).then_inc(cleared, 16)
            sp.wait_ge(cleared, 32)


def build(nc, A, out, phases=range(8)):
    with ExitStack() as ctx:
        kit = Kit(nc, A, ctx)
        load_x(kit)
        clear_lists(kit)
        steps = [lambda: mha(kit, "L0_xattn"), lambda: moe(kit, "L0_ffn"), lambda: attention(kit, "L1_xattn"),
                 lambda: moe(kit, "L1_ffn"), lambda: mlstm(kit, "L2_xattn"), lambda: moe(kit, "L2_ffn"), lambda: mha(kit, "L3_xattn"),
                 lambda: quantised_ffn(kit, "L3_ffn")]
        for n in phases:
            steps[n]()
        store_x(kit, out)


def arrays_for(inputs):
    a = {k: np.asarray(v) for k, v in inputs.items()}
    r = {}
    r["x"] = np.ascontiguousarray(a["x"].reshape(TOK, C))
    r["ctx"] = np.ascontiguousarray(a["ctx_1024"].reshape(TOK, C))
    r["ctxT"] = np.ascontiguousarray(a["ctx_1024"].reshape(TOK, C).T)
    r["ident"] = np.eye(P, dtype=np.float32)
    r["head_mask"] = (np.arange(P)[:, None] // 8 % 8 == np.arange(8)[None, :]).astype(np.float32)
    r["half_mask8"] = (np.arange(P)[:, None] // 64 == np.arange(C)[None, :] // 8 % 2).astype(np.float32)
    r["earlier"] = np.triu(np.ones((P, P), np.float32), 1)
    r["ones"] = np.ones((P, P), np.float32)
    r["iota"] = np.arange(128, dtype=np.float32)[None, :]

    def up(w):
        return np.ascontiguousarray(w.transpose(1, 0, 2))

    def down(w):
        return np.ascontiguousarray(w.reshape(w.shape[0], FK, P, C).transpose(2, 0, 1, 3))

    r["L0_ffn_w1"] = up(a["L0_ffn_expert_w1"].transpose(0, 2, 1))
    r["L0_ffn_w2"] = down(a["L0_ffn_expert_w2"].transpose(0, 2, 1))
    r["L0_ffn_b1"], r["L0_ffn_b2"] = a["L0_ffn_expert_b1"], a["L0_ffn_expert_b2"]
    r["L1_ffn_w1"], r["L1_ffn_w2"] = up(a["L1_ffn_w1"]), down(a["L1_ffn_w2"])
    r["L1_ffn_b1"], r["L1_ffn_b2"] = a["L1_ffn_b1"], a["L1_ffn_b2"]
    with_fallback = lambda n: np.concatenate([a[f"L2_ffn_{n}"], a[f"L2_ffn_f{n.lower()}"][None]])
    r["L2_ffn_w1"], r["L2_ffn_w2"] = up(with_fallback("W1")), down(with_fallback("W2"))
    r["L2_ffn_b1"], r["L2_ffn_b2"] = with_fallback("b1"), with_fallback("b2")
    r["L0_ffn_router_w"] = np.ascontiguousarray(a["L0_ffn_router_w"].T)
    r["L1_ffn_router_w"] = np.ascontiguousarray(a["L1_ffn_router_w"].T)
    r["L2_ffn_router_w"] = np.ascontiguousarray(a["L2_ffn_Wr"].T)
    r["L1_ffn_router_b"] = a["L1_ffn_router_b"]
    r["L0_ffn_router_b"] = r["L2_ffn_router_b"] = np.zeros(8, np.float32)
    r["fold"] = np.tile(np.eye(S, dtype=np.float32), (2, 1))
    for n in ("q", "k", "v", "o"):
        for layer in ("L0", "L1", "L3"):
            w = a[f"{layer}_xattn_W{n}"]
            r[f"{layer}_xattn_W{n}"] = w if layer == "L3" else np.ascontiguousarray(w.T)
            r[f"{layer}_xattn_b{n}"] = a[f"{layer}_xattn_b{n}"]
    gate_w = np.zeros((C, 3, 40), np.float32)
    gate_w[:, :, 0:8] = a["L2_xattn_igate_w"].reshape(8, 3, C).transpose(2, 1, 0)
    gate_w[:, :, 32:40] = a["L2_xattn_fgate_w"].reshape(8, 3, C).transpose(2, 1, 0)
    r["L2_xattn_gate_w"] = gate_w
    r["L2_xattn_igate_b"], r["L2_xattn_fgate_b"], r["L2_xattn_out_w"] = (
        a[f"L2_xattn_{n}"] for n in ("igate_b", "fgate_b", "out_w"))
    heads = np.arange(8)
    r["head_mask16"] = (np.arange(P)[:, None] // 16 % 4 == np.arange(4)[None, :]).astype(np.float32)
    r["half_mask16"] = (np.arange(P)[:, None] // 64 == np.arange(C)[None, :] // 16 % 2).astype(np.float32)
    r["head_of_half"] = (heads[:, None] % 4 == np.arange(4)[None, :]).astype(np.float32)
    r["half_of_head"] = (heads[:, None] // 4 == np.arange(2)[None, :]).astype(np.float32)
    r["later"] = np.where(np.arange(S)[:, None] < np.arange(S)[None, :], np.float32(-2.0 ** 100), np.float32(0))
    r["L3_ffn_w1"] = np.ascontiguousarray(a["L3_ffn_w1"].T)
    r["L3_ffn_w2"] = np.ascontiguousarray(a["L3_ffn_w2"].T.reshape(FK, P, C).transpose(1, 0, 2))
    r["L3_ffn_conv_w"] = np.ascontiguousarray(a["L3_ffn_conv_w"][:, 0, :].T)
    r["L3_ffn_conv_b"] = a["L3_ffn_conv_b"]
    return r


def kernel(**inputs):
    import concourse.bacc as bacc
    from concourse.bass_utils import run_bass_kernel_spmd

    nc = bacc.Bacc("TRN2", target_bir_lowering=False, num_devices=1)
    arrays, A = {}, {}
    for name, a in arrays_for(inputs).items():
        arrays[f"in_{name}_dram"] = a
        A[name] = nc.dram_tensor(f"in_{name}_dram", a.shape, mybir.dt.from_np(a.dtype), kind="ExternalInput").ap()
    out = nc.dram_tensor("out_0_dram", (TOK, C), FP32, kind="ExternalOutput").ap()
    build(nc, A, out)
    result = run_bass_kernel_spmd(nc, [arrays], core_ids=[0])
    return result.results[0]["out_0_dram"].reshape(B, S, C)
```

```python
import numpy as np
from contextlib import ExitStack
import concourse.bass as bass
from concourse import mybir

FP32 = mybir.dt.float32
BF16 = mybir.dt.bfloat16
I32 = mybir.dt.int32
U32 = mybir.dt.uint32
ALU = mybir.AluOpType
ACT = mybir.ActivationFunctionType
AX = mybir.AxisListType

B, S, C = 64, 64, 128
TOK = B * S
P = 128
TILES = TOK // P
GT = 4
GROUP = GT * P
NG = TILES // GT
PAIRS = GT
LN_EPS = 1e-5
FF = 512
FK = FF // P
MAX_E = 16
TOP_K = 2
SLOTS = (TOK * TOP_K // P + MAX_E + 2) * P


class Chain:

    def __init__(self, engine, sem, per=0):
        self.engine, self.sem, self.per, self.base, self.n = engine, sem, per, 0, 0

    def start(self, i):
        assert self.n in (0, self.per), (self.n, self.per)
        self.base, self.n = i * self.per, 0

    def done(self, instruction):
        self.n += 1
        instruction.then_inc(self.sem, 1)

    def sync(self):
        self.engine.wait_ge(self.sem, self.base + self.n)

    def step(self, instruction):
        self.done(instruction)
        self.sync()


class Kit:

    def __init__(self, nc, A, ctx):
        self.nc, self.A = nc, A
        sb = lambda name, shape, dt=FP32: ctx.enter_context(nc.sbuf_tensor(name, shape, dt))
        self.X = sb("residual", [P, TILES, C])
        self.XN = sb("normed", [P, TILES, C])
        self.experts_in = ctx.enter_context(nc.semaphore("experts_in"))
        self.experts_loaded = 0
        self.packed = nc.dram_tensor("packed_rows", (SLOTS, C), FP32, kind="Internal").ap()
        self.expert_out = nc.dram_tensor("expert_rows", (SLOTS, C), FP32, kind="Internal").ap()
        self.marks = ctx.enter_context(nc.semaphore("marks"))
        self.minus_half = sb("minus_half", [P, GT])
        self.ident = sb("identity", [P, P])
        self.ones = sb("ones", [P, P])
        self.earlier = sb("earlier", [P, P])
        self.iota = sb("iota", [P, P])

    def passed(self, engine):
        engine.sem_inc(self.marks, 1)


def scoped(nc, stack, tag):
    sb = lambda name, shape, dt=FP32: stack.enter_context(nc.sbuf_tensor(f"{tag}_{name}", shape, dt))
    ps = lambda name, shape, dt=FP32: stack.enter_context(nc.psum_tensor(f"{tag}_{name}", shape, dt))
    taken = []

    def clear():
        if taken:
            nc.clear_and_free_semaphores(taken)
            nc.all_engine_barrier()

    stack.callback(clear)

    def sem(name):
        taken.append(nc.alloc_semaphore(name=f"{tag}_{name}"))
        return taken[-1]
    return sb, ps, sem



LN_STEPS = 2 * GT


def layernorm(nc, v, chain, x_group, xn, stats, mv, var, var_ready, rstd, rstd_ready, turn, passed):
    for j in range(GT):
        chain.done(nc.vector.bn_stats(stats[:, j, :], x_group(j)))
    chain.sync()
    passed(v)
    for j in range(GT):
        chain.done(nc.vector.bn_aggr(mv[:, j, :], stats[:, j, :]))
    chain.sync()
    nc.vector.tensor_scalar(var[:, :], mv[:, :, 1], LN_EPS, None, ALU.add).then_inc(var_ready, 1)
    v.wait_ge(rstd_ready, turn + 1)
    for j in range(GT):
        ins = nc.vector.tensor_scalar(xn[:, j, :], x_group(j), mv[:, j, 0:1], rstd[:, j:j + 1], ALU.subtract, ALU.mult)
    return ins


def inverse_root(nc, pool, var, var_ready, rstd, rstd_ready, minus_half, turn):
    pool.wait_ge(var_ready, turn + 1)
    nc.gpsimd.tensor_tensor(rstd[:, :], var[:, :], minus_half[:, :], ALU.pow).then_inc(rstd_ready, 1)


def load_x(kit):
    nc, A = kit.nc, kit.A
    with ExitStack() as st:
        _, _, sem = scoped(nc, st, "load")
        loaded = sem("loaded")
        block = st.enter_context(nc.Block())

        @block.vector
        def _(v):
            nc.vector.memset(kit.minus_half[:, :], -0.5)

        @block.sync
        def _(sp):
            sp.dma_start(kit.X[:, :, :], A["x"].rearrange("(t p) c -> p t c", p=P)).then_inc(loaded, 16)
            sp.dma_start(kit.ident[:, :], A["ident"]).then_inc(loaded, 16)
            sp.dma_start(kit.earlier[:, :], A["earlier"]).then_inc(loaded, 16)
            sp.dma_start(kit.ones[:, :], A["ones"]).then_inc(loaded, 16)
            sp.dma_start(kit.iota[:, :], A["iota"].to_broadcast([P, P])).then_inc(loaded, 16)
            sp.wait_ge(loaded, 80)


def store_x(kit, out):
    nc = kit.nc
    with ExitStack() as st:
        _, _, sem = scoped(nc, st, "store")
        stored = sem("stored")
        block = st.enter_context(nc.Block())

        @block.sync
        def _(sp):
            sp.dma_start(out.rearrange("(t p) c -> p t c", p=P), kit.X[:, :, :]).then_inc(stored, 16)
            sp.wait_ge(stored, 16)


def pipelined(engine, steps, count, step, loop_from, loop_to):
    assert (loop_to - loop_from) % 2 == 0

    def plain(a, b):
        for n in range(a, b):
            step(n, n % 2, lambda i: 0 <= i < count, lambda i, k: i >= k)
    plain(steps[0], loop_from)
    with engine.Fori(0, (loop_to - loop_from) // 2) as m:
        for u in range(2):
            step(m * 2 + (loop_from + u), (loop_from + u) % 2, lambda i: True, lambda i, k: True)
    plain(loop_to, steps[1])


def mha(kit, tag):
    nc = kit.nc
    H, DH = 16, C // 16
    HH = H // 2
    VW = 2 * 2 * DH + 2
    with ExitStack() as st:
        sb, _, _ = scoped(nc, st, tag)
        QT, KT = sb("QT", [C, TOK]), sb("KT", [C, TOK])
        V2 = sb("V2", [P, TILES, 2 * HH // 2, VW])
        mha_project(kit, tag, QT, KT, V2, DH, VW)
        mha_attend(kit, tag, QT, KT, V2, H, DH, HH, VW)


def mha_project(kit, tag, QT, KT, V2, DH, VW):
    nc, A = kit.nc, kit.A
    NB = GROUP // S
    with ExitStack() as st:
        sb, ps, sem = scoped(nc, st, tag + "_p")
        w = {n: sb(n, [C, C]) for n in ("Wq", "Wk", "Wv")}
        bias = {n: sb(n, [C, 1]) for n in ("bq", "bk")}
        bo = sb("bo", [P, C])
        half_mask = sb("half_mask", [P, C])
        cT = [sb(f"cT{i}", [C, NB, 2, S]) for i in range(2)]
        stats, mv, var, rstd = sb("stats", [P, GT, 6]), sb("mv", [P, GT, 2]), sb("var", [P, GT]), sb("rstd", [P, GT])
        xn, xnT = [sb(f"xn{i}", [P, GT, C]) for i in range(2)], [sb(f"xnT{i}", [C, GROUP]) for i in range(2)]
        p_x, p_k, p_q = ps("p_x", [P, 512]), ps("p_k", [P, 512]), ps("p_q", [P, 512])
        p_v = [ps(f"p_v{i}", [P, 512]) for i in range(2)]
        wkv_in, rest_in = sem("wkv_in"), sem("rest_in")
        ctx_in = [sem(f"ctx_in{i}") for i in range(2)]
        var_ready, rstd_ready, xn_ready, xT_ps, xnT_ready, q_ps, k_ps, v_ps, qT_ready, kT_ready, v_ready, dve, ones_set, bo_added = (
            sem(n) for n in "var_ready rstd_ready xn_ready xT_ps xnT_ready q_ps k_ps v_ps qT_ready kT_ready v_ready dve ones_set bo_added".split())
        X = kit.X
        block = st.enter_context(nc.Block())
        span = (-1, NG + 1)

        def run(engine, step):
            pipelined(engine, span, NG, step, 2, NG - 2)

        @block.sync
        def _(sp):
            for n in ("Wk", "Wv"):
                sp.dma_start(w[n][:, :], A[f"{tag}_{n}"]).then_inc(wkv_in, 16)

            def step(n, s, live, after):
                if live(n + 1):
                    if after(n + 1, 2):
                        sp.wait_ge(v_ps, 2 * n)
                    for twice in range(2):
                        sp.dma_start(cT[1 - s][:, :, twice, :], A["ctxT"][:, bass.ds((n + 1) * GROUP, GROUP)].rearrange(
                            "c (b s) -> c b s", s=S)).then_inc(ctx_in[1 - s], 16)
            run(sp, step)

        @block.gpsimd
        def _(pool):
            pool.wait_ge(rest_in, 16 * 5)

            def step(n, s, live, after):
                if live(n):
                    xg = X[:, bass.ds(n * GT, GT), :]
                    inverse_root(nc, pool, var, var_ready, rstd, rstd_ready, kit.minus_half, n)
                    pool.wait_ge(xn_ready, n + 1)
                    nc.gpsimd.tensor_tensor(xg, xg, bo[:, :].unsqueeze(1).to_broadcast([P, GT, C]), ALU.add).then_inc(bo_added, 1)
            run(pool, step)

        @block.scalar
        def _(act):
            act.dma_start(half_mask[:, :], A["half_mask8"]).then_inc(rest_in, 16)
            for n in bias:
                act.dma_start(bias[n][:, :], A[f"{tag}_{n}"].rearrange("(c a) -> c a", a=1)).then_inc(rest_in, 16)
            act.dma_start(w["Wq"][:, :], A[f"{tag}_Wq"]).then_inc(rest_in, 16)
            act.dma_start(bo[:, :], A[f"{tag}_bo"].rearrange("(a c) -> a c", a=1).to_broadcast([P, C])).then_inc(rest_in, 16)
            act.wait_ge(rest_in, 16 * 5)

            def step(n, s, live, after):
                if live(n + 1):
                    act.wait_ge(k_ps, n + 2)
                    nc.scalar.activation(KT[:, bass.ds((n + 1) * GROUP, GROUP)], p_k[:, :], ACT.Identity, bias=bias["bk"][:, :]).then_inc(kT_ready, 1)
                if live(n - 1):
                    act.wait_ge(q_ps, n)
                    nc.scalar.activation(QT[:, bass.ds((n - 1) * GROUP, GROUP)], p_q[:, :], ACT.Identity, bias=bias["bq"][:, :]).then_inc(qT_ready, 1)
                if live(n):
                    act.wait_ge(xT_ps, n + 1)
                    nc.scalar.activation(xnT[s][:, :], p_x[:, :], ACT.Copy).then_inc(xnT_ready, 1)
            run(act, step)

        @block.vector
        def _(v):
            nc.vector.memset(V2[:, :, :, 4 * DH:VW], 0.0).then_inc(ones_set, 1)
            v.wait_ge(ones_set, 1)
            nc.vector.memset(V2[0:S, :, :, 4 * DH:4 * DH + 1], 1.0).then_inc(ones_set, 1)
            nc.vector.memset(V2[S:P, :, :, 4 * DH + 1:VW], 1.0).then_inc(ones_set, 1)
            v.wait_ge(rest_in, 16 * 5)
            hm = half_mask[:, :].rearrange("p (f i c) -> p i f c", f=2, c=2 * DH)

            def values(g):
                for half in range(2):
                    v.wait_ge(v_ps, 2 * g + half + 1)
                    for b in range(4):
                        vin = p_v[half][:, C * b:C * b + C].rearrange("p (f i c) -> p i f c", f=2, c=2 * DH)
                        vout = V2[:, bass.ds(g * GT + 2 * half + b // 2, 1), 4 * (b % 2):4 * (b % 2) + 4, 0:4 * DH].squeeze(1)
                        ins = nc.vector.tensor_tensor(vout.rearrange("p i (f c) -> p i f c", f=2), vin, hm, ALU.mult)
                    ins.then_inc(v_ready, 1)

            def step(n, s, live, after):
                x = lambda j: X[:, bass.ds(n * GT + j, 1), :].squeeze(1)
                if live(n):
                    for j in range(GT):
                        ins = nc.vector.bn_stats(stats[:, j, :], x(j))
                    ins.then_inc(dve, 1)
                    v.wait_ge(dve, 2 * n + 1)
                    kit.passed(v)
                    for j in range(GT):
                        ins = nc.vector.bn_aggr(mv[:, j, :], stats[:, j, :])
                    ins.then_inc(dve, 1)
                    v.wait_ge(dve, 2 * n + 2)
                    nc.vector.tensor_scalar(var[:, :], mv[:, :, 1], LN_EPS, None, ALU.add).then_inc(var_ready, 1)
                if live(n + 1):
                    values(n + 1)
                if live(n):
                    v.wait_ge(rstd_ready, n + 1)
                    if after(n, 2):
                        v.wait_ge(xT_ps, n - 1)
                    for j in range(GT):
                        ins = nc.vector.tensor_scalar(xn[s][:, j, :], x(j), mv[:, j, 0:1], rstd[:, j:j + 1], ALU.subtract, ALU.mult)
                    ins.then_inc(xn_ready, 1)
            run(v, step)

        @block.tensor
        def _(pe):
            pe.wait_ge(wkv_in, 32)

            def step(n, s, live, after):
                if live(n + 1):
                    pe.wait_ge(ctx_in[1 - s], 16 * (n + 1 - (1 - s)) + 32)
                    if after(n + 1, 1):
                        pe.wait_ge(kT_ready, n + 1)
                    nc.tensor.matmul(p_k[:, :], w["Wk"][:, :], cT[1 - s][:, :, 0, :], start=True, stop=True).then_inc(k_ps, 1)
                    for half in range(2):
                        if after(n + 1, 1):
                            pe.wait_ge(v_ready, 2 * n + half + 1)
                        for b in range(4):
                            ins = nc.tensor.matmul(p_v[half][:, b * C:(b + 1) * C], cT[1 - s][:, half * 4 + b], w["Wv"][:, :],
                                                   start=True, stop=True)
                        ins.then_inc(v_ps, 1)
                if live(n - 1):
                    if not after(n - 1, 1):
                        pe.wait_ge(rest_in, 16 * 5)
                    pe.wait_ge(xnT_ready, n)
                    if after(n - 1, 1):
                        pe.wait_ge(qT_ready, n - 1)
                    nc.tensor.matmul(p_q[:, :], w["Wq"][:, :], xnT[1 - s][:, :], start=True, stop=True).then_inc(q_ps, 1)
                if live(n):
                    pe.wait_ge(xn_ready, n + 1)
                    if after(n, 1):
                        pe.wait_ge(xnT_ready, n)
                    for j in range(GT):
                        ins = nc.tensor.transpose(p_x[:, j * P:(j + 1) * P], xn[s][:, j, :], kit.ident[:, :])
                    ins.then_inc(xT_ps, 1)
            run(pe, step)


def mha_attend(kit, tag, QT, KT, V2, H, DH, HH, VW):
    nc, A = kit.nc, kit.A
    SCALE = DH ** -0.5
    with ExitStack() as st:
        sb, ps, sem = scoped(nc, st, tag + "_a")
        Wo, bv = sb("Wo", [C, C]), sb("bv", [C, 1])
        head_mask, fold = sb("head_mask", [P, HH]), sb("fold", [P, S])
        Qz = [sb(f"Qz{i}", [C, 2, 2, S]) for i in range(2)]
        Km = [sb(f"Km{i}", [C, 2, HH, S]) for i in range(2)]
        Pm = [sb(f"Pm{i}", [P, H * S]) for i in range(2)]
        mx, rs = sb("mx", [P, 2, H]), sb("rs", [P, 2, H])
        PT = sb("PT", [P, H * S])
        O = [sb(f"O{i}", [P, 2, 2, C // 2]) for i in range(2)]
        OT = sb("OT", [C, P])
        p_s = [ps(f"p_s{i}", [P, H * S]) for i in range(2)]
        p_t = [ps(f"p_t{i}", [P, H * S // 2]) for i in range(2)]
        p_o, p_y = ps("p_o", [P, 512]), ps("p_y", [P, 512])
        consts_in, zeros_set = sem("consts_in"), sem("zeros_set")
        qz_ready, km_ready, s_ps, mx_ready, d_ready, p_ready, t_ps, pT_ready, o_ps, rs_ready, o_ready, oT_ps, oT_ready, y_ps, y_added = (
            sem(n) for n in "qz_ready km_ready s_ps mx_ready d_ready p_ready t_ps pT_ready o_ps rs_ready o_ready oT_ps oT_ready y_ps y_added".split())
        X = kit.X
        block = st.enter_context(nc.Block())
        pair = lambda j: bass.ds(j * P, P)

        def run(engine, step):
            pipelined(engine, (-3, TILES + 3), TILES, step, 6, TILES - 4)

        @block.sync
        def _(sp):
            for dst, src in ((head_mask[:, :], A["head_mask"]), (fold[:, :], A["fold"]), (Wo[:, :], A[f"{tag}_Wo"]),
                             (bv[:, :], A[f"{tag}_bv"].rearrange("(c a) -> c a", a=1))):
                sp.dma_start(dst, src).then_inc(consts_in, 16)
            sp.wait_ge(consts_in, 64)

        @block.gpsimd
        def _(pool):
            pool.wait_ge(consts_in, 64)

            def keys(j, s, after):
                if after(j, 2):
                    pool.wait_ge(s_ps, j - 1)
                kt = KT[:, pair(j)].rearrange("c (b s) -> c b s", s=S)
                for b in range(2):
                    ins = nc.gpsimd.tensor_tensor(Km[s][:, b], kt[:, b].unsqueeze(1).to_broadcast([P, HH, S]),
                                                  head_mask[:, :].unsqueeze(2).to_broadcast([P, HH, S]), ALU.mult)
                ins.then_inc(km_ready, 1)

            def step(n, s, live, after):
                if live(n + 3):
                    keys(n + 3, 1 - s, after)
            run(pool, step)

        @block.scalar
        def _(act):
            act.wait_ge(zeros_set, 4)
            act.wait_ge(consts_in, 64)

            def queries(j, s, after):
                if after(j, 2):
                    act.wait_ge(s_ps, j - 1)
                for h in range(2):
                    rows = slice(64 * h, 64 * h + 64)
                    ins = nc.scalar.activation(Qz[s][rows, :, h, :], QT[rows, pair(j)].rearrange("c (b s) -> c b s", s=S), ACT.Copy)
                ins.then_inc(qz_ready, 1)

            def step(n, s, live, after):
                if live(n + 3):
                    queries(n + 3, 1 - s, after)
                if live(n + 1):
                    act.wait_ge(d_ready, n + 2)
                    nc.scalar.activation(Pm[1 - s][:, :], Pm[1 - s][:, :], ACT.Exp, scale=SCALE).then_inc(p_ready, 1)
                if live(n):
                    if after(n, 1):
                        act.wait_ge(o_ps, n)
                    for h in range(2):
                        act.wait_ge(t_ps, 2 * n + h + 1)
                        nc.scalar.activation(PT[:, h * 512:(h + 1) * 512], p_t[h][:, :], ACT.Copy).then_inc(pT_ready, 1)
                if live(n - 2):
                    act.wait_ge(oT_ps, n - 1)
                    nc.scalar.activation(OT[:, :], p_y[:, 0:P], ACT.Identity, bias=bv[:, :]).then_inc(oT_ready, 1)
            run(act, step)

        @block.vector
        def _(v):
            for i in range(2):
                nc.vector.memset(Qz[i][:, :, :, :], 0.0).then_inc(zeros_set, 1)
                nc.vector.memset(O[i][:, :, :, :], 0.0).then_inc(zeros_set, 1)
            v.wait_ge(zeros_set, 4)

            def subtract_max(j, s, after):
                v.wait_ge(s_ps, j + 1)
                s3 = p_s[s][:, :].rearrange("p (h k) -> p h k", k=S)
                nc.vector.tensor_reduce(mx[:, s, :], s3, AX.X, ALU.max).then_inc(mx_ready, 1)
                v.wait_ge(mx_ready, j + 1)
                if after(j, 2):
                    v.wait_ge(t_ps, 2 * j - 2)
                nc.vector.tensor_tensor(Pm[s][:, :].rearrange("p (h k) -> p h k", k=S), s3,
                                        mx[:, s, :].unsqueeze(2).to_broadcast([P, H, S]), ALU.subtract).then_inc(d_ready, 1)

            def normalise(j, s, after):
                v.wait_ge(o_ps, j + 1)
                po = p_o[:, 0:H // 2 * VW].rearrange("p (h c) -> p h c", c=VW)
                r = rs[:, s, :]
                nc.vector.reciprocal(r.rearrange("p (h c) -> p h c", c=2), po[:, :, 4 * DH:VW]).then_inc(rs_ready, 1)
                v.wait_ge(rs_ready, j + 1)
                if after(j, 2):
                    v.wait_ge(oT_ps, j - 1)
                for f in range(2):
                    q = slice(f * S, (f + 1) * S)
                    ins = nc.vector.tensor_tensor(
                        O[s][q, :, f, :].rearrange("p b (i a c) -> p b i a c", a=2, c=DH),
                        po[q, :, f * 2 * DH:(f + 1) * 2 * DH].rearrange("p (b i) (a c) -> p b i a c", b=2, c=DH),
                        r[q].rearrange("p (b i a) -> p b i a", b=2, a=2).unsqueeze(4).to_broadcast([S, 2, HH // 2, 2, DH]),
                        ALU.mult)
                ins.then_inc(o_ready, 1)

            def step(n, s, live, after):
                if live(n + 1):
                    subtract_max(n + 1, 1 - s, after)
                if live(n - 3):
                    v.wait_ge(y_ps, n - 2)
                    x = X[:, bass.ds(n - 3, 1), :].squeeze(1)
                    nc.vector.tensor_tensor(x, x, p_y[:, P:P + C], ALU.add).then_inc(y_added, 1)
                if live(n - 1):
                    normalise(n - 1, 1 - s, after)
            run(v, step)

        @block.tensor
        def _(pe):
            pe.wait_ge(consts_in, 64)
            pe.wait_ge(zeros_set, 4)

            def step(n, s, live, after):
                if live(n + 1):
                    j, t = n + 1, 1 - s
                    pe.wait_ge(qz_ready, j + 1)
                    pe.wait_ge(km_ready, j + 1)
                    if after(j, 2):
                        pe.wait_ge(d_ready, j - 1)
                    for b in range(2):
                        ins = nc.tensor.matmul(p_s[t][:, b * 512:(b + 1) * 512], Qz[t][:, b], Km[t][:, b], start=True, stop=True)
                    ins.then_inc(s_ps, 1)
                if live(n - 3):
                    pe.wait_ge(oT_ready, n - 2)
                    nc.tensor.matmul(p_y[:, P:P + C], OT[:, :], Wo[:, :], start=True, stop=True).then_inc(y_ps, 1)
                if live(n - 1):
                    j = n - 1
                    if after(j, 1):
                        pe.wait_ge(o_ready, j)
                    for h in range(2):
                        pe.wait_ge(pT_ready, 2 * j + h + 1)
                        for i in range(4 * h, 4 * h + 4):
                            ins = nc.tensor.matmul(p_o[:, i * VW:(i + 1) * VW], PT[:, i * P:(i + 1) * P],
                                                   V2[:, bass.ds(j, 1), i, :].squeeze(1), start=True, stop=True)
                    ins.then_inc(o_ps, 1)
                if live(n):
                    pe.wait_ge(p_ready, n + 1)
                    for h in range(2):
                        if after(n, 1):
                            pe.wait_ge(pT_ready, 2 * n - 1 + h)
                        for i in range(4):
                            ins = nc.tensor.transpose(p_t[h][:, i * P:(i + 1) * P], Pm[s][:, (4 * h + i) * P:(4 * h + i + 1) * P],
                                                      kit.ident[:, :])
                        ins.then_inc(t_ps, 1)
                if live(n - 2):
                    j = n - 2
                    pe.wait_ge(o_ready, j + 1)
                    if after(j, 1):
                        pe.wait_ge(y_added, j)
                    for b in range(2):
                        ins = nc.tensor.matmul(p_y[:, b * S:(b + 1) * S], O[s][:, b, :, :], fold[:, :], start=True, stop=True)
                    ins.then_inc(oT_ps, 1)
            run(pe, step)


class Moe:

    def __init__(self, routed, cap, fallback, gates):
        self.routed, self.cap, self.fallback, self.gates = routed, cap, fallback, gates
        self.experts = routed + fallback
        most = TOK * TOP_K // P + self.experts - 1
        self.tiles = most + most % 2


MOES = {
    "L0_ffn": Moe(8, None, 0, "probs_sum"),
    "L1_ffn": Moe(16, -(-5 * TOK * TOP_K // (4 * 16)), 0, "kept_softmax"),
    "L2_ffn": Moe(8, int(1.25 * (TOK * TOP_K / 8)), 1, "probs_clip"),
}


def load_experts(kit, sp, tag):
    A, E = kit.A, MOES[tag].experts
    sp.dma_start(kit.W1[:, 0:E, :], A[f"{tag}_w1"]).then_inc(kit.experts_in, 16)
    sp.dma_start(kit.W2[:, 0:E, :, :], A[f"{tag}_w2"]).then_inc(kit.experts_in, 16)
    sp.dma_start(kit.B1[:, 0:E, :], A[f"{tag}_b1"]).then_inc(kit.experts_in, 16)
    sp.dma_start(kit.B2[:, 0:E, :], A[f"{tag}_b2"].unsqueeze(0).to_broadcast([P, E, C])).then_inc(kit.experts_in, 16)
    kit.experts_loaded += 64


def moe(kit, tag):
    nc = kit.nc
    with ExitStack() as st:
        sb, _, _ = scoped(nc, st, tag)
        E = MOES[tag].experts
        kit.W1, kit.W2 = sb("w1", [C, E, FF]), sb("w2", [P, E, FK, C])
        kit.B1, kit.B2 = sb("b1", [P, E, FK]), sb("b2", [P, E, C])
        r = Route()
        r.values = sb("values", [P, TILES, TOP_K])
        r.chosen = sb("chosen", [P, TILES, TOP_K])
        r.logits = sb("logits", [P, TILES, MOES[tag].routed])
        r.gate = sb("gate", [P, TOP_K, TILES])
        r.slot_out = sb("slot_out", [P, TILES, TOP_K], I32)
        r.slot_back = sb("slot_back", [P, TILES, TOP_K], I32)
        r.tile_expert = sb("tile_expert", [1, MOES[tag].tiles], I32)
        router(kit, tag, r)
        plan(kit, tag, r)
        dispatch(kit, tag, r)
        run_experts(kit, tag, r)
        combine(kit, tag, r)


class Route:
    pass


def router(kit, tag, r):
    nc, A, m = kit.nc, kit.A, MOES[tag]
    E = m.routed
    with ExitStack() as st:
        sb, ps, sem = scoped(nc, st, tag + "_r")
        wr = sb("wr", [C, E])
        br = sb("br", [P, E])
        stats, mv, var, rstd = sb("stats", [P, GT, 6]), sb("mv", [P, GT, 2]), sb("var", [P, GT]), sb("rstd", [P, GT])
        xn, xnT = [sb(f"xn{i}", [P, GT, C]) for i in range(2)], [sb(f"xnT{i}", [C, GROUP]) for i in range(2)]
        lg = sb("lg", [P, GT, E])
        top, top_i = sb("top", [P, GT, 8]), sb("top_i", [P, GT, 8], U32)
        p_x, p_l = [ps(f"p_x{i}", [P, GROUP]) for i in range(2)], [ps(f"p_l{i}", [P, 512]) for i in range(2)]
        weights, var_ready, rstd_ready, xn_ready = sem("weights"), sem("var_ready"), sem("rstd_ready"), sem("xn_ready")
        xT_ps, xnT_ready, logits_ps, lg_read, topped, kept, dve = (
            sem(n) for n in ("xT_ps", "xnT_ready", "logits_ps", "lg_read", "topped", "kept", "dve"))
        N_WEIGHTS = 32
        X = kit.X
        block = st.enter_context(nc.Block())

        def run(engine, step):
            pipelined(engine, (0, NG + 1), NG, step, 2, NG)

        @block.sync
        def _(sp):
            sp.dma_start(wr[:, :], A[f"{tag}_router_w"]).then_inc(weights, 16)
            sp.dma_start(br[:, :], A[f"{tag}_router_b"].rearrange("(a c) -> a c", a=1).to_broadcast([P, E])).then_inc(weights, 16)
            load_experts(kit, sp, tag)

        @block.gpsimd
        def _(pool):
            def step(n, s, live, after):
                if live(n):
                    inverse_root(nc, pool, var, var_ready, rstd, rstd_ready, kit.minus_half, n)
            run(pool, step)

        @block.tensor
        def _(pe):
            pe.wait_ge(weights, N_WEIGHTS)

            def step(n, s, live, after):
                if live(n - 1):
                    t = 1 - s
                    pe.wait_ge(xnT_ready, n)
                    if after(n - 1, 2):
                        pe.wait_ge(lg_read, n - 2)
                    for j in range(GT):
                        ins = nc.tensor.matmul(p_l[t][:, j * E:(j + 1) * E], xnT[t][:, j * P:(j + 1) * P], wr[:, :], start=True, stop=True)
                    ins.then_inc(logits_ps, 1)
                if live(n):
                    pe.wait_ge(xn_ready, n + 1)
                    if after(n, 2):
                        pe.wait_ge(xnT_ready, n - 1)
                    for j in range(GT):
                        ins = nc.tensor.transpose(p_x[s][:, j * P:(j + 1) * P], xn[s][:, j, :], kit.ident[:, :])
                    ins.then_inc(xT_ps, 1)
            run(pe, step)

        @block.scalar
        def _(act):
            def step(n, s, live, after):
                if live(n):
                    act.wait_ge(xT_ps, n + 1)
                    if after(n, 2):
                        act.wait_ge(logits_ps, n - 1)
                    nc.scalar.activation(xnT[s][:, :], p_x[s][:, :], ACT.Copy).then_inc(xnT_ready, 1)
                    act.wait_ge(xn_ready, n + 1)
                    nc.scalar.activation(kit.XN[:, bass.ds(n * GT, GT), :], xn[s][:, :, :], ACT.Copy).then_inc(kept, 1)
            run(act, step)

        @block.vector
        def _(v):
            v.wait_ge(weights, N_WEIGHTS)
            LN = 2

            def step(n, s, live, after):
                x = lambda j: X[:, bass.ds(n * GT + j, 1), :].squeeze(1)
                if live(n):
                    for j in range(GT):
                        ins = nc.vector.bn_stats(stats[:, j, :], x(j))
                    ins.then_inc(dve, 1)
                    v.wait_ge(dve, LN * n + 1)
                    kit.passed(v)
                    for j in range(GT):
                        ins = nc.vector.bn_aggr(mv[:, j, :], stats[:, j, :])
                    ins.then_inc(dve, 1)
                    v.wait_ge(dve, LN * n + 2)
                    nc.vector.tensor_scalar(var[:, :], mv[:, :, 1], LN_EPS, None, ALU.add).then_inc(var_ready, 1)
                if live(n - 1):
                    v.wait_ge(logits_ps, n)
                    if after(n - 1, 1):
                        v.wait_ge(topped, 3 * (n - 1))
                    nc.vector.tensor_tensor(lg[:, :, :], p_l[1 - s][:, 0:GT * E].rearrange("p (t e) -> p t e", e=E),
                                            br[:, :].unsqueeze(1).to_broadcast([P, GT, E]), ALU.add).then_inc(lg_read, 1)
                if live(n):
                    v.wait_ge(rstd_ready, n + 1)
                    if after(n, 2):
                        v.wait_ge(xT_ps, n - 1)
                        v.wait_ge(kept, n - 1)
                    for j in range(GT):
                        ins = nc.vector.tensor_scalar(xn[s][:, j, :], x(j), mv[:, j, 0:1], rstd[:, j:j + 1], ALU.subtract, ALU.mult)
                    ins.then_inc(xn_ready, 1)
                if live(n - 1):
                    m = n - 1
                    v.wait_ge(lg_read, m + 1)
                    kit.passed(v)
                    for j in range(GT):
                        ins = nc.vector.max(top[:, j, :], lg[:, j, :])
                    ins.then_inc(topped, 1)
                    v.wait_ge(topped, 3 * m + 1)
                    kit.passed(v)
                    for j in range(GT):
                        ins = nc.vector.max_index(top_i[:, j, :], top[:, j, :], lg[:, j, :])
                    ins.then_inc(topped, 1)
                    v.wait_ge(topped, 3 * m + 2)
                    tiles = bass.ds(m * GT, GT)
                    nc.vector.tensor_copy(r.values[:, tiles, :], top[:, :, 0:TOP_K])
                    nc.vector.tensor_copy(r.logits[:, tiles, :], lg[:, :, :])
                    nc.vector.tensor_copy(r.chosen[:, tiles, :], top_i[:, :, 0:TOP_K]).then_inc(topped, 1)
            run(v, step)


def plan(kit, tag, r):
    nc, A, m = kit.nc, kit.A, MOES[tag]
    E, R, T = m.experts, m.routed, TILES
    with ExitStack() as st:
        sb, ps, sem = scoped(nc, st, tag + "_p")
        earlier, ones, iota = kit.earlier, kit.ones, kit.iota
        restart = sb("restart", [P, E, T])
        M = [sb("M0", [P, E, T]), sb("M1", [P, E, T])]
        both, pos, tot, inc, row = (sb(n, [P, E, T]) for n in ("both", "pos", "tot", "inc", "row"))
        ex = sb("ex", [P, T, R])
        es, pr, den, kp, sl = sb("es", [P, T]), sb("pr", [P, 2, T]), sb("den", [P, T]), sb("kp", [P, 2, T]), sb("sl", [P, 2, T])
        open_, over = sb("open", [P, T]), sb("over", [P, T])
        cnt, cnt_i, nt, cum, base = sb("cnt", [P, E]), sb("cnt_i", [P, E], I32), sb("nt", [P, E]), sb("cum", [P, E]), sb("base", [P, E])
        ones_e = sb("ones_e", [P, E])
        le = sb("le", [1, m.tiles, E])
        te = sb("te", [1, m.tiles])
        p_in, p_tot = ps("p_in", [P, 512]), ps("p_tot", [P, 512])
        dve, counted, exps, asked = sem("dve"), sem("counted"), sem("exps"), sem("asked")
        block = st.enter_context(nc.Block())
        ROUNDS = 1 if not m.fallback else E

        @block.scalar
        def _(act):
            act.wait_ge(exps, 1)
            nc.scalar.activation(ex[:, :, :], ex[:, :, :], ACT.Exp)
            nc.scalar.activation(pr[:, :, :], pr[:, :, :], ACT.Exp).then_inc(exps, 1)

        @block.tensor
        def _(pe):
            for n in range(ROUNDS):
                pe.wait_ge(asked, n + 1)
                src = both[:, n, :] if m.fallback else both[:, :, :]
                width = T if m.fallback else E * T
                nc.tensor.matmul(p_in[:, 0:width], earlier[:, :], src, start=True, stop=True)
                nc.tensor.matmul(p_tot[:, 0:width], ones[:, :], src, start=True, stop=True).then_inc(counted, 1)

        @block.vector
        def _(v):
            c = Chain(v, dve)
            tt, ts = nc.vector.tensor_tensor, nc.vector.tensor_scalar
            c.done(nc.vector.memset(restart[:, :, :], 1.0))
            c.done(nc.vector.memset(ones_e[:, :], 1.0))
            c.done(nc.vector.memset(open_[:, :], 1.0))
            c.done(nc.vector.memset(M[0][:, :, :], 0.0))
            c.done(nc.vector.memset(M[1][:, :, :], 0.0))
            top = r.values[:, :, 0]
            c.done(tt(ex[:, :, :], r.logits[:, :, :], top.unsqueeze(2).to_broadcast([P, T, R]), ALU.subtract))
            for k in range(TOP_K):
                last = tt(pr[:, k, :], r.values[:, :, k], top, ALU.subtract)
                if k == 0:
                    c.done(last)
                else:
                    last.then_inc(exps, 1)
            c.sync()
            c.done(nc.vector.memset(restart[:, :, 0], 0.0))
            for k in range(TOP_K):
                c.done(tt(M[k][:, 0:R, :], r.chosen[:, :, k].unsqueeze(1).to_broadcast([P, R, T]),
                          iota[:, 0:R].unsqueeze(2).to_broadcast([P, R, T]), ALU.is_equal))
            c.sync()
            if not m.fallback:
                tt(both[:, :, :], M[0][:, :, :], M[1][:, :, :], ALU.add).then_inc(asked, 1)
                v.wait_ge(counted, 1)
                c.step(nc.vector.tensor_copy(tot[:, :, :], p_tot[:, 0:E * T].rearrange("p (e t) -> p e t", t=T)))
                c.step(nc.vector.tensor_tensor_scan(inc[:, :, :].rearrange("p e t -> p (e t)"), restart[:, :, :].rearrange("p e t -> p (e t)"),
                                                    tot[:, :, :].rearrange("p e t -> p (e t)"), 0.0, ALU.mult, ALU.add))
                c.step(tt(pos[:, :, :], inc[:, :, :], tot[:, :, :], ALU.subtract))
                c.step(tt(pos[:, :, :], pos[:, :, :], p_in[:, 0:E * T].rearrange("p (e t) -> p e t", t=T), ALU.add))
                if m.cap:
                    c.step(ts(row[:, :, :], pos[:, :, :], float(m.cap), None, ALU.is_lt))
                    for k in range(TOP_K):
                        c.done(tt(M[k][:, :, :], M[k][:, :, :], row[:, :, :], ALU.mult))
                c.step(ts(cnt[:, :], inc[:, :, T - 1], float(m.cap or TOK * TOP_K), None, ALU.min))
            else:
                c.step(tt(row[:, 0:R, :], M[0][:, 0:R, :], M[1][:, 0:R, :], ALU.add))
                for e in range(E):
                    if e < R:
                        tt(both[:, e, :], row[:, e, :], open_[:, :], ALU.mult).then_inc(asked, 1)
                    else:
                        ts(both[:, e, :], open_[:, :], -1.0, 1.0, ALU.mult, ALU.add).then_inc(asked, 1)
                    v.wait_ge(counted, e + 1)
                    c.step(nc.vector.tensor_copy(tot[:, e, :], p_tot[:, 0:T]))
                    c.step(nc.vector.tensor_tensor_scan(inc[:, e, :], restart[:, e, :], tot[:, e, :], 0.0, ALU.mult, ALU.add))
                    c.step(tt(pos[:, e, :], inc[:, e, :], tot[:, e, :], ALU.subtract))
                    c.step(tt(pos[:, e, :], pos[:, e, :], p_in[:, 0:T], ALU.add))
                    if e < R:
                        c.step(nc.vector.scalar_tensor_tensor(over[:, :], pos[:, e, :], float(m.cap), both[:, e, :], ALU.is_ge, ALU.mult))
                        c.step(tt(open_[:, :], open_[:, :], over[:, :], ALU.subtract))
                for k in range(TOP_K):
                    c.done(tt(M[k][:, 0:R, :], M[k][:, 0:R, :], open_[:, :].unsqueeze(1).to_broadcast([P, R, T]), ALU.mult))
                c.done(nc.vector.tensor_copy(M[0][:, R, :], both[:, R, :]))
                c.done(ts(cnt[:, 0:R], inc[:, 0:R, T - 1], float(m.cap), None, ALU.min))
                c.done(nc.vector.tensor_copy(cnt[:, R:E], inc[:, R:E, T - 1]))
                c.sync()
            c.step(ts(cnt_i[:, :], cnt[:, :], float(P - 1), None, ALU.add))
            c.step(ts(cnt_i[:, :], cnt_i[:, :], P.bit_length() - 1, None, ALU.logical_shift_right))
            c.step(nc.vector.tensor_copy(nt[:, :], cnt_i[:, :]))
            c.step(nc.vector.tensor_tensor_scan(cum[:, :], ones_e[:, :], nt[:, :], 0.0, ALU.mult, ALU.add))
            c.step(tt(base[:, :], cum[:, :], nt[:, :], ALU.subtract))
            c.step(ts(base[:, :], base[:, :], float(P), None, ALU.mult))
            c.step(tt(row[:, :, :], pos[:, :, :], base[:, :].unsqueeze(2).to_broadcast([P, E, T]), ALU.add))
            n = m.tiles
            c.step(tt(le[:, :, :], cum[0:1, :].unsqueeze(1).to_broadcast([1, n, E]), iota[0:1, 0:n].unsqueeze(2).to_broadcast([1, n, E]), ALU.is_le))
            c.step(nc.vector.tensor_reduce(te[:, :], le[:, :, :], AX.X, ALU.add))
            c.done(ts(r.tile_expert[:, :], te[:, :], float(E - 1), None, ALU.min))
            for k in range(TOP_K):
                c.step(nc.vector.tensor_reduce(kp[:, k, :], M[k][:, :, :].rearrange("p e t -> p t e"), AX.X, ALU.add))
                c.step(tt(pos[:, :, :], M[k][:, :, :], row[:, :, :], ALU.mult))
                c.step(nc.vector.tensor_reduce(sl[:, k, :], pos[:, :, :].rearrange("p e t -> p t e"), AX.X, ALU.add))
                c.step(nc.vector.tensor_copy(r.slot_back[:, :, k], sl[:, k, :]))
                c.step(ts(over[:, :], kp[:, k, :], float(-NOWHERE), float(NOWHERE), ALU.mult, ALU.add))
                c.step(tt(r.slot_out[:, :, k], sl[:, k, :], over[:, :], ALU.add))
            v.wait_ge(exps, 2)
            if m.gates == "kept_softmax":
                c.step(tt(den[:, :], pr[:, 0, :], pr[:, 1, :], ALU.add))
                c.step(nc.vector.reciprocal(den[:, :], den[:, :]))
                for k in range(TOP_K):
                    c.step(tt(pr[:, k, :], pr[:, k, :], den[:, :], ALU.mult))
                    c.step(tt(pr[:, k, :], pr[:, k, :], kp[:, k, :], ALU.mult))
                c.step(tt(den[:, :], pr[:, 0, :], pr[:, 1, :], ALU.add))
                c.step(ts(den[:, :], den[:, :], 1e-9, None, ALU.add))
            else:
                c.step(nc.vector.tensor_reduce(es[:, :], ex[:, :, :], AX.X, ALU.add))
                c.step(nc.vector.reciprocal(es[:, :], es[:, :]))
                for k in range(TOP_K):
                    c.step(tt(pr[:, k, :], pr[:, k, :], es[:, :], ALU.mult))
                c.step(tt(den[:, :], pr[:, 0, :], pr[:, 1, :], ALU.add))
                c.step(ts(den[:, :], den[:, :], 1e-9, None, ALU.max if m.gates == "probs_clip" else ALU.add))
            c.step(nc.vector.reciprocal(den[:, :], den[:, :]))
            for k in range(TOP_K):
                c.done(tt(r.gate[:, k, :], pr[:, k, :], den[:, :], ALU.mult))
            c.sync()
            if m.fallback:
                for k in range(TOP_K):
                    c.done(tt(r.gate[:, k, :], r.gate[:, k, :], open_[:, :], ALU.mult))
                    c.done(tt(kp[:, k, :], kp[:, k, :], open_[:, :], ALU.mult))
                c.sync()
                c.step(tt(r.gate[:, 0, :], r.gate[:, 0, :], M[0][:, R, :], ALU.add))


NOWHERE = 1 << 20


def dispatch(kit, tag, r):
    nc = kit.nc
    with ExitStack() as st:
        sb, _, sem = scoped(nc, st, tag + "_d")
        rows, where = sb("rows", [P, GT, C]), sb("where", [P, GT, TOP_K], I32)
        staged = [sem(f"staged{j}") for j in range(GT)]
        sent = [sem(f"sent{j}") for j in range(GT)]
        block = st.enter_context(nc.Block())

        @block.vector
        def _(v):
            with v.Fori(0, NG) as g:
                for j in range(GT):
                    v.wait_ge(sent[j], 32 * g)
                    nc.vector.tensor_copy(rows[:, j, :], kit.XN[:, bass.ds(g * GT + j, 1), :].squeeze(1))
                    nc.vector.tensor_copy(where[:, j, :], r.slot_out[:, bass.ds(g * GT + j, 1), :].squeeze(1)).then_inc(staged[j], 1)

        @block.gpsimd
        def _(pool):
            with pool.Fori(0, NG) as g:
                for j in range(GT):
                    pool.wait_ge(staged[j], g + 1)
                    kit.passed(pool)
                    for k in range(TOP_K):
                        nc.gpsimd.indirect_dma_start(
                            out=kit.packed[:, :], out_offset=bass.IndirectOffsetOnAxis(ap=where[:, j, k:k + 1], axis=0),
                            in_=rows[:, j, :], in_offset=None, bounds_check=SLOTS - 1, oob_is_err=False).then_inc(sent[j], 16)
            for j in range(GT):
                pool.wait_ge(sent[j], 32 * NG)


def run_experts(kit, tag, r):
    nc, m = kit.nc, MOES[tag]
    T = m.tiles
    HALF = FF // 2
    with ExitStack() as st:
        sb, ps, sem = scoped(nc, st, tag + "_e")
        xin, xT = sb("xin", [P, 2, C]), sb("xT", [C, 2, P])
        w1 = [sb(f"w1_{i}", [C, FF]) for i in range(2)]
        b1 = sb("b1", [P, 2, FK])
        hT, y = [sb(f"hT{i}", [P, FK, P]) for i in range(2)], sb("y", [P, 2, C])
        p_x, p_h, p_y = ([ps(f"{n}{i}", [P, 512]) for i in range(2)] for n in ("p_x", "p_h", "p_y"))
        in_done, out_done = [sem(f"in_done{i}") for i in range(2)], [sem(f"out_done{i}") for i in range(2)]
        x_ps, xT_ready, w1a_ready, w1b_ready, b1_ready, h_ps, hb_ready, g_ready, y_ps, y_ready = (
            sem(n) for n in "x_ps xT_ready w1a_ready w1b_ready b1_ready h_ps hb_ready g_ready y_ps y_ready".split())
        experts = (kit.experts_in, kit.experts_loaded)
        block = st.enter_context(nc.Block())

        def expert(engine, i):
            return engine.value_load(r.tile_expert[0:1, bass.ds(i, 1)], min_val=0, max_val=m.experts - 1)

        def steps(engine, body):
            body(0, 0, 0, True)
            body(1, 1, 0, True)
            with engine.Fori(0, (T - 2) // 2) as n:
                for s in range(2):
                    body(n * 2 + (2 + s), s, n + 1, False)

        @block.sync
        def _(sp):
            def load(i, s, half, first):
                if not first:
                    sp.wait_ge(x_ps, i - 1)
                sp.dma_start(xin[:, s, :], kit.packed[bass.ds(i * P, P), :]).then_inc(in_done[s], 16)
            steps(sp, load)

        @block.gpsimd
        def _(pool):
            pool.wait_ge(*experts)

            def weights(i, s, half, first):
                e = expert(pool, i)
                if not first:
                    pool.wait_ge(h_ps, i - 1)
                nc.gpsimd.tensor_copy(w1[s][:, HALF:], kit.W1[:, bass.ds(e, 1), HALF:].squeeze(1)).then_inc(w1b_ready, 1)
                if not first:
                    pool.wait_ge(hb_ready, i - 1)
                nc.gpsimd.tensor_copy(b1[:, s, :], kit.B1[:, bass.ds(e, 1), :].squeeze(1)).then_inc(b1_ready, 1)
            steps(pool, weights)

        @block.scalar
        def _(act):
            act.wait_ge(*experts)

            def weights(i, s, half, first):
                e = expert(act, i)
                if not first:
                    act.wait_ge(h_ps, i - 1)
                nc.scalar.activation(w1[s][:, :HALF], kit.W1[:, bass.ds(e, 1), :HALF].squeeze(1), ACT.Copy).then_inc(w1a_ready, 1)

            def gelu(i, s):
                act.wait_ge(hb_ready, i + 1)
                hidden = hT[s][:, :, :].rearrange("p k t -> p (k t)")
                nc.scalar.activation(hidden, hidden, ACT.Gelu).then_inc(g_ready, 1)

            def send(i, s, half):
                act.wait_ge(y_ready, i + 1)
                act.dma_start(kit.expert_out[bass.ds(i * P, P), :], y[:, s, :]).then_inc(out_done[s], 16)

            weights(0, 0, 0, True)
            weights(1, 1, 0, True)
            gelu(0, 0)
            weights(2, 0, 1, False)
            gelu(1, 1)
            with act.Fori(0, (T - 4) // 2) as n:
                for s in range(2):
                    weights(n * 2 + 3 + s, 1 - s, 0, False)
                    send(n * 2 + s, s, 0)
                    gelu(n * 2 + 2 + s, s)
            weights(T - 1, 1, 0, False)
            send(T - 4, 0, 0)
            gelu(T - 2, 0)
            send(T - 3, 1, 0)
            gelu(T - 1, 1)
            send(T - 2, 0, 0)
            send(T - 1, 1, 0)
            for s in range(2):
                act.wait_ge(out_done[s], 16 * (T // 2))

        @block.vector
        def _(v):
            def rows(i, s, half, first):
                v.wait_ge(x_ps, i + 1)
                if not first:
                    v.wait_ge(h_ps, i - 1)
                nc.vector.tensor_copy(xT[:, s, :], p_x[s][:, 0:P]).then_inc(xT_ready, 1)

            def add_b1(i, s, first=False):
                v.wait_ge(h_ps, i + 1)
                v.wait_ge(b1_ready, i + 1)
                if not first:
                    v.wait_ge(y_ps, i - 1)
                nc.vector.tensor_tensor(hT[s][:, :, :], p_h[s][:, :].rearrange("p (k t) -> p k t", t=P),
                                        b1[:, s, :].unsqueeze(2).to_broadcast([P, FK, P]), ALU.add).then_inc(hb_ready, 1)

            def add_b2(i, s, half, first=False):
                e = expert(v, i)
                v.wait_ge(y_ps, i + 1)
                if not first:
                    v.wait_ge(out_done[s], half * 16)
                nc.vector.tensor_tensor(y[:, s, :], p_y[s][:, 0:C], kit.B2[:, bass.ds(e, 1), :].squeeze(1), ALU.add).then_inc(y_ready, 1)

            v.wait_ge(*experts)
            rows(0, 0, 0, True)
            rows(1, 1, 0, True)
            add_b1(0, 0, True)
            rows(2, 0, 1, False)
            add_b1(1, 1, True)
            add_b2(0, 0, 0, True)
            rows(3, 1, 1, False)
            add_b1(2, 0)
            add_b2(1, 1, 0, True)
            with v.Fori(0, (T - 4) // 2) as n:
                for s in range(2):
                    rows(n * 2 + 4 + s, s, 0, False)
                    add_b1(n * 2 + 3 + s, 1 - s)
                    add_b2(n * 2 + 2 + s, s, n + 1)
            add_b1(T - 1, 1)
            add_b2(T - 2, 0, T // 2 - 1)
            add_b2(T - 1, 1, T // 2 - 1)

        @block.tensor
        def _(pe):
            def rows(i, s, half, first=False):
                pe.wait_ge(in_done[s], 16 * half + 16)
                if not first:
                    pe.wait_ge(xT_ready, i - 1)
                nc.tensor.transpose(p_x[s][:, 0:P], xin[:, s, :], kit.ident[:, :]).then_inc(x_ps, 1)

            def up(i, s, first=False):
                pe.wait_ge(xT_ready, i + 1)
                pe.wait_ge(w1a_ready, i + 1)
                pe.wait_ge(w1b_ready, i + 1)
                if not first:
                    pe.wait_ge(hb_ready, i - 1)
                for k in range(FK):
                    ins = nc.tensor.matmul(p_h[s][:, k * P:(k + 1) * P], w1[s][:, k * P:(k + 1) * P], xT[:, s, :], start=True, stop=True)
                ins.then_inc(h_ps, 1)

            def down(i, s, first=False):
                e = expert(pe, i)
                pe.wait_ge(g_ready, i + 1)
                if not first:
                    pe.wait_ge(y_ready, i - 1)
                for k in range(FK):
                    ins = nc.tensor.matmul(p_y[s][:, 0:C], hT[s][:, k, :], kit.W2[:, bass.ds(e, 1), k, :].squeeze(1),
                                           start=(k == 0), stop=(k == FK - 1))
                ins.then_inc(y_ps, 1)

            pe.wait_ge(*experts)
            rows(0, 0, 0, True)
            rows(1, 1, 0, True)
            up(0, 0, True)
            rows(2, 0, 1)
            up(1, 1, True)
            down(0, 0, True)
            rows(3, 1, 1)
            up(2, 0)
            down(1, 1, True)
            with pe.Fori(0, (T - 4) // 2) as n:
                for s in range(2):
                    rows(n * 2 + 4 + s, s, n + 2)
                    up(n * 2 + 3 + s, 1 - s)
                    down(n * 2 + 2 + s, s)
            up(T - 1, 1)
            down(T - 2, 0)
            down(T - 1, 1)


def combine(kit, tag, r):
    nc = kit.nc
    with ExitStack() as st:
        sb, _, sem = scoped(nc, st, tag + "_c")
        rows, where = [sb(f"rows{i}", [P, GT, TOP_K, C]) for i in range(2)], [sb(f"where{i}", [P, GT, TOP_K], I32) for i in range(2)]
        staged, halved, used = sem("staged"), sem("halved"), sem("used")
        here = [[sem(f"here{i}{j}") for j in range(GT)] for i in range(2)]
        block = st.enter_context(nc.Block())

        def run(engine, step):
            pipelined(engine, (-1, NG), NG, step, 3, NG - 1)

        @block.vector
        def _(v):
            def step(n, s, live, after):
                if live(n + 1):
                    nc.vector.tensor_copy(where[1 - s][:, :, :], r.slot_back[:, bass.ds((n + 1) * GT, GT), :]).then_inc(staged, 1)
                if live(n):
                    for j in range(GT):
                        t = bass.ds(n * GT + j, 1)
                        v.wait_ge(here[s][j], 16 * (n - s) + 32)
                        x = kit.X[:, t, :].squeeze(1)
                        ins = nc.vector.scalar_tensor_tensor(x, rows[s][:, j, 0, :], r.gate[:, 0, t], x, ALU.mult, ALU.add)
                    ins.then_inc(halved, 1)
                    v.wait_ge(halved, n + 1)
                    for j in range(GT):
                        t = bass.ds(n * GT + j, 1)
                        x = kit.X[:, t, :].squeeze(1)
                        ins = nc.vector.scalar_tensor_tensor(x, rows[s][:, j, 1, :], r.gate[:, 1, t], x, ALU.mult, ALU.add)
                    ins.then_inc(used, 1)
            run(v, step)

        @block.gpsimd
        def _(pool):
            def step(n, s, live, after):
                if live(n + 1):
                    t = 1 - s
                    pool.wait_ge(staged, n + 2)
                    if after(n + 1, 2):
                        pool.wait_ge(used, n)
                    kit.passed(pool)
                    for j in range(GT):
                        for k in range(TOP_K):
                            nc.gpsimd.indirect_dma_start(
                                out=rows[t][:, j, k, :], out_offset=None, in_=kit.expert_out[0:MOES[tag].tiles * P, :],
                                in_offset=bass.IndirectOffsetOnAxis(ap=where[t][:, j, k:k + 1], axis=0)).then_inc(here[t][j], 16)
            run(pool, step)


def attention(kit, tag):
    nc, A = kit.nc, kit.A
    SCALE = C ** -0.5
    NB = GROUP // S
    with ExitStack() as st:
        sb, ps, sem = scoped(nc, st, tag)
        w = {n: sb(n, [C, C]) for n in ("Wq", "Wk", "Wv", "Wo")}
        bias = {n: sb(n, [C, 1]) for n in ("bq", "bk", "bv")}
        bo = sb("bo", [P, C])
        cT = [sb(f"cT{i}", [C, GROUP]) for i in range(2)]
        stats, mv, var, rstd = sb("stats", [P, GT, 6]), sb("mv", [P, GT, 2]), sb("var", [P, GT]), sb("rstd", [P, GT])
        xn = [sb(f"xn{i}", [P, GT, C]) for i in range(2)]
        xnT = sb("xnT", [C, TOK])
        QT, KT, V = ([sb(f"{n}{i}", shape) for i in range(2)] for n, shape in (("QT", [C, GROUP]), ("KT", [C, GROUP]), ("V", [S, NB * C])))
        Pm, mx, su, rs = sb("Pm", [P, PAIRS, S]), sb("mx", [P, PAIRS]), sb("su", [P, PAIRS]), sb("rs", [P, PAIRS])
        PT, aT = sb("PT", [S, GROUP]), sb("aT", [C, GROUP])
        p_x, p_q, p_k, p_st, p_a, p_y = (ps(n, [P, 512]) for n in ("p_x", "p_q", "p_k", "p_st", "p_a", "p_y"))
        p_v = ps("p_v", [P, 1024])
        kv_in, rest_in, dve, var_ready, rstd_ready = (sem(n) for n in ("kv_in", "rest_in", "dve", "var_ready", "rstd_ready"))
        ctx_in = [sem(f"ctx_in{i}") for i in range(2)]
        (xn_ready, xT_ps, xnT_ready, q_ps, k_ps, v_ps, qT_ready, kT_ready, v_ready, s_ps, mx_ready, d_ready, e_ready, sums, p_ready, t_ps,
         pT_ready, a_ps, a_ready, y_ps, y_added, bo_added) = (sem(n) for n in (
             "xn_ready xT_ps xnT_ready q_ps k_ps v_ps qT_ready kT_ready v_ready s_ps mx_ready d_ready e_ready sums p_ready t_ps "
             "pT_ready a_ps a_ready y_ps y_added bo_added").split())
        X = kit.X
        block = st.enter_context(nc.Block())
        group, tiles = lambda n: bass.ds(n * GROUP, GROUP), lambda n: bass.ds(n * GT, GT)

        def run(engine, step):
            pipelined(engine, (-2, NG + 2), NG, step, 4, NG - 2)

        @block.sync
        def _(sp):
            for n in ("Wk", "Wv"):
                sp.dma_start(w[n][:, :], A[f"{tag}_{n}"]).then_inc(kv_in, 16)
            for n in ("Wq", "Wo"):
                sp.dma_start(w[n][:, :], A[f"{tag}_{n}"]).then_inc(rest_in, 16)
            for n in bias:
                sp.dma_start(bias[n][:, :], A[f"{tag}_{n}"].rearrange("(c a) -> c a", a=1)).then_inc(rest_in, 16)
            sp.dma_start(bo[:, :], A[f"{tag}_bo"].rearrange("(a c) -> a c", a=1).to_broadcast([P, C])).then_inc(rest_in, 16)

            def step(n, s, live, after):
                if live(n + 1):
                    if after(n + 1, 2):
                        sp.wait_ge(v_ps, n)
                    sp.dma_start(cT[1 - s][:, :], A["ctxT"][:, group(n + 1)]).then_inc(ctx_in[1 - s], 16)
            run(sp, step)

        @block.gpsimd
        def _(pool):
            pool.wait_ge(rest_in, 96)

            def step(n, s, live, after):
                if live(n + 2):
                    xg = X[:, tiles(n + 2), :]
                    inverse_root(nc, pool, var, var_ready, rstd, rstd_ready, kit.minus_half, n + 2)
                    pool.wait_ge(xn_ready, n + 3)
                    nc.gpsimd.tensor_tensor(xg, xg, bo[:, :].unsqueeze(1).to_broadcast([P, GT, C]), ALU.add).then_inc(bo_added, 1)
            run(pool, step)

        @block.scalar
        def _(act):
            act.wait_ge(rest_in, 96)

            def step(n, s, live, after):
                t = 1 - s
                if live(n - 1):
                    act.wait_ge(d_ready, n)
                    nc.scalar.activation(Pm[:, :, :], Pm[:, :, :], ACT.Exp, scale=SCALE).then_inc(e_ready, 1)
                if live(n):
                    act.wait_ge(v_ps, n + 1)
                    if after(n, 2):
                        act.wait_ge(a_ps, n - 1)
                    nc.scalar.activation(V[s][:, :], p_v[0:S, :], ACT.Copy).then_inc(v_ready, 1)
                if live(n + 1):
                    act.wait_ge(xT_ps, n + 2)
                    nc.scalar.activation(xnT[:, group(n + 1)], p_x[:, :], ACT.Copy).then_inc(xnT_ready, 1)
                if live(n - 1):
                    act.wait_ge(t_ps, n)
                    nc.scalar.activation(PT[:, :], p_st[0:S, :], ACT.Copy).then_inc(pT_ready, 1)
                if live(n + 1):
                    act.wait_ge(q_ps, n + 2)
                    if after(n + 1, 2):
                        act.wait_ge(s_ps, n)
                    nc.scalar.activation(QT[t][:, :], p_q[:, :], ACT.Identity, bias=bias["bq"][:, :]).then_inc(qT_ready, 1)
            run(act, step)

        @block.vector
        def _(v):
            v.wait_ge(rest_in, 96)
            tt, ts = nc.vector.tensor_tensor, nc.vector.tensor_scalar

            def step(n, s, live, after):
                x = lambda j: X[:, bass.ds((n + 2) * GT + j, 1), :].squeeze(1)
                wide = lambda t: t[:, :].unsqueeze(2).to_broadcast([P, PAIRS, S])
                if live(n - 1):
                    v.wait_ge(s_ps, n)
                    s3 = p_st[:, 0:PAIRS * S].rearrange("p (j k) -> p j k", k=S)
                    nc.vector.tensor_reduce(mx[:, :], s3, AX.X, ALU.max).then_inc(mx_ready, 1)
                    v.wait_ge(mx_ready, n)
                    if after(n - 1, 1):
                        v.wait_ge(t_ps, n - 1)
                    tt(Pm[:, :, :], s3, wide(mx), ALU.subtract).then_inc(d_ready, 1)
                if live(n + 2):
                    for j in range(GT):
                        ins = nc.vector.bn_stats(stats[:, j, :], x(j))
                    ins.then_inc(dve, 1)
                    v.wait_ge(dve, 2 * n + 5)
                    kit.passed(v)
                    for j in range(GT):
                        ins = nc.vector.bn_aggr(mv[:, j, :], stats[:, j, :])
                    ins.then_inc(dve, 1)
                    v.wait_ge(dve, 2 * n + 6)
                    ts(var[:, :], mv[:, :, 1], LN_EPS, None, ALU.add).then_inc(var_ready, 1)
                if live(n):
                    v.wait_ge(k_ps, n + 1)
                    if after(n, 2):
                        v.wait_ge(s_ps, n - 1)
                    ts(KT[s][:, :], p_k[:, :], bias["bk"][:, :], None, ALU.add).then_inc(kT_ready, 1)
                if live(n - 1):
                    v.wait_ge(e_ready, n)
                    nc.vector.tensor_reduce(su[:, :], Pm[:, :, :], AX.X, ALU.add).then_inc(sums, 1)
                    v.wait_ge(sums, 2 * n - 1)
                    nc.vector.reciprocal(rs[:, :], su[:, :]).then_inc(sums, 1)
                    v.wait_ge(sums, 2 * n)
                    tt(Pm[:, :, :], Pm[:, :, :], wide(rs), ALU.mult).then_inc(p_ready, 1)
                if live(n - 2):
                    m = n - 2
                    v.wait_ge(a_ps, m + 1)
                    if after(m, 1):
                        v.wait_ge(y_ps, m)
                    nc.vector.scalar_tensor_tensor(aT[:, :], p_a[:, :], bias["bv"][:, :], xnT[:, group(m)], ALU.add, ALU.add).then_inc(a_ready, 1)
                if live(n + 2):
                    v.wait_ge(rstd_ready, n + 3)
                    if after(n + 2, 2):
                        v.wait_ge(xT_ps, n + 1)
                    for j in range(GT):
                        ins = ts(xn[s][:, j, :], x(j), mv[:, j, 0:1], rstd[:, j:j + 1], ALU.subtract, ALU.mult)
                    ins.then_inc(xn_ready, 1)
                if live(n - 2):
                    m = n - 2
                    v.wait_ge(y_ps, m + 1)
                    v.wait_ge(bo_added, m + 1)
                    xg = X[:, tiles(m), :]
                    tt(xg, xg, p_y[:, :].rearrange("p (t c) -> p t c", c=C), ALU.add).then_inc(y_added, 1)
            run(v, step)

        @block.tensor
        def _(pe):
            pe.wait_ge(rest_in, 96)
            pe.wait_ge(kv_in, 32)

            def step(n, s, live, after):
                t = 1 - s
                if live(n - 1):
                    pe.wait_ge(qT_ready, n)
                    pe.wait_ge(kT_ready, n)
                    if after(n - 1, 1):
                        pe.wait_ge(pT_ready, n - 1)
                    kit.passed(pe)
                    for b in range(NB):
                        c = slice(b * S, (b + 1) * S)
                        ins = nc.tensor.matmul(p_st[b % 2 * S:(b % 2 + 1) * S, b // 2 * S:(b // 2 + 1) * S], QT[t][:, c], KT[t][:, c],
                                               start=True, stop=True)
                    ins.then_inc(s_ps, 1)
                if live(n):
                    pe.wait_ge(ctx_in[s], 8 * (n - s) + 16)
                    if after(n, 1):
                        pe.wait_ge(kT_ready, n)
                    nc.tensor.matmul(p_k[:, :], w["Wk"][:, :], cT[s][:, :], start=True, stop=True).then_inc(k_ps, 1)
                    if after(n, 1):
                        pe.wait_ge(v_ready, n)
                    kit.passed(pe)
                    for b in range(NB):
                        ins = nc.tensor.matmul(p_v[0:S, b * C:(b + 1) * C], cT[s][:, b * S:(b + 1) * S], w["Wv"][:, :], start=True, stop=True)
                    ins.then_inc(v_ps, 1)
                if live(n - 2):
                    m = n - 2
                    pe.wait_ge(v_ready, m + 1)
                    pe.wait_ge(pT_ready, m + 1)
                    if after(m, 1):
                        pe.wait_ge(a_ready, m)
                    kit.passed(pe)
                    for b in range(NB):
                        ins = nc.tensor.matmul(p_a[:, b * S:(b + 1) * S], V[s][:, b * C:(b + 1) * C], PT[:, b * S:(b + 1) * S], start=True, stop=True)
                    ins.then_inc(a_ps, 1)
                if live(n + 1):
                    pe.wait_ge(xn_ready, n + 2)
                    if after(n + 1, 1):
                        pe.wait_ge(xnT_ready, n + 1)
                    for j in range(GT):
                        ins = nc.tensor.transpose(p_x[:, j * P:(j + 1) * P], xn[t][:, j, :], kit.ident[:, :])
                    ins.then_inc(xT_ps, 1)
                if live(n - 2):
                    m = n - 2
                    pe.wait_ge(a_ready, m + 1)
                    if after(m, 1):
                        pe.wait_ge(y_added, m)
                    for j in range(GT):
                        ins = nc.tensor.matmul(p_y[:, j * C:(j + 1) * C], aT[:, j * P:(j + 1) * P], w["Wo"][:, :], start=True, stop=True)
                    ins.then_inc(y_ps, 1)
                if live(n - 1):
                    pe.wait_ge(p_ready, n)
                    kit.passed(pe)
                    for j in range(PAIRS):
                        ins = nc.tensor.transpose(p_st[0:S, j * P:(j + 1) * P], Pm[:, j, :], kit.ident[:, :])
                    ins.then_inc(t_ps, 1)
                if live(n + 1):
                    pe.wait_ge(xnT_ready, n + 2)
                    if after(n + 1, 1):
                        pe.wait_ge(qT_ready, n + 1)
                    nc.tensor.matmul(p_q[:, :], w["Wq"][:, :], xnT[:, group(n + 1)], start=True, stop=True).then_inc(q_ps, 1)
            run(pe, step)


def mlstm(kit, tag):
    nc = kit.nc
    H, DH = 8, 16
    HH = H // 2
    VW = 2 * 2 * DH + 2
    with ExitStack() as st:
        sb, _, _ = scoped(nc, st, tag)
        QT, KT = sb("QT", [C, TOK]), sb("KT", [C, TOK])
        V2 = sb("V2", [P, B, 2, VW])
        gm, M = sb("gm", [H, TOK]), sb("M", [H, TOK])
        en = sb("en", [P, TILES, 2 * HH])
        mlstm_gates(kit, tag, QT, KT, V2, gm, M, en, H, DH, HH, VW)
        mlstm_attend(kit, tag, QT, KT, V2, gm, M, en, H, DH, HH, VW)


def mlstm_gates(kit, tag, QT, KT, V2, gm, M, en, H, DH, HH, VW):
    nc, A = kit.nc, kit.A
    NB = GROUP // S
    FAR = -1e30
    with ExitStack() as st:
        sb, ps, sem = scoped(nc, st, tag + "_g")
        gate_w = sb("gate_w", [C, 3, P])
        ib, fb = sb("ib", [H, 1]), sb("fb", [H, 1])
        half_mask = sb("half_mask", [P, C])
        hoh, foh = sb("hoh", [H, HH]), sb("foh", [H, 2])
        c2 = [sb(f"c2_{i}", [P, NB, C]) for i in range(2)]
        stats, mv, var, rstd = sb("stats", [P, GT, 6]), sb("mv", [P, GT, 2]), sb("var", [P, GT]), sb("rstd", [P, GT])
        xn = [sb(f"xn{i}", [P, GT, C]) for i in range(2)]
        na, lf, cs, low = (sb(n, [H, GROUP]) for n in ("na", "lf", "cs", "low"))
        i_, f_ = [sb(f"i_{k}", [H, GROUP]) for k in range(2)], [sb(f"f_{k}", [H, GROUP]) for k in range(2)]
        restart, drop = sb("restart", [H, GROUP]), sb("drop", [H, GROUP])
        nm = sb("nm", [P, NB, 2, S])
        head_rows = sb("head_rows", [P, HH])
        p_x = [ps(f"p_x{i}", [P, 512]) for i in range(2)]
        p_g, p_n = ps("p_g", [P, 512]), ps("p_n", [P, 512])
        keys_in, weights = sem("keys_in"), sem("weights")
        c2_in = [sem(f"c2_in{i}") for i in range(2)]
        (set_up, var_ready, rstd_ready, xn_ready, xT_ps, xnT_ready, g_ps, fi_ready, na_ready, exp_ready, l_ready, scanned,
         m_ready, nm_ready, n_ps, en_ready, v_ready, dve) = (sem(n) for n in (
             "set_up var_ready rstd_ready xn_ready xT_ps xnT_ready g_ps fi_ready na_ready exp_ready l_ready scanned "
             "m_ready nm_ready n_ps en_ready v_ready dve").split())
        N_WEIGHTS, SET_UP = 16 * 6, 11
        X = kit.X
        block = st.enter_context(nc.Block())
        group = lambda n: bass.ds(n * GROUP, GROUP)

        def run(engine, step):
            pipelined(engine, (0, NG + 2), NG, step, 4, NG)

        @block.sync
        def _(sp):
            row = lambda name, parts, n: A[name].rearrange("(a c) -> a c", a=1).to_broadcast([parts, n])
            col = lambda name: A[name].rearrange("(c a) -> c a", a=1)
            for dst, src in ((gate_w[:, :, :], A[f"{tag}_gate_w"]), (ib[:, :], col(f"{tag}_igate_b")), (fb[:, :], col(f"{tag}_fgate_b")),
                             (half_mask[:, :], A["half_mask16"]), (hoh[:, :], A["head_of_half"]), (foh[:, :], A["half_of_head"])):
                sp.dma_start(dst, src).then_inc(weights, 16)
            sp.dma_start(KT[:, :], A["ctxT"]).then_inc(keys_in, 16)

            def step(n, s, live, after):
                if live(n):
                    if after(n, 2):
                        sp.wait_ge(v_ready, n - 1)
                    for twice in range(2):
                        sp.dma_start(c2[s][twice * S:(twice + 1) * S, :, :],
                                     A["ctx"][group(n), :].rearrange("(b s) c -> s b c", s=S)).then_inc(c2_in[s], 16)
            run(sp, step)

        @block.gpsimd
        def _(pool):
            pool.wait_ge(weights, N_WEIGHTS)
            pool.wait_ge(set_up, SET_UP)

            def step(n, s, live, after):
                if live(n):
                    inverse_root(nc, pool, var, var_ready, rstd, rstd_ready, kit.minus_half, n)
                    pool.wait_ge(c2_in[s], 16 * (n - s) + 32)
                    hm = half_mask[:, :].rearrange("p (f i c) -> p i f c", f=2, c=2 * DH)
                    for b in range(NB):
                        ins = nc.gpsimd.tensor_tensor(
                            V2[:, bass.ds(n * NB + b, 1), :, 0:4 * DH].squeeze(1).rearrange("p i (f c) -> p i f c", f=2),
                            c2[s][:, b, :].rearrange("p (f i c) -> p i f c", f=2, c=2 * DH), hm, ALU.mult)
                    ins.then_inc(v_ready, 1)
                if live(n - 1):
                    pool.wait_ge(m_ready, n)
                    if after(n - 1, 1):
                        pool.wait_ge(n_ps, n - 1)
                    nc.gpsimd.tensor_tensor(nm[0:H, :, :, :], low[:, :].rearrange("h (b s) -> h b s", s=S).unsqueeze(2).to_broadcast([H, NB, 2, S]),
                                            foh[:, :].unsqueeze(1).unsqueeze(3).to_broadcast([H, NB, 2, S]), ALU.mult).then_inc(nm_ready, 1)
            run(pool, step)

        @block.scalar
        def _(act):
            act.wait_ge(weights, N_WEIGHTS)

            def step(n, s, live, after):
                if live(n - 1):
                    act.wait_ge(g_ps, n)
                    if after(n - 1, 2):
                        act.wait_ge(m_ready, n - 2)
                    nc.scalar.activation(f_[1 - s][:, :], p_g[32:40, :], ACT.Identity, bias=fb[:, :])
                    nc.scalar.activation(i_[1 - s][:, :], p_g[0:H, :], ACT.Identity, bias=ib[:, :]).then_inc(fi_ready, 1)
                if live(n - 1):
                    act.wait_ge(na_ready, n)
                    nc.scalar.activation(na[:, :], na[:, :], ACT.Exp).then_inc(exp_ready, 1)
                    act.wait_ge(exp_ready, n)
                    nc.scalar.activation(na[:, :], na[:, :], ACT.Ln, bias=1.0).then_inc(l_ready, 1)
                if live(n):
                    act.wait_ge(xT_ps, n + 1)
                    nc.scalar.activation(QT[:, group(n)], p_x[s][:, :], ACT.Copy).then_inc(xnT_ready, 1)
                if live(n - 2):
                    act.wait_ge(n_ps, n - 1)
                    if not after(n - 2, 1):
                        act.wait_ge(set_up, SET_UP)
                    nc.scalar.activation(en[:, bass.ds((n - 2) * GT, GT), :].rearrange("p j h -> p (j h)"), p_n[:, 0:PAIRS * 2 * HH],
                                         ACT.Exp).then_inc(en_ready, 1)
            run(act, step)

        @block.vector
        def _(v):
            tt, ts, stt = nc.vector.tensor_tensor, nc.vector.tensor_scalar, nc.vector.scalar_tensor_tensor
            at = 0

            def setup(ins):
                nonlocal at
                at += 1
                ins.then_inc(set_up, 1)
                v.wait_ge(set_up, at)

            setup(nc.vector.memset(restart[:, :], 1.0))
            setup(nc.vector.memset(restart[:, :].rearrange("h (b s) -> h b s", s=S)[:, :, 0], 0.0))
            setup(nc.vector.memset(drop[:, :], 0.0))
            setup(nc.vector.memset(drop[:, :].rearrange("h (b s) -> h b s", s=S)[:, :, 0], FAR))
            setup(nc.vector.memset(V2[:, :, :, 4 * DH:VW], 0.0))
            setup(nc.vector.memset(V2[0:S, :, :, 4 * DH:4 * DH + 1], 1.0))
            setup(nc.vector.memset(V2[S:P, :, :, 4 * DH + 1:VW], 1.0))
            setup(nc.vector.memset(nm[:, :, :, :], 0.0))
            setup(nc.vector.memset(head_rows[:, :], 0.0))
            v.wait_ge(weights, N_WEIGHTS)
            setup(nc.vector.tensor_copy(head_rows[0:H, :], hoh[:, :]))
            setup(tt(gate_w[:, 1, :], gate_w[:, 1, :], gate_w[:, 2, :], ALU.add))
            assert at == SET_UP

            def step(n, s, live, after):
                x = lambda j: X[:, bass.ds(n * GT + j, 1), :].squeeze(1)
                if live(n):
                    for j in range(GT):
                        ins = nc.vector.bn_stats(stats[:, j, :], x(j))
                    ins.then_inc(dve, 1)
                    v.wait_ge(dve, 2 * n + 1)
                    kit.passed(v)
                    for j in range(GT):
                        ins = nc.vector.bn_aggr(mv[:, j, :], stats[:, j, :])
                    ins.then_inc(dve, 1)
                    v.wait_ge(dve, 2 * n + 2)
                    ts(var[:, :], mv[:, :, 1], LN_EPS, None, ALU.add).then_inc(var_ready, 1)
                if live(n - 1):
                    v.wait_ge(fi_ready, n)
                    if after(n - 1, 1):
                        v.wait_ge(m_ready, n - 1)
                    stt(na[:, :], f_[1 - s][:, :], -1.0, f_[1 - s][:, :], ALU.mult, ALU.min).then_inc(na_ready, 1)
                if live(n):
                    v.wait_ge(rstd_ready, n + 1)
                    if after(n, 2):
                        v.wait_ge(xT_ps, n - 1)
                    for j in range(GT):
                        ins = ts(xn[s][:, j, :], x(j), mv[:, j, 0:1], rstd[:, j:j + 1], ALU.subtract, ALU.mult)
                    ins.then_inc(xn_ready, 1)
                if live(n - 1):
                    m = n - 1
                    v.wait_ge(l_ready, n)
                    stt(lf[:, :], f_[1 - s][:, :], 0.0, na[:, :], ALU.min, ALU.subtract).then_inc(scanned, 1)
                    v.wait_ge(scanned, 4 * m + 1)
                    nc.vector.tensor_tensor_scan(cs[:, :], restart[:, :], lf[:, :], 0.0, ALU.mult, ALU.add).then_inc(scanned, 1)
                    v.wait_ge(scanned, 4 * m + 2)
                    tt(gm[:, group(m)], i_[1 - s][:, :], cs[:, :], ALU.subtract).then_inc(scanned, 1)
                    v.wait_ge(scanned, 4 * m + 3)
                    nc.vector.tensor_tensor_scan(M[:, group(m)], drop[:, :], gm[:, group(m)], FAR, ALU.add, ALU.max).then_inc(scanned, 1)
                    v.wait_ge(scanned, 4 * m + 4)
                    if after(m, 1):
                        v.wait_ge(nm_ready, m)
                    stt(low[:, :], cs[:, :], -1.0, M[:, group(m)], ALU.mult, ALU.subtract).then_inc(m_ready, 1)
            run(v, step)

        @block.tensor
        def _(pe):
            pe.wait_ge(weights, N_WEIGHTS)
            pe.wait_ge(keys_in, 16)
            pe.wait_ge(set_up, SET_UP)

            def step(n, s, live, after):
                if live(n - 1):
                    m = n - 1
                    if after(m, 1):
                        pe.wait_ge(fi_ready, m)
                    pe.wait_ge(xnT_ready, m + 1)
                    kit.passed(pe)
                    nc.tensor.matmul(p_g[:, :], gate_w[:, 1, :], KT[:, group(m)], start=True, stop=False)
                    nc.tensor.matmul(p_g[:, :], gate_w[:, 0, :], QT[:, group(m)], start=False, stop=True).then_inc(g_ps, 1)
                if live(n):
                    pe.wait_ge(xn_ready, n + 1)
                    if after(n, 2):
                        pe.wait_ge(xnT_ready, n - 1)
                    for j in range(GT):
                        ins = nc.tensor.transpose(p_x[s][:, j * P:(j + 1) * P], xn[s][:, j, :], kit.ident[:, :])
                    ins.then_inc(xT_ps, 1)
                if live(n - 2):
                    pe.wait_ge(nm_ready, n - 1)
                    if after(n - 2, 1):
                        pe.wait_ge(en_ready, n - 2)
                    kit.passed(pe)
                    for b in range(NB):
                        ins = nc.tensor.matmul(p_n[:, b * HH:(b + 1) * HH], nm[:, b], head_rows[:, :], start=True, stop=True)
                    ins.then_inc(n_ps, 1)
            run(pe, step)


def mlstm_attend(kit, tag, QT, KT, V2, gm, M, en, H, DH, HH, VW):
    nc, A = kit.nc, kit.A
    EPS = 1e-6
    N = 2 * HH
    with ExitStack() as st:
        sb, ps, sem = scoped(nc, st, tag + "_a")
        out_w = sb("out_w", [P, C // 2])
        head_mask = sb("head_mask", [P, HH])
        pick = sb("pick", [P, 2, S])
        hoh, foh = sb("hoh", [H, HH]), sb("foh", [H, 2])
        minus_foh = sb("minus_foh", [H, 2])
        later32, later = sb("later32", [S, S]), sb("later", [S, N, S], BF16)
        ident2 = sb("ident2", [S, 2, S], BF16)
        Qz = [sb(f"Qz{i}", [C, 2, 2, S]) for i in range(2)]
        Km = [sb(f"Km{i}", [C, 2, HH, S]) for i in range(2)]
        left = [sb(f"left{i}", [P, 2, 2, S]) for i in range(2)]
        right = [sb(f"right{i}", [P, 2, HH, S]) for i in range(2)]
        D, Cm = sb("D", [P, 2, 512]), [sb(f"Cm{i}", [P, 512]) for i in range(2)]
        CT = sb("CT", [P, 512])
        n1, n2, nrm = sb("n1", [P, N]), sb("n2", [P, N]), sb("nrm", [P, N])
        raw, sq = sb("raw", [P, N, DH]), sb("sq", [P, N, DH])
        cen, hs, hh = sb("cen", [P, 2, N, DH]), sb("hs", [P, 2, N, DH]), sb("hh", [P, 2, N, DH])
        total, hv, hr = sb("total", [P, N]), sb("hv", [P, 2, N]), sb("hr", [P, 2, N])
        minus_half, ln_eps = sb("minus_half", [P, N]), sb("ln_eps", [P, 1])
        p_d, p_q = ([ps(f"{n}{i}", [P, 512]) for i in range(2)] for n in ("p_d", "p_q"))
        p_t, p_o, p_y = (ps(n, [P, 512]) for n in ("p_t", "p_o", "p_y"))
        consts_in = sem("consts_in")
        (set_up, qz_ready, km_ready, left_ready, right_ready, d_ps, q_ps, e_ready, c_ready, t_ps, cT_ready, o_ps, o_read, dve,
         hv_ready, hr_ready, hn_ready, y_ps, y_added, sums_ready, scaled) = (sem(n) for n in (
             "set_up qz_ready km_ready left_ready right_ready d_ps q_ps e_ready c_ready t_ps cT_ready o_ps o_read dve "
             "hv_ready hr_ready hn_ready y_ps y_added sums_ready scaled").split())
        N_CONSTS = 16 * 8
        SET_UP = 15
        X = kit.X
        block = st.enter_context(nc.Block())
        pair = lambda j: bass.ds(j * P, P)

        def run(engine, step):
            pipelined(engine, (-3, TILES + 5), TILES, step, 8, TILES - 4)

        @block.sync
        def _(sp):
            for dst, src in ((head_mask[:, :], A["head_mask16"]), (pick[:, :, :].rearrange("p f s -> p (f s)"), A["ident"]),
                             (hoh[:, :], A["head_of_half"]), (foh[:, :], A["half_of_head"]),
                             (later32[:, :], A["later"]), (minus_foh[:, :], A["minus_half_of_head"])):
                sp.dma_start(dst, src).then_inc(consts_in, 16)
            for f in range(2):
                half = A[f"{tag}_out_w"][f * 64:f * 64 + 64]
                sp.dma_start(out_w[f * S:(f + 1) * S, :], half.rearrange("(a c) -> a c", a=1).to_broadcast([S, C // 2])).then_inc(consts_in, 16)
            sp.wait_ge(consts_in, N_CONSTS)

        @block.gpsimd
        def _(pool):
            pool.wait_ge(consts_in, N_CONSTS)
            pool.wait_ge(set_up, SET_UP)

            def moving(j, s, after):
                if after(j, 2):
                    pool.wait_ge(d_ps, j - 1)
                b3 = lambda t: t[:, pair(j)].rearrange("h (b s) -> h b s", s=S)
                for b in range(2):
                    ins = nc.gpsimd.tensor_tensor(right[s][0:H, b], b3(gm)[:, b].unsqueeze(1).to_broadcast([H, HH, S]),
                                                  hoh[:, :].unsqueeze(2).to_broadcast([H, HH, S]), ALU.mult)
                ins.then_inc(right_ready, 1)
                if after(j, 2):
                    pool.wait_ge(q_ps, j - 1)
                for b in range(2):
                    ins = nc.gpsimd.tensor_tensor(Km[s][:, b], b3(KT)[:, b].unsqueeze(1).to_broadcast([C, HH, S]),
                                                  head_mask[:, :].unsqueeze(2).to_broadcast([C, HH, S]), ALU.mult)
                ins.then_inc(km_ready, 1)

            def weigh(j, s, after):
                pool.wait_ge(scaled, j + 1)
                if after(j, 2):
                    pool.wait_ge(y_ps, j - 1)
                nc.gpsimd.tensor_tensor(hh[:, s].rearrange("p (b h) c -> p b (h c)", h=HH), hs[:, s].rearrange("p (b h) c -> p b (h c)", h=HH),
                   out_w[:, :].unsqueeze(1).to_broadcast([P, 2, C // 2]), ALU.mult).then_inc(hn_ready, 1)

            def step(n, s, live, after):
                if live(n + 3):
                    moving(n + 3, 1 - s, after)
                if live(n - 2):
                    pool.wait_ge(hv_ready, n - 1)
                    if after(n - 2, 2):
                        pool.wait_ge(scaled, n - 3)
                    nc.gpsimd.tensor_tensor(hr[:, s, :], hv[:, s, :], minus_half[:, :], ALU.pow).then_inc(hr_ready, 1)
                if live(n - 3):
                    weigh(n - 3, 1 - s, after)
            run(pool, step)

        @block.scalar
        def _(act):
            act.wait_ge(consts_in, N_CONSTS)
            act.wait_ge(set_up, SET_UP)

            def queries(j, s, after):
                if after(j, 2):
                    act.wait_ge(q_ps, j - 1)
                for f in range(2):
                    rows = slice(64 * f, 64 * f + 64)
                    ins = nc.scalar.activation(Qz[s][rows, :, f, :], QT[rows, pair(j)].rearrange("c (b s) -> c b s", s=S), ACT.Copy)
                ins.then_inc(qz_ready, 1)

            def minus_m(j, s, after):
                if after(j, 2):
                    act.wait_ge(d_ps, j - 1)
                for f in range(2):
                    ins = nc.scalar.activation(left[s][32:40, :, f, :], M[:, pair(j)].rearrange("h (b s) -> h b s", s=S), ACT.Copy,
                                               scale=minus_foh[:, f:f + 1])
                ins.then_inc(left_ready, 1)

            def step(n, s, live, after):
                if live(n + 3):
                    minus_m(n + 3, 1 - s, after)
                    queries(n + 3, 1 - s, after)
                if live(n + 1):
                    act.wait_ge(d_ps, n + 2)
                    if after(n + 1, 2):
                        act.wait_ge(c_ready, n)
                    nc.scalar.activation(D[:, 1 - s, :], p_d[1 - s][:, :], ACT.Exp).then_inc(e_ready, 1)
                if live(n - 2):
                    act.wait_ge(sums_ready, n - 1)
                    nc.scalar.activation(hv[:, s, :], hv[:, s, :], ACT.Identity, scale=1.0 / DH, bias=ln_eps[:, :]).then_inc(hv_ready, 1)
                if live(n):
                    act.wait_ge(t_ps, n + 1)
                    if after(n, 1):
                        act.wait_ge(o_ps, n)
                    nc.scalar.activation(CT[:, :], p_t[:, :], ACT.Copy).then_inc(cT_ready, 1)
            run(act, step)

        @block.vector
        def _(v):
            tt, ts, stt = nc.vector.tensor_tensor, nc.vector.tensor_scalar, nc.vector.scalar_tensor_tensor
            at = 0

            def setup(ins):
                nonlocal at
                at += 1
                ins.then_inc(set_up, 1)
                v.wait_ge(set_up, at)

            for i in range(2):
                setup(nc.vector.memset(left[i][:, :, :, :], 0.0))
                setup(nc.vector.memset(right[i][:, :, :, :], 0.0))
                setup(nc.vector.memset(Qz[i][:, :, :, :], 0.0))
            v.wait_ge(consts_in, N_CONSTS)
            for i in range(2):
                setup(tt(left[i][0:H], left[i][0:H], foh[:, :].unsqueeze(1).unsqueeze(3).to_broadcast([H, 2, 2, S]), ALU.add))
                setup(tt(right[i][32:40], right[i][32:40], hoh[:, :].unsqueeze(1).unsqueeze(3).to_broadcast([H, 2, HH, S]), ALU.add))
            setup(nc.vector.memset(minus_half[:, :], -0.5))
            setup(nc.vector.memset(ln_eps[:, :], LN_EPS))
            setup(ts(en[:, :, :], en[:, :, :], EPS, None, ALU.add))
            setup(nc.vector.tensor_copy(ident2[:, :, :], pick[0:S, 0, :].unsqueeze(1).to_broadcast([S, 2, S])))
            setup(nc.vector.tensor_copy(later[:, :, :], later32[:, :].unsqueeze(1).to_broadcast([S, N, S])))
            assert at == SET_UP

            def product(j, s, after):
                v.wait_ge(e_ready, j + 1)
                v.wait_ge(q_ps, j + 1)
                if after(j, 2):
                    v.wait_ge(t_ps, j - 1)
                stt(Cm[s][:, :], p_q[s][:, :], DH ** -0.5, D[:, s, :], ALU.mult, ALU.mult).then_inc(c_ready, 1)

            STEPS = 7

            def normalise(j, s, after):
                at = 0

                def own(ins):
                    nonlocal at
                    at += 1
                    ins.then_inc(dve, 1)
                    v.wait_ge(dve, STEPS * j + at)

                v.wait_ge(o_ps, j + 1)
                po = p_o[:, 0:4 * VW].rearrange("p (h c) -> p h c", c=VW)
                own(nc.vector.tensor_copy(n1[:, :].rearrange("p (h c) -> p h c", c=2), po[:, :, 4 * DH:VW]))
                own(stt(n2[:, :], n1[:, :], -1.0, n1[:, :], ALU.mult, ALU.max))
                own(stt(n2[:, :], n2[:, :], EPS, en[:, bass.ds(j, 1), :].squeeze(1), ALU.add, ALU.max))
                own(nc.vector.reciprocal(nrm[:, :], n2[:, :]))
                for f in range(2):
                    q = slice(f * S, (f + 1) * S)
                    ins = tt(raw[q].rearrange("p (h a) c -> p h a c", a=2),
                             po[q, :, f * 2 * DH:(f + 1) * 2 * DH].rearrange("p h (a c) -> p h a c", c=DH),
                             nrm[q].rearrange("p (h a) -> p h a", a=2).unsqueeze(3).to_broadcast([S, HH, 2, DH]), ALU.mult)
                ins.then_inc(o_read, 1)
                v.wait_ge(o_read, j + 1)
                own(nc.vector.tensor_reduce(total[:, :], raw[:, :, :], AX.X, ALU.add))
                own(stt(cen[:, s], total[:, :].unsqueeze(2).to_broadcast([P, N, DH]), -1.0 / DH, raw[:, :, :], ALU.mult, ALU.add))
                own(tt(sq[:, :, :], cen[:, s], cen[:, s], ALU.mult))
                assert at == STEPS
                if after(j, 2):
                    v.wait_ge(hr_ready, j - 1)
                nc.vector.tensor_reduce(hv[:, s, :], sq[:, :, :], AX.X, ALU.add).then_inc(sums_ready, 1)

            def scale(j, s, after):
                v.wait_ge(hr_ready, j + 1)
                if after(j, 2):
                    v.wait_ge(hn_ready, j - 1)
                tt(hs[:, s], cen[:, s], hr[:, s, :].unsqueeze(2).to_broadcast([P, N, DH]), ALU.mult).then_inc(scaled, 1)

            def step(n, s, live, after):
                if live(n + 1):
                    product(n + 1, 1 - s, after)
                if live(n - 3):
                    scale(n - 3, 1 - s, after)
                if live(n - 5):
                    v.wait_ge(y_ps, n - 4)
                    x = X[:, bass.ds(n - 5, 1), :].squeeze(1)
                    tt(x, x, p_y[:, 0:C], ALU.add).then_inc(y_added, 1)
                if live(n - 1):
                    normalise(n - 1, 1 - s, after)
            run(v, step)

        @block.tensor
        def _(pe):
            pe.wait_ge(set_up, SET_UP)

            def step(n, s, live, after):
                if live(n + 1):
                    j, t = n + 1, 1 - s
                    if after(j, 2):
                        pe.wait_ge(e_ready, j - 1)
                    pe.wait_ge(left_ready, j + 1)
                    pe.wait_ge(right_ready, j + 1)
                    kit.passed(pe)
                    for b in range(2):
                        nc.tensor.matmul(p_d[t][:, b * 256:(b + 1) * 256], left[t][:, b], right[t][:, b], start=(b == 0),
                                         stop=False, skip_group_check=True)
                    nc.tensor.matmul(p_d[t][:, :], ident2[:, :, :], later[:, :, :], start=False, stop=True,
                                     skip_group_check=True).then_inc(d_ps, 1)
                    pe.wait_ge(qz_ready, j + 1)
                    pe.wait_ge(km_ready, j + 1)
                    if after(j, 2):
                        pe.wait_ge(c_ready, j - 1)
                    for b in range(2):
                        ins = nc.tensor.matmul(p_q[t][:, b * 256:(b + 1) * 256], Qz[t][:, b], Km[t][:, b], start=True, stop=True)
                    ins.then_inc(q_ps, 1)
                if live(n - 1):
                    j = n - 1
                    if after(j, 1):
                        pe.wait_ge(o_read, j)
                    pe.wait_ge(cT_ready, j + 1)
                    for i in range(4):
                        ins = nc.tensor.matmul(p_o[:, i * VW:(i + 1) * VW], CT[:, i * P:(i + 1) * P],
                                               V2[:, bass.ds(2 * j + i // 2, 1), i % 2, :].squeeze(1), start=True, stop=True)
                    ins.then_inc(o_ps, 1)
                if live(n):
                    pe.wait_ge(c_ready, n + 1)
                    if after(n, 1):
                        pe.wait_ge(cT_ready, n)
                    for i in range(4):
                        ins = nc.tensor.transpose(p_t[:, i * P:(i + 1) * P], Cm[s][:, i * P:(i + 1) * P], kit.ident[:, :])
                    ins.then_inc(t_ps, 1)
                if live(n - 4):
                    j = n - 4
                    pe.wait_ge(hn_ready, j + 1)
                    if after(j, 1):
                        pe.wait_ge(y_added, j)
                    kit.passed(pe)
                    for b in range(2):
                        for f in range(2):
                            ins = nc.tensor.matmul(p_y[b * S:(b + 1) * S, f * 64:f * 64 + 64], pick[:, f, :],
                                                   hh[:, s, b * HH:(b + 1) * HH, :], start=True, stop=True)
                    ins.then_inc(y_ps, 1)
            run(pe, step)


def quantised_ffn(kit, tag):
    nc = kit.nc
    TAPS = 3
    ROUND = 1.5 * 2.0 ** 23
    with ExitStack() as st:
        sb, _, _ = scoped(nc, st, tag)
        xT = sb("xT", [C, TOK])
        w1t, w2q = sb("w1t", [C, TAPS, FF]), sb("w2q", [P, FK, C], BF16)
        wmean = sb("wmean", [P, 2])
        identb, conv_b = sb("identb", [P, P], BF16), sb("conv_b", [P, FF])
        quantise_tokens(kit, tag, xT, w1t, w2q, wmean, identb, conv_b, TAPS, ROUND)
        quantised_products(kit, tag, xT, w1t, w2q, wmean, identb, conv_b, TAPS, ROUND)


def quantise_tokens(kit, tag, xT, w1t, w2q, wmean, identb, conv_b, TAPS, ROUND):
    nc, A = kit.nc, kit.A
    with ExitStack() as st:
        sb, ps, sem = scoped(nc, st, tag + "_q")
        w1, w2 = sb("w1", [C, FF]), sb("w2", [P, FK, C])
        taps = sb("taps", [P, TAPS, FF])
        wsum, wscale, wq = sb("wsum", [P, 2]), sb("wscale", [P, 2]), sb("wq", [P, FF])
        stats, mv, var, rstd = sb("stats", [P, GT, 6]), sb("mv", [P, GT, 2]), sb("var", [P, GT]), sb("rstd", [P, GT])
        xn, xq = [sb(f"xn{i}", [P, GT, C]) for i in range(2)], [sb(f"xq{i}", [P, GT, C]) for i in range(2)]
        amax = sb("amax", [P, GT])
        aback, ascale = [sb(f"aback{i}", [P, GT]) for i in range(2)], [sb(f"ascale{i}", [P, GT]) for i in range(2)]
        p_x, p_w = [ps(f"p_x{i}", [P, 512]) for i in range(2)], ps("p_w", [P, 512])
        weights, w_ps, set_up, dve = sem("weights"), sem("w_ps"), sem("set_up"), sem("dve")
        var_ready, rstd_ready, xn_ready, max_ready, rounded, xq_ready, xT_ps, xT_ready = (
            sem(n) for n in "var_ready rstd_ready xn_ready max_ready rounded xq_ready xT_ps xT_ready".split())
        N_WEIGHTS = 16 * 6
        X = kit.X
        block = st.enter_context(nc.Block())

        def run(engine, step):
            pipelined(engine, (0, NG + 1), NG, step, 2, NG)

        @block.sync
        def _(sp):
            for dst, src in ((w1[:, :], A[f"{tag}_w1"]), (w2[:, :, :], A[f"{tag}_w2"])):
                sp.dma_start(dst, src).then_inc(weights, 16)
            for k in range(TAPS):
                sp.dma_start(taps[:, k, :], A[f"{tag}_conv_w"][k:k + 1, :].to_broadcast([P, FF])).then_inc(weights, 16)
            sp.dma_start(conv_b[:, :], A[f"{tag}_conv_b"].rearrange("(a c) -> a c", a=1).to_broadcast([P, FF])).then_inc(weights, 16)
            sp.wait_ge(weights, N_WEIGHTS)

        @block.gpsimd
        def _(pool):
            def step(n, s, live, after):
                if live(n):
                    inverse_root(nc, pool, var, var_ready, rstd, rstd_ready, kit.minus_half, n)
            run(pool, step)

        @block.vector
        def _(v):
            tt, ts = nc.vector.tensor_tensor, nc.vector.tensor_scalar
            DVE_STEPS = 5
            wide = lambda t: t[:, :].unsqueeze(2).to_broadcast([P, GT, C])

            def step(n, s, live, after):
                x = lambda j: X[:, bass.ds(n * GT + j, 1), :].squeeze(1)
                if live(n):
                    for j in range(GT):
                        ins = nc.vector.bn_stats(stats[:, j, :], x(j))
                    ins.then_inc(dve, 1)
                    v.wait_ge(dve, DVE_STEPS * n + 1)
                    kit.passed(v)
                    for j in range(GT):
                        ins = nc.vector.bn_aggr(mv[:, j, :], stats[:, j, :])
                    ins.then_inc(dve, 1)
                    v.wait_ge(dve, DVE_STEPS * n + 2)
                    ts(var[:, :], mv[:, :, 1], LN_EPS, None, ALU.add).then_inc(var_ready, 1)
                if live(n - 1):
                    t = 1 - s
                    v.wait_ge(max_ready, n)
                    tt(xn[t][:, :, :], xn[t][:, :, :], wide(ascale[t]), ALU.mult).then_inc(xn_ready, 1)
                    v.wait_ge(xn_ready, n)
                    ts(xn[t][:, :, :], xn[t][:, :, :], ROUND, ROUND, ALU.add, ALU.subtract).then_inc(rounded, 1)
                if live(n):
                    v.wait_ge(rstd_ready, n + 1)
                    if after(n, 2):
                        v.wait_ge(xq_ready, n - 1)
                    for j in range(GT):
                        ins = ts(xn[s][:, j, :], x(j), mv[:, j, 0:1], rstd[:, j:j + 1], ALU.subtract, ALU.mult)
                    ins.then_inc(dve, 1)
                    v.wait_ge(dve, DVE_STEPS * n + 3)
                    nc.vector.tensor_reduce(amax[:, :], xn[s][:, :, :], AX.X, ALU.max, apply_absolute_value=True).then_inc(dve, 1)
                    v.wait_ge(dve, DVE_STEPS * n + 4)
                    ts(aback[s][:, :], amax[:, :], 1e-5, 1.0 / 127.0, ALU.max, ALU.mult).then_inc(dve, 1)
                    v.wait_ge(dve, DVE_STEPS * n + 5)
                    nc.vector.reciprocal(ascale[s][:, :], aback[s][:, :]).then_inc(max_ready, 1)
            run(v, step)

            at = 0

            def setup(ins):
                nonlocal at
                at += 1
                ins.then_inc(set_up, 1)
                v.wait_ge(set_up, at)

            v.wait_ge(weights, N_WEIGHTS)
            both = (w1[:, :], w2[:, :, :].rearrange("p k c -> p (k c)"))
            for n in range(2):
                setup(nc.vector.tensor_reduce(wsum[:, n:n + 1], both[n], AX.X, ALU.add, apply_absolute_value=True))
            setup(nc.vector.tensor_copy(identb[:, :], kit.ident[:, :]))
            v.wait_ge(w_ps, 1)
            setup(ts(wmean[:, :], p_w[:, 0:2], 1.0 / (C * FF), 1e-5, ALU.mult, ALU.max))
            setup(nc.vector.reciprocal(wscale[:, :], wmean[:, :]))

            def ternary(n):
                setup(ts(wq[:, :], both[n], wscale[:, n:n + 1], ROUND, ALU.mult, ALU.add))
                setup(ts(wq[:, :], wq[:, :], ROUND, None, ALU.subtract))
                setup(ts(wq[:, :], wq[:, :], -1.0, 1.0, ALU.max, ALU.min))

            ternary(1)
            setup(nc.vector.tensor_copy(w2q[:, :, :].rearrange("p k c -> p (k c)"), wq[:, :]))
            ternary(0)
            setup(ts(wq[:, :], wq[:, :], wmean[:, 0:1], None, ALU.mult))
            for k in range(TAPS):
                setup(tt(w1t[:, k, :], wq[:, :], taps[:, k, :], ALU.mult))

        @block.scalar
        def _(act):
            def step(n, s, live, after):
                if live(n - 1):
                    t = 1 - s
                    act.wait_ge(rounded, n)
                    if after(n - 1, 2):
                        act.wait_ge(xT_ps, n - 2)
                    for j in range(GT):
                        ins = nc.scalar.activation(xq[t][:, j, :], xn[t][:, j, :], ACT.Copy, scale=aback[t][:, j:j + 1])
                    ins.then_inc(xq_ready, 1)
                    act.wait_ge(xT_ps, n)
                    nc.scalar.activation(xT[:, bass.ds((n - 1) * GROUP, GROUP)], p_x[t][:, :], ACT.Copy).then_inc(xT_ready, 1)
            run(act, step)

        @block.tensor
        def _(pe):
            def step(n, s, live, after):
                if live(n - 1):
                    t = 1 - s
                    pe.wait_ge(xq_ready, n)
                    if after(n - 1, 2):
                        pe.wait_ge(xT_ready, n - 2)
                    for j in range(GT):
                        ins = nc.tensor.transpose(p_x[t][:, j * P:(j + 1) * P], xq[t][:, j, :], kit.ident[:, :])
                    ins.then_inc(xT_ps, 1)
            run(pe, step)
            pe.wait_ge(set_up, 2)
            nc.tensor.matmul(p_w[:, 0:2], kit.ones[:, :], wsum[:, :], start=True, stop=True).then_inc(w_ps, 1)


def quantised_products(kit, tag, xT, w1t, w2q, wmean, identb, conv_b, TAPS, ROUND):
    nc = kit.nc
    with ExitStack() as st:
        sb, ps, sem = scoped(nc, st, tag + "_m")
        xs = [sb(f"xs{i}", [C, TAPS, P]) for i in range(2)]
        h = [sb(f"h{i}", [P, FF]) for i in range(2)]
        hmax, hback, hscale = sb("hmax", [P, 2]), sb("hback", [P, 2]), sb("hscale", [P, 2])
        y_scale = sb("y_scale", [P, TILES])
        minus_round = sb("minus_round", [P, 1])
        hq, hT = sb("hq", [P, 2, FF], BF16), sb("hT", [P, 2, FF], BF16)
        p_h = [ps(f"p_h{i}", [P, FF]) for i in range(2)]
        p_t = [ps(f"p_t{i}", [P, 2 * FF], BF16) for i in range(2)]
        p_y = [ps(f"p_y{i}", [P, 512]) for i in range(2)]
        set_up, dve, max_ready = sem("set_up"), sem("dve"), sem("max_ready")
        xs_ready, h_ps, hb_ready, s_ready, scaled, hq_ready, hT_ps, hT_ready, y_ps, y_added = (
            sem(n) for n in "xs_ready h_ps hb_ready s_ready scaled hq_ready hT_ps hT_ready y_ps y_added".split())
        X = kit.X
        block = st.enter_context(nc.Block())

        def run(engine, step):
            pipelined(engine, (-3, TILES + 2), TILES, step, 4, TILES - 4)

        @block.gpsimd
        def _(pool):
            pool.wait_ge(set_up, 3)

            def shift(j, s, after):
                if after(j, 2):
                    pool.wait_ge(h_ps, j - 1)
                t3 = lambda t: t.rearrange("c (b s) -> c b s", s=S)
                src = t3(xT[:, bass.ds(j * P, P)])
                nc.gpsimd.tensor_copy(t3(xs[s][:, 1, :]), src)
                nc.gpsimd.tensor_copy(t3(xs[s][:, 0, :])[:, :, 1:S], src[:, :, 0:S - 1])
                nc.gpsimd.tensor_copy(t3(xs[s][:, 2, :])[:, :, 0:S - 1], src[:, :, 1:S]).then_inc(xs_ready, 1)

            def step(n, s, live, after):
                if live(n + 3):
                    shift(n + 3, 1 - s, after)
            run(pool, step)

        @block.vector
        def _(v):
            tt, ts, stt = nc.vector.tensor_tensor, nc.vector.tensor_scalar, nc.vector.scalar_tensor_tensor
            for i in range(2):
                nc.vector.memset(xs[i][:, :, :], 0.0).then_inc(set_up, 1)
            nc.vector.memset(minus_round[:, :], -ROUND).then_inc(set_up, 1)
            DVE_STEPS = 2

            def quantise(j, s, after):
                one = lambda t: t[:, s:s + 1]
                v.wait_ge(s_ready, j + 1)
                nc.vector.tensor_reduce(one(hmax), h[s][:, :], AX.X, ALU.max, apply_absolute_value=True).then_inc(max_ready, 1)
                v.wait_ge(max_ready, j + 1)
                ts(one(hback), one(hmax), 1e-5, 1.0 / 127.0, ALU.max, ALU.mult).then_inc(dve, 1)
                v.wait_ge(dve, DVE_STEPS * j + 1)
                nc.vector.reciprocal(one(hscale), one(hback)).then_inc(dve, 1)
                ts(y_scale[:, bass.ds(j, 1)], one(hback), wmean[:, 1:2], None, ALU.mult)
                v.wait_ge(dve, DVE_STEPS * j + 2)
                ts(h[s][:, :], h[s][:, :], one(hscale), ROUND, ALU.mult, ALU.add).then_inc(scaled, 1)

            def step(n, s, live, after):
                if live(n + 2):
                    j = n + 2
                    v.wait_ge(h_ps, j + 1)
                    if after(j, 2):
                        v.wait_ge(hq_ready, j - 1)
                    tt(h[s][:, :], p_h[s][:, :], conv_b[:, :], ALU.add).then_inc(hb_ready, 1)
                if live(n - 2):
                    j = n - 2
                    v.wait_ge(y_ps, j + 1)
                    v.wait_ge(scaled, j + 1)
                    x = X[:, bass.ds(j, 1), :].squeeze(1)
                    stt(x, p_y[s][:, 0:C], y_scale[:, bass.ds(j, 1)], x, ALU.mult, ALU.add).then_inc(y_added, 1)
                if live(n + 1):
                    quantise(n + 1, 1 - s, after)
            run(v, step)

        @block.scalar
        def _(act):
            act.wait_ge(set_up, 3)

            def step(n, s, live, after):
                if live(n + 2):
                    act.wait_ge(hb_ready, n + 3)
                    nc.scalar.activation(h[s][:, :], h[s][:, :], ACT.Silu).then_inc(s_ready, 1)
                if live(n):
                    act.wait_ge(hT_ps, n + 1)
                    if after(n, 2):
                        act.wait_ge(y_ps, n - 1)
                    nc.scalar.activation(hT[:, s, :], p_t[s][:, 0:FF], ACT.Copy).then_inc(hT_ready, 1)
                if live(n + 1):
                    act.wait_ge(scaled, n + 2)
                    if after(n + 1, 2):
                        act.wait_ge(hT_ps, n)
                    nc.scalar.activation(hq[:, 1 - s, :], h[1 - s][:, :], ACT.Identity, bias=minus_round[:, :]).then_inc(hq_ready, 1)
            run(act, step)

        @block.tensor
        def _(pe):
            def step(n, s, live, after):
                if live(n + 2):
                    j = n + 2
                    pe.wait_ge(xs_ready, j + 1)
                    if after(j, 2):
                        pe.wait_ge(hb_ready, j - 1)
                    for k in range(TAPS):
                        ins = nc.tensor.matmul(p_h[s][:, :], xs[s][:, k, :], w1t[:, k, :], start=(k == 0), stop=(k == TAPS - 1))
                    ins.then_inc(h_ps, 1)
                if live(n - 1):
                    j, t = n - 1, 1 - s
                    pe.wait_ge(hT_ready, j + 1)
                    if after(j, 2):
                        pe.wait_ge(y_added, j - 1)
                    for k in range(FK):
                        ins = nc.tensor.matmul(p_y[t][:, 0:C], hT[:, t, k * P:(k + 1) * P], w2q[:, k, :], start=(k == 0), stop=(k == FK - 1))
                    ins.then_inc(y_ps, 1)
                if live(n):
                    pe.wait_ge(hq_ready, n + 1)
                    if after(n, 2):
                        pe.wait_ge(hT_ready, n - 1)
                    for k in range(FK):
                        ins = nc.tensor.transpose(p_t[s][:, k * P:(k + 1) * P], hq[:, s, k * P:(k + 1) * P], identb[:, :])
                    ins.then_inc(hT_ps, 1)
            run(pe, step)


def clear_lists(kit):
    nc = kit.nc
    with ExitStack() as st:
        sb, _, sem = scoped(nc, st, "clear")
        zeros = sb("zeros", [P, SLOTS // P * C // 2])
        zeroed, cleared = sem("zeroed"), sem("cleared")
        block = st.enter_context(nc.Block())

        @block.vector
        def _(v):
            nc.vector.memset(zeros[:, :], 0.0).then_inc(zeroed, 1)

        @block.sync
        def _(sp):
            sp.wait_ge(zeroed, 1)
            half = SLOTS // 2
            for h in range(2):
                sp.dma_start(kit.packed[h * half:(h + 1) * half, :].rearrange("(p n) c -> p (n c)", p=P), zeros[:, :]).then_inc(cleared, 16)
            sp.wait_ge(cleared, 32)


def build(nc, A, out, phases=range(8)):
    with ExitStack() as ctx:
        kit = Kit(nc, A, ctx)
        load_x(kit)
        clear_lists(kit)
        steps = [lambda: mha(kit, "L0_xattn"), lambda: moe(kit, "L0_ffn"), lambda: attention(kit, "L1_xattn"),
                 lambda: moe(kit, "L1_ffn"), lambda: mlstm(kit, "L2_xattn"), lambda: moe(kit, "L2_ffn"), lambda: mha(kit, "L3_xattn"),
                 lambda: quantised_ffn(kit, "L3_ffn")]
        for n in phases:
            steps[n]()
        store_x(kit, out)


def arrays_for(inputs):
    a = {k: np.asarray(v) for k, v in inputs.items()}
    r = {}
    r["x"] = np.ascontiguousarray(a["x"].reshape(TOK, C))
    r["ctx"] = np.ascontiguousarray(a["ctx_1024"].reshape(TOK, C))
    r["ctxT"] = np.ascontiguousarray(a["ctx_1024"].reshape(TOK, C).T)
    r["ident"] = np.eye(P, dtype=np.float32)
    r["head_mask"] = (np.arange(P)[:, None] // 8 % 8 == np.arange(8)[None, :]).astype(np.float32)
    r["half_mask8"] = (np.arange(P)[:, None] // 64 == np.arange(C)[None, :] // 8 % 2).astype(np.float32)
    r["earlier"] = np.triu(np.ones((P, P), np.float32), 1)
    r["ones"] = np.ones((P, P), np.float32)
    r["iota"] = np.arange(128, dtype=np.float32)[None, :]

    def up(w):
        return np.ascontiguousarray(w.transpose(1, 0, 2))

    def down(w):
        return np.ascontiguousarray(w.reshape(w.shape[0], FK, P, C).transpose(2, 0, 1, 3))

    r["L0_ffn_w1"] = up(a["L0_ffn_expert_w1"].transpose(0, 2, 1))
    r["L0_ffn_w2"] = down(a["L0_ffn_expert_w2"].transpose(0, 2, 1))
    bias = lambda b: np.ascontiguousarray(b.reshape(-1, FK, P).transpose(2, 0, 1))
    r["L0_ffn_b1"], r["L0_ffn_b2"] = bias(a["L0_ffn_expert_b1"]), a["L0_ffn_expert_b2"]
    r["L1_ffn_w1"], r["L1_ffn_w2"] = up(a["L1_ffn_w1"]), down(a["L1_ffn_w2"])
    r["L1_ffn_b1"], r["L1_ffn_b2"] = bias(a["L1_ffn_b1"]), a["L1_ffn_b2"]
    with_fallback = lambda n: np.concatenate([a[f"L2_ffn_{n}"], a[f"L2_ffn_f{n.lower()}"][None]])
    r["L2_ffn_w1"], r["L2_ffn_w2"] = up(with_fallback("W1")), down(with_fallback("W2"))
    r["L2_ffn_b1"], r["L2_ffn_b2"] = bias(with_fallback("b1")), with_fallback("b2")
    r["L0_ffn_router_w"] = np.ascontiguousarray(a["L0_ffn_router_w"].T)
    r["L1_ffn_router_w"] = np.ascontiguousarray(a["L1_ffn_router_w"].T)
    r["L2_ffn_router_w"] = np.ascontiguousarray(a["L2_ffn_Wr"].T)
    r["L1_ffn_router_b"] = a["L1_ffn_router_b"]
    r["L0_ffn_router_b"] = r["L2_ffn_router_b"] = np.zeros(8, np.float32)
    r["fold"] = np.tile(np.eye(S, dtype=np.float32), (2, 1))
    for n in ("q", "k", "v", "o"):
        for layer in ("L0", "L1", "L3"):
            w = a[f"{layer}_xattn_W{n}"]
            r[f"{layer}_xattn_W{n}"] = w if layer == "L3" else np.ascontiguousarray(w.T)
            r[f"{layer}_xattn_b{n}"] = a[f"{layer}_xattn_b{n}"]
    gate_w = np.zeros((C, 3, P), np.float32)
    gate_w[:, :, 0:8] = a["L2_xattn_igate_w"].reshape(8, 3, C).transpose(2, 1, 0)
    gate_w[:, :, 32:40] = a["L2_xattn_fgate_w"].reshape(8, 3, C).transpose(2, 1, 0)
    r["L2_xattn_gate_w"] = gate_w
    r["L2_xattn_igate_b"], r["L2_xattn_fgate_b"], r["L2_xattn_out_w"] = (
        a[f"L2_xattn_{n}"] for n in ("igate_b", "fgate_b", "out_w"))
    heads = np.arange(8)
    r["head_mask16"] = (np.arange(P)[:, None] // 16 % 4 == np.arange(4)[None, :]).astype(np.float32)
    r["half_mask16"] = (np.arange(P)[:, None] // 64 == np.arange(C)[None, :] // 16 % 2).astype(np.float32)
    r["head_of_half"] = (heads[:, None] % 4 == np.arange(4)[None, :]).astype(np.float32)
    r["half_of_head"] = (heads[:, None] // 4 == np.arange(2)[None, :]).astype(np.float32)
    r["minus_half_of_head"] = -r["half_of_head"]
    r["later"] = np.where(np.arange(S)[:, None] < np.arange(S)[None, :], np.float32(-2.0 ** 100), np.float32(0))
    r["L3_ffn_w1"] = np.ascontiguousarray(a["L3_ffn_w1"].T)
    r["L3_ffn_w2"] = np.ascontiguousarray(a["L3_ffn_w2"].T.reshape(FK, P, C).transpose(1, 0, 2))
    r["L3_ffn_conv_w"] = np.ascontiguousarray(a["L3_ffn_conv_w"][:, 0, :].T)
    r["L3_ffn_conv_b"] = a["L3_ffn_conv_b"]
    return r


def kernel(**inputs):
    import concourse.bacc as bacc
    from concourse.bass_utils import run_bass_kernel_spmd

    nc = bacc.Bacc("TRN2", target_bir_lowering=False, num_devices=1)
    arrays, A = {}, {}
    for name, a in arrays_for(inputs).items():
        arrays[f"in_{name}_dram"] = a
        A[name] = nc.dram_tensor(f"in_{name}_dram", a.shape, mybir.dt.from_np(a.dtype), kind="ExternalInput").ap()
    out = nc.dram_tensor("out_0_dram", (TOK, C), FP32, kind="ExternalOutput").ap()
    build(nc, A, out)
    result = run_bass_kernel_spmd(nc, [arrays], core_ids=[0])
    return result.results[0]["out_0_dram"].reshape(B, S, C)
```

```python
import numpy as np
from contextlib import ExitStack
import concourse.bass as bass
from concourse import mybir

FP32 = mybir.dt.float32
BF16 = mybir.dt.bfloat16
I32 = mybir.dt.int32
U32 = mybir.dt.uint32
ALU = mybir.AluOpType
ACT = mybir.ActivationFunctionType
AX = mybir.AxisListType

B, S, C = 64, 64, 128
TOK = B * S
P = 128
TILES = TOK // P
GT = 4
GROUP = GT * P
NG = TILES // GT
PAIRS = GT
LN_EPS = 1e-5
FF = 512
FK = FF // P
TOP_K = 2


class Chain:

    def __init__(self, engine, sem):
        self.engine, self.sem, self.n = engine, sem, 0

    def done(self, instruction):
        self.n += 1
        instruction.then_inc(self.sem, 1)

    def sync(self):
        self.engine.wait_ge(self.sem, self.n)

    def step(self, instruction):
        self.done(instruction)
        self.sync()


class Kit:

    def __init__(self, nc, A, ctx):
        self.nc, self.A = nc, A
        sb = lambda name, shape, dt=FP32: ctx.enter_context(nc.sbuf_tensor(name, shape, dt))
        self.X = sb("residual", [P, TILES, C])
        self.token = sb("token", [P, TILES])
        self.experts_in = ctx.enter_context(nc.semaphore("experts_in"))
        self.experts_loaded = 0
        self.normed = nc.dram_tensor("normed_rows", (TOK, C), FP32, kind="Internal").ap()
        self.expert_out = nc.dram_tensor("expert_rows", (max(m.tiles for m in MOES.values()) * P, C), FP32, kind="Internal").ap()
        self.marks = ctx.enter_context(nc.semaphore("marks"))
        self.minus_half = sb("minus_half", [P, GT])
        self.ident = sb("identity", [P, P])
        self.ones = sb("ones", [P, P])
        self.not_earlier = sb("not_earlier", [P, P])
        self.iota = sb("iota", [P, P])
        self.gate = sb("gate", [P, TOP_K, TILES])
        self.slot_back = sb("slot_back", [P, TILES, TOP_K], I32)

    def passed(self, engine):
        engine.sem_inc(self.marks, 1)


def scoped(nc, stack, tag):
    sb = lambda name, shape, dt=FP32: stack.enter_context(nc.sbuf_tensor(f"{tag}_{name}", shape, dt))
    ps = lambda name, shape, dt=FP32: stack.enter_context(nc.psum_tensor(f"{tag}_{name}", shape, dt))
    taken = []

    def clear():
        if taken:
            nc.clear_and_free_semaphores(taken)
            nc.all_engine_barrier()

    stack.callback(clear)

    def sem(name):
        taken.append(nc.alloc_semaphore(name=f"{tag}_{name}"))
        return taken[-1]
    return sb, ps, sem



def inverse_root(nc, pool, var, var_ready, rstd, rstd_ready, minus_half, turn):
    pool.wait_ge(var_ready, turn + 1)
    nc.gpsimd.tensor_tensor(rstd[:, :], var[:, :], minus_half[:, :], ALU.pow).then_inc(rstd_ready, 1)


def load_x(kit):
    nc, A = kit.nc, kit.A
    with ExitStack() as st:
        _, _, sem = scoped(nc, st, "load")
        loaded = sem("loaded")
        block = st.enter_context(nc.Block())

        @block.vector
        def _(v):
            nc.vector.memset(kit.minus_half[:, :], -0.5)

        @block.sync
        def _(sp):
            sp.dma_start(kit.X[:, :, :], A["x"].rearrange("(t p) c -> p t c", p=P)).then_inc(loaded, 16)
            sp.dma_start(kit.ident[:, :], A["ident"]).then_inc(loaded, 16)
            sp.dma_start(kit.not_earlier[:, :], A["not_earlier"]).then_inc(loaded, 16)
            sp.dma_start(kit.ones[:, :], A["ones"]).then_inc(loaded, 16)
            sp.dma_start(kit.iota[:, :], A["iota"].to_broadcast([P, P])).then_inc(loaded, 16)
            sp.dma_start(kit.token[:, :], A["token"]).then_inc(loaded, 16)
            sp.wait_ge(loaded, 96)


def pipelined(engine, steps, count, step, loop_from, loop_to):
    assert (loop_to - loop_from) % 2 == 0

    def plain(a, b):
        for n in range(a, b):
            step(n, n % 2, lambda i: 0 <= i < count, lambda i, k: i >= k)
    plain(steps[0], loop_from)
    with engine.Fori(0, (loop_to - loop_from) // 2) as m:
        for u in range(2):
            step(m * 2 + (loop_from + u), (loop_from + u) % 2, lambda i: True, lambda i, k: True)
    plain(loop_to, steps[1])


def mha(kit, tag, experts=None):
    nc = kit.nc
    H, DH = 16, C // 16
    HH = H // 2
    VW = 2 * 2 * DH + 2
    with ExitStack() as st:
        sb, _, _ = scoped(nc, st, tag)
        QT, KT = sb("QT", [C, TOK]), sb("KT", [C, TOK])
        V2 = sb("V2", [P, TILES, 2 * HH // 2, VW])
        mha_project(kit, tag, experts, QT, KT, V2, DH, VW)
        mha_attend(kit, tag, QT, KT, V2, H, DH, HH, VW)


def mha_project(kit, tag, experts, QT, KT, V2, DH, VW):
    nc, A = kit.nc, kit.A
    NB = GROUP // S
    with ExitStack() as st:
        sb, ps, sem = scoped(nc, st, tag + "_p")
        w = {n: sb(n, [C, C]) for n in ("Wq", "Wk", "Wv")}
        bias = {n: sb(n, [C, 1]) for n in ("bq", "bk")}
        bo = sb("bo", [P, C])
        half_mask = sb("half_mask", [P, C])
        cT = [sb(f"cT{i}", [C, NB, 2, S]) for i in range(2)]
        stats, mv, var, rstd = sb("stats", [P, GT, 6]), sb("mv", [P, GT, 2]), sb("var", [P, GT]), sb("rstd", [P, GT])
        xn, xnT = [sb(f"xn{i}", [P, GT, C]) for i in range(2)], [sb(f"xnT{i}", [C, GROUP]) for i in range(2)]
        p_x, p_k, p_q = ps("p_x", [P, 512]), ps("p_k", [P, 512]), ps("p_q", [P, 512])
        p_v = [ps(f"p_v{i}", [P, 512]) for i in range(2)]
        wkv_in, rest_in = sem("wkv_in"), sem("rest_in")
        ctx_in = [sem(f"ctx_in{i}") for i in range(2)]
        var_ready, rstd_ready, xn_ready, xT_ps, xnT_ready, q_ps, k_ps, v_ps, qT_ready, kT_ready, v_ready, dve, ones_set, bo_added = (
            sem(n) for n in "var_ready rstd_ready xn_ready xT_ps xnT_ready q_ps k_ps v_ps qT_ready kT_ready v_ready dve ones_set bo_added".split())
        X = kit.X
        results = Results(kit, experts, sb, sem) if experts else None
        block = st.enter_context(nc.Block())
        span = (-1, NG + 1)

        def add_bo(engine, n):
            xg = X[:, bass.ds(n * GT, GT), :]
            engine.tensor_tensor(xg, xg, bo[:, :].unsqueeze(1).to_broadcast([P, GT, C]), ALU.add).then_inc(bo_added, 1)

        def run(engine, step):
            pipelined(engine, span, NG, step, 2, NG - 2)

        @block.sync
        def _(sp):
            for n in ("Wk", "Wv"):
                sp.dma_start(w[n][:, :], A[f"{tag}_{n}"]).then_inc(wkv_in, 16)

            def step(n, s, live, after):
                if live(n + 1):
                    if after(n + 1, 2):
                        sp.wait_ge(v_ps, 2 * n)
                    for twice in range(2):
                        sp.dma_start(cT[1 - s][:, :, twice, :], A["ctxT"][:, bass.ds((n + 1) * GROUP, GROUP)].rearrange(
                            "c (b s) -> c b s", s=S)).then_inc(ctx_in[1 - s], 16)
            run(sp, step)

        @block.gpsimd
        def _(pool):
            if results:
                for g in range(2):
                    results.fetch(pool, g, g, lambda i, k: i >= k)
            pool.wait_ge(rest_in, 16 * 5)

            def step(n, s, live, after):
                if live(n):
                    inverse_root(nc, pool, var, var_ready, rstd, rstd_ready, kit.minus_half, n)
                if results and live(n) and live(n + 2):
                    results.fetch(pool, n + 2, s, after)
                if live(n - 1) and not results:
                    pool.wait_ge(xn_ready, n)
                    add_bo(nc.gpsimd, n - 1)
            run(pool, step)

        @block.scalar
        def _(act):
            act.dma_start(half_mask[:, :], A["half_mask8"]).then_inc(rest_in, 16)
            for n in bias:
                act.dma_start(bias[n][:, :], A[f"{tag}_{n}"].rearrange("(c a) -> c a", a=1)).then_inc(rest_in, 16)
            act.dma_start(w["Wq"][:, :], A[f"{tag}_Wq"]).then_inc(rest_in, 16)
            act.dma_start(bo[:, :], A[f"{tag}_bo"].rearrange("(a c) -> a c", a=1).to_broadcast([P, C])).then_inc(rest_in, 16)
            act.wait_ge(rest_in, 16 * 5)

            def step(n, s, live, after):
                if live(n + 1):
                    act.wait_ge(k_ps, n + 2)
                    nc.scalar.activation(KT[:, bass.ds((n + 1) * GROUP, GROUP)], p_k[:, :], ACT.Identity, bias=bias["bk"][:, :]).then_inc(kT_ready, 1)
                if live(n - 1):
                    act.wait_ge(q_ps, n)
                    nc.scalar.activation(QT[:, bass.ds((n - 1) * GROUP, GROUP)], p_q[:, :], ACT.Identity, bias=bias["bq"][:, :]).then_inc(qT_ready, 1)
                if live(n):
                    act.wait_ge(xT_ps, n + 1)
                    nc.scalar.activation(xnT[s][:, :], p_x[:, :], ACT.Copy).then_inc(xnT_ready, 1)
            run(act, step)

        @block.vector
        def _(v):
            if results:
                results.stage(0, 0)
                results.stage(1, 1)
            nc.vector.memset(V2[:, :, :, 4 * DH:VW], 0.0).then_inc(ones_set, 1)
            v.wait_ge(ones_set, 1)
            nc.vector.memset(V2[0:S, :, :, 4 * DH:4 * DH + 1], 1.0).then_inc(ones_set, 1)
            nc.vector.memset(V2[S:P, :, :, 4 * DH + 1:VW], 1.0).then_inc(ones_set, 1)
            v.wait_ge(rest_in, 16 * 5)
            hm = half_mask[:, :].rearrange("p (f i c) -> p i f c", f=2, c=2 * DH)

            def values(g):
                for half in range(2):
                    v.wait_ge(v_ps, 2 * g + half + 1)
                    for b in range(4):
                        vin = p_v[half][:, C * b:C * b + C].rearrange("p (f i c) -> p i f c", f=2, c=2 * DH)
                        vout = V2[:, bass.ds(g * GT + 2 * half + b // 2, 1), 4 * (b % 2):4 * (b % 2) + 4, 0:4 * DH].squeeze(1)
                        ins = nc.vector.tensor_tensor(vout.rearrange("p i (f c) -> p i f c", f=2), vin, hm, ALU.mult)
                    ins.then_inc(v_ready, 1)


            def step(n, s, live, after):
                x = lambda j: X[:, bass.ds(n * GT + j, 1), :].squeeze(1)
                if live(n):
                    if results:
                        results.add(v, n, s, live)
                    for j in range(GT):
                        ins = nc.vector.bn_stats(stats[:, j, :], x(j))
                    ins.then_inc(dve, 1)
                    v.wait_ge(dve, 2 * n + 1)
                    kit.passed(v)
                    for j in range(GT):
                        ins = nc.vector.bn_aggr(mv[:, j, :], stats[:, j, :])
                    ins.then_inc(dve, 1)
                    v.wait_ge(dve, 2 * n + 2)
                    nc.vector.tensor_scalar(var[:, :], mv[:, :, 1], LN_EPS, None, ALU.add).then_inc(var_ready, 1)
                if live(n + 1):
                    values(n + 1)
                if live(n):
                    v.wait_ge(rstd_ready, n + 1)
                    if after(n, 2):
                        v.wait_ge(xT_ps, n - 1)
                    for j in range(GT):
                        ins = nc.vector.tensor_scalar(xn[s][:, j, :], x(j), mv[:, j, 0:1], rstd[:, j:j + 1], ALU.subtract, ALU.mult)
                    ins.then_inc(xn_ready, 1)
                    if results:
                        v.wait_ge(xn_ready, n + 1)
                        add_bo(nc.vector, n)
            run(v, step)

        @block.tensor
        def _(pe):
            pe.wait_ge(wkv_in, 32)

            def step(n, s, live, after):
                if live(n + 1):
                    pe.wait_ge(ctx_in[1 - s], 16 * (n + 1 - (1 - s)) + 32)
                    if after(n + 1, 1):
                        pe.wait_ge(kT_ready, n + 1)
                    nc.tensor.matmul(p_k[:, :], w["Wk"][:, :], cT[1 - s][:, :, 0, :], start=True, stop=True).then_inc(k_ps, 1)
                    for half in range(2):
                        if after(n + 1, 1):
                            pe.wait_ge(v_ready, 2 * n + half + 1)
                        for b in range(4):
                            ins = nc.tensor.matmul(p_v[half][:, b * C:(b + 1) * C], cT[1 - s][:, half * 4 + b], w["Wv"][:, :],
                                                   start=True, stop=True)
                        ins.then_inc(v_ps, 1)
                if live(n - 1):
                    if not after(n - 1, 1):
                        pe.wait_ge(rest_in, 16 * 5)
                    pe.wait_ge(xnT_ready, n)
                    if after(n - 1, 1):
                        pe.wait_ge(qT_ready, n - 1)
                    nc.tensor.matmul(p_q[:, :], w["Wq"][:, :], xnT[1 - s][:, :], start=True, stop=True).then_inc(q_ps, 1)
                if live(n):
                    pe.wait_ge(xn_ready, n + 1)
                    if after(n, 1):
                        pe.wait_ge(xnT_ready, n)
                    for j in range(GT):
                        ins = nc.tensor.transpose(p_x[:, j * P:(j + 1) * P], xn[s][:, j, :], kit.ident[:, :])
                    ins.then_inc(xT_ps, 1)
            run(pe, step)


def mha_attend(kit, tag, QT, KT, V2, H, DH, HH, VW):
    nc, A = kit.nc, kit.A
    SCALE = DH ** -0.5
    with ExitStack() as st:
        sb, ps, sem = scoped(nc, st, tag + "_a")
        Wo, bv = sb("Wo", [C, C]), sb("bv", [C, 1])
        head_mask, fold = sb("head_mask", [P, HH]), sb("fold", [P, S])
        Qz = [sb(f"Qz{i}", [C, 2, 2, S]) for i in range(2)]
        Km = [sb(f"Km{i}", [C, 2, HH, S]) for i in range(2)]
        Pm = [sb(f"Pm{i}", [P, H * S]) for i in range(2)]
        mx, rs = sb("mx", [P, 2, H]), sb("rs", [P, 2, H])
        PT = sb("PT", [P, H * S])
        O = [sb(f"O{i}", [P, 2, 2, C // 2]) for i in range(2)]
        OT = sb("OT", [C, P])
        p_s = [ps(f"p_s{i}", [P, H * S]) for i in range(2)]
        p_t = [ps(f"p_t{i}", [P, H * S // 2]) for i in range(2)]
        p_o, p_y = ps("p_o", [P, 512]), ps("p_y", [P, 512])
        consts_in, zeros_set = sem("consts_in"), sem("zeros_set")
        qz_ready, km_ready, s_ps, mx_ready, d_ready, p_ready, t_ps, pT_ready, o_ps, rs_ready, o_ready, oT_ps, oT_ready, y_ps, y_added = (
            sem(n) for n in "qz_ready km_ready s_ps mx_ready d_ready p_ready t_ps pT_ready o_ps rs_ready o_ready oT_ps oT_ready y_ps y_added".split())
        X = kit.X
        block = st.enter_context(nc.Block())
        pair = lambda j: bass.ds(j * P, P)

        def run(engine, step):
            pipelined(engine, (-3, TILES + 3), TILES, step, 6, TILES - 4)

        @block.sync
        def _(sp):
            for dst, src in ((head_mask[:, :], A["head_mask"]), (fold[:, :], A["fold"]), (Wo[:, :], A[f"{tag}_Wo"]),
                             (bv[:, :], A[f"{tag}_bv"].rearrange("(c a) -> c a", a=1))):
                sp.dma_start(dst, src).then_inc(consts_in, 16)
            sp.wait_ge(consts_in, 64)

        @block.gpsimd
        def _(pool):
            pool.wait_ge(consts_in, 64)

            def keys(j, s, after):
                if after(j, 2):
                    pool.wait_ge(s_ps, j - 1)
                kt = KT[:, pair(j)].rearrange("c (b s) -> c b s", s=S)
                for b in range(2):
                    ins = nc.gpsimd.tensor_tensor(Km[s][:, b], kt[:, b].unsqueeze(1).to_broadcast([P, HH, S]),
                                                  head_mask[:, :].unsqueeze(2).to_broadcast([P, HH, S]), ALU.mult)
                ins.then_inc(km_ready, 1)

            def step(n, s, live, after):
                if live(n + 3):
                    keys(n + 3, 1 - s, after)
            run(pool, step)

        @block.scalar
        def _(act):
            act.wait_ge(zeros_set, 4)
            act.wait_ge(consts_in, 64)

            def queries(j, s, after):
                if after(j, 2):
                    act.wait_ge(s_ps, j - 1)
                for h in range(2):
                    rows = slice(64 * h, 64 * h + 64)
                    ins = nc.scalar.activation(Qz[s][rows, :, h, :], QT[rows, pair(j)].rearrange("c (b s) -> c b s", s=S), ACT.Copy)
                ins.then_inc(qz_ready, 1)

            def step(n, s, live, after):
                if live(n + 1):
                    act.wait_ge(d_ready, n + 2)
                    nc.scalar.activation(Pm[1 - s][:, :], Pm[1 - s][:, :], ACT.Exp, scale=SCALE).then_inc(p_ready, 1)
                if live(n):
                    if after(n, 1):
                        act.wait_ge(o_ps, n)
                    for h in range(2):
                        act.wait_ge(t_ps, 2 * n + h + 1)
                        nc.scalar.activation(PT[:, h * 512:(h + 1) * 512], p_t[h][:, :], ACT.Copy).then_inc(pT_ready, 1)
                if live(n - 2):
                    act.wait_ge(oT_ps, n - 1)
                    nc.scalar.activation(OT[:, :], p_y[:, 0:P], ACT.Identity, bias=bv[:, :]).then_inc(oT_ready, 1)
                if live(n + 3):
                    queries(n + 3, 1 - s, after)
            run(act, step)

        @block.vector
        def _(v):
            for i in range(2):
                nc.vector.memset(Qz[i][:, :, :, :], 0.0).then_inc(zeros_set, 1)
                nc.vector.memset(O[i][:, :, :, :], 0.0).then_inc(zeros_set, 1)
            v.wait_ge(zeros_set, 4)

            def subtract_max(j, s, after):
                v.wait_ge(s_ps, j + 1)
                s3 = p_s[s][:, :].rearrange("p (h k) -> p h k", k=S)
                nc.vector.tensor_reduce(mx[:, s, :], s3, AX.X, ALU.max).then_inc(mx_ready, 1)
                v.wait_ge(mx_ready, j + 1)
                if after(j, 2):
                    v.wait_ge(t_ps, 2 * j - 2)
                nc.vector.tensor_tensor(Pm[s][:, :].rearrange("p (h k) -> p h k", k=S), s3,
                                        mx[:, s, :].unsqueeze(2).to_broadcast([P, H, S]), ALU.subtract).then_inc(d_ready, 1)

            def normalise(j, s, after):
                v.wait_ge(o_ps, j + 1)
                po = p_o[:, 0:H // 2 * VW].rearrange("p (h c) -> p h c", c=VW)
                r = rs[:, s, :]
                nc.vector.reciprocal(r.rearrange("p (h c) -> p h c", c=2), po[:, :, 4 * DH:VW]).then_inc(rs_ready, 1)
                v.wait_ge(rs_ready, j + 1)
                if after(j, 2):
                    v.wait_ge(oT_ps, j - 1)
                for f in range(2):
                    q = slice(f * S, (f + 1) * S)
                    ins = nc.vector.tensor_tensor(
                        O[s][q, :, f, :].rearrange("p b (i a c) -> p b i a c", a=2, c=DH),
                        po[q, :, f * 2 * DH:(f + 1) * 2 * DH].rearrange("p (b i) (a c) -> p b i a c", b=2, c=DH),
                        r[q].rearrange("p (b i a) -> p b i a", b=2, a=2).unsqueeze(4).to_broadcast([S, 2, HH // 2, 2, DH]),
                        ALU.mult)
                ins.then_inc(o_ready, 1)

            def step(n, s, live, after):
                if live(n + 1):
                    subtract_max(n + 1, 1 - s, after)
                if live(n - 3):
                    v.wait_ge(y_ps, n - 2)
                    x = X[:, bass.ds(n - 3, 1), :].squeeze(1)
                    nc.vector.tensor_tensor(x, x, p_y[:, P:P + C], ALU.add).then_inc(y_added, 1)
                if live(n - 1):
                    normalise(n - 1, 1 - s, after)
            run(v, step)

        @block.tensor
        def _(pe):
            pe.wait_ge(consts_in, 64)
            pe.wait_ge(zeros_set, 4)

            def step(n, s, live, after):
                if live(n + 1):
                    j, t = n + 1, 1 - s
                    pe.wait_ge(qz_ready, j + 1)
                    pe.wait_ge(km_ready, j + 1)
                    if after(j, 2):
                        pe.wait_ge(d_ready, j - 1)
                    for b in range(2):
                        ins = nc.tensor.matmul(p_s[t][:, b * 512:(b + 1) * 512], Qz[t][:, b], Km[t][:, b], start=True, stop=True)
                    ins.then_inc(s_ps, 1)
                if live(n - 3):
                    pe.wait_ge(oT_ready, n - 2)
                    nc.tensor.matmul(p_y[:, P:P + C], OT[:, :], Wo[:, :], start=True, stop=True).then_inc(y_ps, 1)
                if live(n - 1):
                    j = n - 1
                    if after(j, 1):
                        pe.wait_ge(o_ready, j)
                    for h in range(2):
                        pe.wait_ge(pT_ready, 2 * j + h + 1)
                        for i in range(4 * h, 4 * h + 4):
                            ins = nc.tensor.matmul(p_o[:, i * VW:(i + 1) * VW], PT[:, i * P:(i + 1) * P],
                                                   V2[:, bass.ds(j, 1), i, :].squeeze(1), start=True, stop=True)
                    ins.then_inc(o_ps, 1)
                if live(n):
                    pe.wait_ge(p_ready, n + 1)
                    for h in range(2):
                        if after(n, 1):
                            pe.wait_ge(pT_ready, 2 * n - 1 + h)
                        for i in range(4):
                            ins = nc.tensor.transpose(p_t[h][:, i * P:(i + 1) * P], Pm[s][:, (4 * h + i) * P:(4 * h + i + 1) * P],
                                                      kit.ident[:, :])
                        ins.then_inc(t_ps, 1)
                if live(n - 2):
                    j = n - 2
                    pe.wait_ge(o_ready, j + 1)
                    if after(j, 1):
                        pe.wait_ge(y_added, j)
                    for b in range(2):
                        ins = nc.tensor.matmul(p_y[:, b * S:(b + 1) * S], O[s][:, b, :, :], fold[:, :], start=True, stop=True)
                    ins.then_inc(oT_ps, 1)
            run(pe, step)


class Moe:

    def __init__(self, routed, cap, fallback, gates):
        self.routed, self.cap, self.fallback, self.gates = routed, cap, fallback, gates
        self.experts = routed + fallback
        most = TOK * TOP_K // P + self.experts - 1
        self.tiles = most + most % 2


MOES = {
    "L0_ffn": Moe(8, None, 0, "probs_sum"),
    "L1_ffn": Moe(16, -(-5 * TOK * TOP_K // (4 * 16)), 0, "kept_softmax"),
    "L2_ffn": Moe(8, int(1.25 * (TOK * TOP_K / 8)), 1, "probs_clip"),
}


def load_experts(kit, sp, tag):
    A, E = kit.A, MOES[tag].experts
    sp.dma_start(kit.W1[:, 0:E, :], A[f"{tag}_w1"]).then_inc(kit.experts_in, 16)
    sp.dma_start(kit.W2[:, 0:E, :, :], A[f"{tag}_w2"]).then_inc(kit.experts_in, 16)
    sp.dma_start(kit.B1[:, 0:E, :], A[f"{tag}_b1"]).then_inc(kit.experts_in, 16)
    sp.dma_start(kit.B2[:, 0:E, :], A[f"{tag}_b2"].unsqueeze(0).to_broadcast([P, E, C])).then_inc(kit.experts_in, 16)
    kit.experts_loaded += 64


def moe(kit, tag):
    nc = kit.nc
    with ExitStack() as st:
        sb, _, _ = scoped(nc, st, tag)
        E = MOES[tag].experts
        kit.W1, kit.W2 = sb("w1", [C, E, FF]), sb("w2", [P, E, FK, C])
        kit.B1, kit.B2 = sb("b1", [P, E, FK]), sb("b2", [P, E, C])
        r = Route()
        r.values = sb("values", [P, TILES, TOP_K])
        r.chosen = sb("chosen", [P, TILES, TOP_K])
        r.logits = sb("logits", [P, TILES, MOES[tag].routed])
        r.slot_tile = sb("slot_tile", [P, TILES, TOP_K])
        r.slot_row = sb("slot_row", [P, TILES, TOP_K])
        r.row_token = sb("row_token", [P, MOES[tag].tiles], I32)
        r.tile_expert = sb("tile_expert", [1, MOES[tag].tiles], I32)
        router(kit, tag, r)
        plan(kit, tag, r)
        list_tokens(kit, tag, r)
        run_experts(kit, tag, r)


class Route:
    pass


def router(kit, tag, r):
    nc, A, m = kit.nc, kit.A, MOES[tag]
    E = m.routed
    with ExitStack() as st:
        sb, ps, sem = scoped(nc, st, tag + "_r")
        wr = sb("wr", [C, E])
        br = sb("br", [P, E])
        stats, mv, var, rstd = sb("stats", [P, GT, 6]), sb("mv", [P, GT, 2]), sb("var", [P, GT]), sb("rstd", [P, GT])
        xn, xnT = [sb(f"xn{i}", [P, GT, C]) for i in range(2)], [sb(f"xnT{i}", [C, GROUP]) for i in range(2)]
        lg = sb("lg", [P, GT, E])
        top, top_i = sb("top", [P, GT, 8]), sb("top_i", [P, GT, 8], U32)
        p_x, p_l = [ps(f"p_x{i}", [P, GROUP]) for i in range(2)], [ps(f"p_l{i}", [P, 512]) for i in range(2)]
        weights, var_ready, rstd_ready, xn_ready = sem("weights"), sem("var_ready"), sem("rstd_ready"), sem("xn_ready")
        xT_ps, xnT_ready, logits_ps, lg_read, topped, dve = (
            sem(n) for n in ("xT_ps", "xnT_ready", "logits_ps", "lg_read", "topped", "dve"))
        kept = [sem(f"kept{i}") for i in range(2)]
        N_WEIGHTS = 32
        X = kit.X
        block = st.enter_context(nc.Block())

        def run(engine, step):
            pipelined(engine, (0, NG + 2), NG, step, 4, NG)

        @block.sync
        def _(sp):
            sp.dma_start(wr[:, :], A[f"{tag}_router_w"]).then_inc(weights, 16)
            sp.dma_start(br[:, :], A[f"{tag}_router_b"].rearrange("(a c) -> a c", a=1).to_broadcast([P, E])).then_inc(weights, 16)
            load_experts(kit, sp, tag)

            def step(n, s, live, after):
                if live(n):
                    sp.wait_ge(xn_ready, n + 1)
                    sp.dma_start(kit.normed[bass.ds(n * GROUP, GROUP), :].rearrange("(t p) c -> p t c", p=P), xn[s][:, :, :]).then_inc(kept[s], 16)
            run(sp, step)
            for s in range(2):
                sp.wait_ge(kept[s], 8 * NG)

        @block.gpsimd
        def _(pool):
            def step(n, s, live, after):
                if live(n):
                    inverse_root(nc, pool, var, var_ready, rstd, rstd_ready, kit.minus_half, n)
            run(pool, step)

        @block.tensor
        def _(pe):
            pe.wait_ge(weights, N_WEIGHTS)

            def step(n, s, live, after):
                if live(n - 1):
                    t = 1 - s
                    pe.wait_ge(xnT_ready, n)
                    if after(n - 1, 2):
                        pe.wait_ge(lg_read, n - 2)
                    for j in range(GT):
                        ins = nc.tensor.matmul(p_l[t][:, j * E:(j + 1) * E], xnT[t][:, j * P:(j + 1) * P], wr[:, :], start=True, stop=True)
                    ins.then_inc(logits_ps, 1)
                if live(n):
                    pe.wait_ge(xn_ready, n + 1)
                    if after(n, 2):
                        pe.wait_ge(xnT_ready, n - 1)
                    for j in range(GT):
                        ins = nc.tensor.transpose(p_x[s][:, j * P:(j + 1) * P], xn[s][:, j, :], kit.ident[:, :])
                    ins.then_inc(xT_ps, 1)
            run(pe, step)

        @block.scalar
        def _(act):
            def step(n, s, live, after):
                if live(n):
                    act.wait_ge(xT_ps, n + 1)
                    if after(n, 2):
                        act.wait_ge(logits_ps, n - 1)
                    nc.scalar.activation(xnT[s][:, :], p_x[s][:, :], ACT.Copy).then_inc(xnT_ready, 1)
            run(act, step)

        @block.vector
        def _(v):
            v.wait_ge(weights, N_WEIGHTS)
            LN = 2

            def step(n, s, live, after):
                x = lambda j: X[:, bass.ds(n * GT + j, 1), :].squeeze(1)
                if live(n):
                    for j in range(GT):
                        ins = nc.vector.bn_stats(stats[:, j, :], x(j))
                    ins.then_inc(dve, 1)
                    v.wait_ge(dve, LN * n + 1)
                    kit.passed(v)
                    for j in range(GT):
                        ins = nc.vector.bn_aggr(mv[:, j, :], stats[:, j, :])
                    ins.then_inc(dve, 1)
                    v.wait_ge(dve, LN * n + 2)
                    nc.vector.tensor_scalar(var[:, :], mv[:, :, 1], LN_EPS, None, ALU.add).then_inc(var_ready, 1)
                if live(n - 2):
                    m = n - 2
                    v.wait_ge(logits_ps, m + 1)
                    if after(m, 1):
                        v.wait_ge(topped, 3 * m)
                    nc.vector.tensor_tensor(lg[:, :, :], p_l[s][:, 0:GT * E].rearrange("p (t e) -> p t e", e=E),
                                            br[:, :].unsqueeze(1).to_broadcast([P, GT, E]), ALU.add).then_inc(lg_read, 1)
                    v.wait_ge(lg_read, m + 1)
                    kit.passed(v)
                    for j in range(GT):
                        ins = nc.vector.max(top[:, j, :], lg[:, j, :])
                    ins.then_inc(topped, 1)
                    v.wait_ge(topped, 3 * m + 1)
                    kit.passed(v)
                    for j in range(GT):
                        ins = nc.vector.max_index(top_i[:, j, :], top[:, j, :], lg[:, j, :])
                    ins.then_inc(topped, 1)
                    v.wait_ge(topped, 3 * m + 2)
                    tiles = bass.ds(m * GT, GT)
                    nc.vector.tensor_copy(r.values[:, tiles, :], top[:, :, 0:TOP_K])
                    nc.vector.tensor_copy(r.logits[:, tiles, :], lg[:, :, :])
                    nc.vector.tensor_copy(r.chosen[:, tiles, :], top_i[:, :, 0:TOP_K]).then_inc(topped, 1)
                if live(n):
                    v.wait_ge(rstd_ready, n + 1)
                    if after(n, 2):
                        v.wait_ge(xT_ps, n - 1)
                        v.wait_ge(kept[s], 8 * (n - s))
                    for j in range(GT):
                        ins = nc.vector.tensor_scalar(xn[s][:, j, :], x(j), mv[:, j, 0:1], rstd[:, j:j + 1], ALU.subtract, ALU.mult)
                    ins.then_inc(xn_ready, 1)
            run(v, step)


def plan(kit, tag, r):
    nc, m = kit.nc, MOES[tag]
    E, R, T = m.experts, m.routed, TILES
    with ExitStack() as st:
        sb, ps, sem = scoped(nc, st, tag + "_p")
        not_earlier, ones, iota = kit.not_earlier, kit.ones, kit.iota
        restart = sb("restart", [P, E, T])
        M = [sb("M0", [P, E, T]), sb("M1", [P, E, T])]
        both, pos, tot, inc, row = (sb(n, [P, E, T]) for n in ("both", "pos", "tot", "inc", "row"))
        ex = sb("ex", [P, T, R])
        es, pr, den, kp, sl = sb("es", [P, T]), sb("pr", [P, 2, T]), sb("den", [P, T]), sb("kp", [P, 2, T]), sb("sl", [P, 2, T])
        open_, over = sb("open", [P, T]), sb("over", [P, T])
        at = [pos, tot]
        away, far, sl_i = sb("away", [P, 2, T]), sb("far", [P, 2, T]), sb("sl_i", [P, 2, T], I32)
        cnt, cnt_i, nt, cum, base = sb("cnt", [P, E]), sb("cnt_i", [P, E], I32), sb("nt", [P, E]), sb("cum", [P, E]), sb("base", [P, E])
        ones_e = sb("ones_e", [P, E])
        le = sb("le", [1, m.tiles, E])
        te = sb("te", [1, m.tiles])
        p_not, p_tot = ps("p_not", [P, 512]), ps("p_tot", [P, 512])
        dve, counted, exps, asked = sem("dve"), sem("counted"), sem("exps"), sem("asked")
        block = st.enter_context(nc.Block())
        ROUNDS = 1 if not m.fallback else E

        @block.scalar
        def _(act):
            act.wait_ge(exps, 1)
            nc.scalar.activation(ex[:, :, :], ex[:, :, :], ACT.Exp)
            nc.scalar.activation(pr[:, :, :], pr[:, :, :], ACT.Exp).then_inc(exps, 1)

        @block.tensor
        def _(pe):
            for n in range(ROUNDS):
                pe.wait_ge(asked, n + 1)
                src = both[:, n, :] if m.fallback else both[:, :, :]
                width = T if m.fallback else E * T
                nc.tensor.matmul(p_tot[:, 0:width], ones[:, :], src, start=True, stop=True)
                nc.tensor.matmul(p_not[:, 0:width], not_earlier[:, :], src, start=True, stop=True).then_inc(counted, 1)

        @block.vector
        def _(v):
            c = Chain(v, dve)
            tt, ts = nc.vector.tensor_tensor, nc.vector.tensor_scalar
            c.done(nc.vector.memset(restart[:, :, :], 1.0))
            c.done(nc.vector.memset(ones_e[:, :], 1.0))
            c.done(nc.vector.memset(open_[:, :], 1.0))
            c.done(nc.vector.memset(M[0][:, :, :], 0.0))
            c.done(nc.vector.memset(M[1][:, :, :], 0.0))
            top = r.values[:, :, 0]
            c.done(tt(ex[:, :, :], r.logits[:, :, :], top.unsqueeze(2).to_broadcast([P, T, R]), ALU.subtract))
            for k in range(TOP_K):
                last = tt(pr[:, k, :], r.values[:, :, k], top, ALU.subtract)
                if k == 0:
                    c.done(last)
                else:
                    last.then_inc(exps, 1)
            c.sync()
            c.done(nc.vector.memset(restart[:, :, 0], 0.0))
            for k in range(TOP_K):
                c.done(tt(M[k][:, 0:R, :], r.chosen[:, :, k].unsqueeze(1).to_broadcast([P, R, T]),
                          iota[:, 0:R].unsqueeze(2).to_broadcast([P, R, T]), ALU.is_equal))
            c.sync()
            if not m.fallback:
                tt(both[:, :, :], M[0][:, :, :], M[1][:, :, :], ALU.add).then_inc(asked, 1)
                v.wait_ge(counted, 1)
                c.step(nc.vector.tensor_tensor_scan(inc[:, :, :].rearrange("p e t -> p (e t)"), restart[:, :, :].rearrange("p e t -> p (e t)"),
                                                    p_tot[:, 0:E * T], 0.0, ALU.mult, ALU.add))
                c.step(tt(pos[:, :, :], inc[:, :, :], p_not[:, 0:E * T].rearrange("p (e t) -> p e t", t=T), ALU.add))
                if m.cap:
                    c.step(ts(row[:, :, :], pos[:, :, :], float(m.cap), None, ALU.is_lt))
                    for k in range(TOP_K):
                        c.done(tt(M[k][:, :, :], M[k][:, :, :], row[:, :, :], ALU.mult))
                c.step(ts(cnt[:, :], inc[:, :, T - 1], float(m.cap or TOK * TOP_K), None, ALU.min))
            else:
                c.step(tt(row[:, 0:R, :], M[0][:, 0:R, :], M[1][:, 0:R, :], ALU.add))
                for e in range(E):
                    if e < R:
                        tt(both[:, e, :], row[:, e, :], open_[:, :], ALU.mult).then_inc(asked, 1)
                    else:
                        ts(both[:, e, :], open_[:, :], -1.0, 1.0, ALU.mult, ALU.add).then_inc(asked, 1)
                    v.wait_ge(counted, e + 1)
                    c.step(nc.vector.tensor_tensor_scan(inc[:, e, :], restart[:, e, :], p_tot[:, 0:T], 0.0, ALU.mult, ALU.add))
                    c.step(tt(pos[:, e, :], inc[:, e, :], p_not[:, 0:T], ALU.add))
                    if e < R:
                        c.step(nc.vector.scalar_tensor_tensor(over[:, :], pos[:, e, :], float(m.cap), both[:, e, :], ALU.is_ge, ALU.mult))
                        c.step(tt(open_[:, :], open_[:, :], over[:, :], ALU.subtract))
                for k in range(TOP_K):
                    c.done(tt(M[k][:, 0:R, :], M[k][:, 0:R, :], open_[:, :].unsqueeze(1).to_broadcast([P, R, T]), ALU.mult))
                c.done(nc.vector.tensor_copy(M[0][:, R, :], both[:, R, :]))
                c.done(ts(cnt[:, 0:R], inc[:, 0:R, T - 1], float(m.cap), None, ALU.min))
                c.done(nc.vector.tensor_copy(cnt[:, R:E], inc[:, R:E, T - 1]))
                c.sync()
            c.step(ts(cnt_i[:, :], cnt[:, :], float(P - 1), None, ALU.add))
            c.step(ts(cnt_i[:, :], cnt_i[:, :], P.bit_length() - 1, None, ALU.logical_shift_right))
            c.step(nc.vector.tensor_copy(nt[:, :], cnt_i[:, :]))
            c.step(nc.vector.tensor_tensor_scan(cum[:, :], ones_e[:, :], nt[:, :], 0.0, ALU.mult, ALU.add))
            c.step(tt(base[:, :], cum[:, :], nt[:, :], ALU.subtract))
            c.step(ts(base[:, :], base[:, :], float(P), None, ALU.mult))
            c.step(tt(row[:, :, :], pos[:, :, :], base[:, :].unsqueeze(2).to_broadcast([P, E, T]), ALU.add))
            n = m.tiles
            c.step(tt(le[:, :, :], cum[0:1, :].unsqueeze(1).to_broadcast([1, n, E]), iota[0:1, 0:n].unsqueeze(2).to_broadcast([1, n, E]), ALU.is_le))
            c.step(nc.vector.tensor_reduce(te[:, :], le[:, :, :], AX.X, ALU.add))
            c.done(ts(r.tile_expert[:, :], te[:, :], float(E - 1), None, ALU.min))
            for k in range(TOP_K):
                c.done(nc.vector.tensor_reduce(kp[:, k, :], M[k][:, :, :].rearrange("p e t -> p t e"), AX.X, ALU.add))
                c.done(tt(at[k][:, :, :], M[k][:, :, :], row[:, :, :], ALU.mult))
            c.sync()
            for k in range(TOP_K):
                c.done(nc.vector.tensor_reduce(sl[:, k, :], at[k][:, :, :].rearrange("p e t -> p t e"), AX.X, ALU.add))
            c.done(ts(away[:, :, :], kp[:, :, :], float(-NOWHERE), float(NOWHERE), ALU.mult, ALU.add))
            c.sync()
            by_choice = lambda t: t[:, :, :].rearrange("p t k -> p k t")
            c.done(nc.vector.tensor_copy(by_choice(kit.slot_back), sl[:, :, :]))
            c.done(tt(far[:, :, :], sl[:, :, :], away[:, :, :], ALU.add))
            c.sync()
            c.step(nc.vector.tensor_copy(sl_i[:, :, :], far[:, :, :]))
            c.step(ts(sl_i[:, :, :], sl_i[:, :, :], P.bit_length() - 1, None, ALU.logical_shift_right))
            c.step(nc.vector.tensor_copy(by_choice(r.slot_tile), sl_i[:, :, :]))
            c.done(nc.vector.scalar_tensor_tensor(by_choice(r.slot_row), by_choice(r.slot_tile), float(-P), far[:, :, :], ALU.mult, ALU.add))
            v.wait_ge(exps, 2)
            if m.gates == "kept_softmax":
                c.step(tt(den[:, :], pr[:, 0, :], pr[:, 1, :], ALU.add))
                c.step(nc.vector.reciprocal(den[:, :], den[:, :]))
                for k in range(TOP_K):
                    c.step(tt(pr[:, k, :], pr[:, k, :], den[:, :], ALU.mult))
                    c.step(tt(pr[:, k, :], pr[:, k, :], kp[:, k, :], ALU.mult))
                c.step(tt(den[:, :], pr[:, 0, :], pr[:, 1, :], ALU.add))
                c.step(ts(den[:, :], den[:, :], 1e-9, None, ALU.add))
            else:
                c.step(nc.vector.tensor_reduce(es[:, :], ex[:, :, :], AX.X, ALU.add))
                c.step(nc.vector.reciprocal(es[:, :], es[:, :]))
                for k in range(TOP_K):
                    c.step(tt(pr[:, k, :], pr[:, k, :], es[:, :], ALU.mult))
                c.step(tt(den[:, :], pr[:, 0, :], pr[:, 1, :], ALU.add))
                c.step(ts(den[:, :], den[:, :], 1e-9, None, ALU.max if m.gates == "probs_clip" else ALU.add))
            c.step(nc.vector.reciprocal(den[:, :], den[:, :]))
            for k in range(TOP_K):
                c.done(tt(kit.gate[:, k, :], pr[:, k, :], den[:, :], ALU.mult))
            c.sync()
            if m.fallback:
                for k in range(TOP_K):
                    c.done(tt(kit.gate[:, k, :], kit.gate[:, k, :], open_[:, :], ALU.mult))
                    c.done(tt(kp[:, k, :], kp[:, k, :], open_[:, :], ALU.mult))
                c.sync()
                c.step(tt(kit.gate[:, 0, :], kit.gate[:, 0, :], M[0][:, R, :], ALU.add))


NOWHERE = 1 << 20


def list_tokens(kit, tag, r):
    nc, T = kit.nc, MOES[tag].tiles
    Q = GT * TOP_K
    with ExitStack() as st:
        sb, ps, sem = scoped(nc, st, tag + "_l")
        at_row, at_tile = ([sb(f"{n}{i}", [P, Q, w], BF16) for i in range(2)] for n, w in (("at_row", P), ("at_tile", T)))
        numbers = [sb(f"numbers{i}", [P, 2, Q, T], BF16) for i in range(2)]
        numbered = sb("numbered", [P, 2 * T])
        p_rows = ps("p_rows", [P, 512])
        rows_ready, matched, tiles_ready, partitions_ready, summed, listed = (
            sem(n) for n in "rows_ready matched tiles_ready partitions_ready summed listed".split())
        block = st.enter_context(nc.Block())
        group = lambda t, n: t[:, bass.ds(n * GT, GT), :].rearrange("p t k -> p (t k)")

        def run(engine, step):
            pipelined(engine, (0, NG), NG, step, 2, NG)

        @block.gpsimd
        def _(pool):
            def step(n, s, live, after):
                pool.wait_ge(matched, n + 1)
                if after(n, 2):
                    pool.wait_ge(summed, n - 1)
                nc.gpsimd.tensor_tensor(numbers[s][:, 0].rearrange("p (t k) n -> p t (k n)", k=TOP_K),
                                        at_tile[s][:, :, :].rearrange("p (t k) n -> p t (k n)", k=TOP_K),
                                        kit.iota[:, bass.ds(n * GT, GT)].unsqueeze(2).to_broadcast([P, GT, TOP_K * T]),
                                        ALU.mult).then_inc(tiles_ready, 1)
            run(pool, step)

        @block.scalar
        def _(act):
            def step(n, s, live, after):
                act.wait_ge(matched, n + 1)
                if after(n, 2):
                    act.wait_ge(summed, n - 1)
                nc.scalar.activation(numbers[s][:, 1], at_tile[s][:, :, :], ACT.Copy, scale=kit.token[:, 0:1]).then_inc(partitions_ready, 1)
            run(act, step)

        @block.vector
        def _(v):
            def step(n, s, live, after):
                if after(n, 2):
                    v.wait_ge(tiles_ready, n - 1)
                    v.wait_ge(partitions_ready, n - 1)
                nc.vector.tensor_tensor(at_tile[s][:, :, :], group(r.slot_tile, n).unsqueeze(2).to_broadcast([P, Q, T]),
                                        kit.iota[:, 0:T].unsqueeze(1).to_broadcast([P, Q, T]), ALU.is_equal).then_inc(matched, 1)
                if after(n, 2):
                    v.wait_ge(summed, n - 1)
                nc.vector.tensor_tensor(at_row[s][:, :, :], group(r.slot_row, n).unsqueeze(2).to_broadcast([P, Q, P]),
                                        kit.iota[:, :].unsqueeze(1).to_broadcast([P, Q, P]), ALU.is_equal).then_inc(rows_ready, 1)
            run(v, step)
            v.wait_ge(summed, NG)
            nc.vector.tensor_copy(numbered[:, :], p_rows[:, 0:2 * T]).then_inc(listed, 1)
            v.wait_ge(listed, 1)
            nc.vector.scalar_tensor_tensor(r.row_token[:, :], numbered[:, 0:T], float(P), numbered[:, T:2 * T], ALU.mult, ALU.add).then_inc(listed, 1)
            v.wait_ge(listed, 2)

        @block.tensor
        def _(pe):
            def step(n, s, live, after):
                pe.wait_ge(rows_ready, n + 1)
                pe.wait_ge(tiles_ready, n + 1)
                pe.wait_ge(partitions_ready, n + 1)
                for q in range(Q):
                    ins = nc.tensor.matmul(p_rows[:, 0:2 * T], at_row[s][:, q, :], numbers[s][:, :, q, :],
                                           start=isinstance(n, int) and n == 0 and q == 0,
                                           stop=isinstance(n, int) and n == NG - 1 and q == Q - 1, skip_group_check=True)
                ins.then_inc(summed, 1)
            pipelined(pe, (0, NG), NG, step, 2, NG - 2)


def run_experts(kit, tag, r):
    nc, m = kit.nc, MOES[tag]
    T = m.tiles
    with ExitStack() as st:
        sb, ps, sem = scoped(nc, st, tag + "_e")
        where = sb("where", [P, 2], I32)
        xin, xT = sb("xin", [P, 2, C]), sb("xT", [C, 2, P])
        w1 = [sb(f"w1_{i}", [C, FF]) for i in range(2)]
        b1 = sb("b1", [P, 2, FK])
        hT, y = [sb(f"hT{i}", [P, FK, P]) for i in range(2)], sb("y", [P, 2, C])
        p_x, p_h, p_y = ([ps(f"{n}{i}", [P, 512]) for i in range(2)] for n in ("p_x", "p_h", "p_y"))
        in_done, out_done = [sem(f"in_done{i}") for i in range(2)], [sem(f"out_done{i}") for i in range(2)]
        staged, x_ps, xT_ready, w1_ready, b1_ready, h_ps, hb_ready, g_ready, y_ps, y_ready = (
            sem(n) for n in "staged x_ps xT_ready w1_ready b1_ready h_ps hb_ready g_ready y_ps y_ready".split())
        experts = (kit.experts_in, kit.experts_loaded)
        block = st.enter_context(nc.Block())

        def expert(engine, i):
            return engine.value_load(r.tile_expert[0:1, bass.ds(i, 1)], min_val=0, max_val=m.experts - 1)

        @block.gpsimd
        def _(pool):
            def fetch(i, s, half, first):
                if not first:
                    pool.wait_ge(x_ps, i - 1)
                nc.gpsimd.tensor_copy(where[:, s:s + 1], r.row_token[:, bass.ds(i, 1)]).then_inc(staged, 1)
                pool.wait_ge(staged, i + 1)
                kit.passed(pool)
                nc.gpsimd.indirect_dma_start(
                    out=xin[:, s, :], out_offset=None, in_=kit.normed[:, :],
                    in_offset=bass.IndirectOffsetOnAxis(ap=where[:, s:s + 1], axis=0)).then_inc(in_done[s], 16)

            def bias(i, s, first):
                e = expert(pool, i)
                if not first:
                    pool.wait_ge(hb_ready, i - 1)
                nc.gpsimd.tensor_copy(b1[:, s, :], kit.B1[:, bass.ds(e, 1), :].squeeze(1)).then_inc(b1_ready, 1)

            fetch(0, 0, 0, True)
            fetch(1, 1, 0, True)
            pool.wait_ge(*experts)
            bias(0, 0, True)
            fetch(2, 0, 1, False)
            bias(1, 1, True)
            with pool.Fori(0, (T - 4) // 2) as n:
                for s in range(2):
                    fetch(n * 2 + 3 + s, 1 - s, 0, False)
                    bias(n * 2 + 2 + s, s, False)
            fetch(T - 1, 1, 0, False)
            bias(T - 2, 0, False)
            bias(T - 1, 1, False)

        @block.scalar
        def _(act):
            act.wait_ge(*experts)

            def weights(i, s, half, first):
                e = expert(act, i)
                if not first:
                    act.wait_ge(h_ps, i - 1)
                nc.scalar.activation(w1[s][:, :], kit.W1[:, bass.ds(e, 1), :].squeeze(1), ACT.Copy).then_inc(w1_ready, 1)

            def gelu(i, s):
                act.wait_ge(hb_ready, i + 1)
                hidden = hT[s][:, :, :].rearrange("p k t -> p (k t)")
                nc.scalar.activation(hidden, hidden, ACT.Gelu).then_inc(g_ready, 1)

            def send(i, s, half):
                act.wait_ge(y_ready, i + 1)
                act.dma_start(kit.expert_out[bass.ds(i * P, P), :], y[:, s, :]).then_inc(out_done[s], 16)

            weights(0, 0, 0, True)
            weights(1, 1, 0, True)
            gelu(0, 0)
            weights(2, 0, 1, False)
            gelu(1, 1)
            with act.Fori(0, (T - 4) // 2) as n:
                for s in range(2):
                    weights(n * 2 + 3 + s, 1 - s, 0, False)
                    send(n * 2 + s, s, 0)
                    gelu(n * 2 + 2 + s, s)
            weights(T - 1, 1, 0, False)
            send(T - 4, 0, 0)
            gelu(T - 2, 0)
            send(T - 3, 1, 0)
            gelu(T - 1, 1)
            send(T - 2, 0, 0)
            send(T - 1, 1, 0)
            for s in range(2):
                act.wait_ge(out_done[s], 16 * (T // 2))

        @block.vector
        def _(v):
            def rows(i, s, half, first):
                v.wait_ge(x_ps, i + 1)
                if not first:
                    v.wait_ge(h_ps, i - 1)
                nc.vector.tensor_copy(xT[:, s, :], p_x[s][:, 0:P]).then_inc(xT_ready, 1)

            def add_b1(i, s, first=False):
                v.wait_ge(h_ps, i + 1)
                v.wait_ge(b1_ready, i + 1)
                if not first:
                    v.wait_ge(y_ps, i - 1)
                nc.vector.tensor_tensor(hT[s][:, :, :], p_h[s][:, :].rearrange("p (k t) -> p k t", t=P),
                                        b1[:, s, :].unsqueeze(2).to_broadcast([P, FK, P]), ALU.add).then_inc(hb_ready, 1)

            def add_b2(i, s, half, first=False):
                e = expert(v, i)
                v.wait_ge(y_ps, i + 1)
                if not first:
                    v.wait_ge(out_done[s], half * 16)
                nc.vector.tensor_tensor(y[:, s, :], p_y[s][:, 0:C], kit.B2[:, bass.ds(e, 1), :].squeeze(1), ALU.add).then_inc(y_ready, 1)

            v.wait_ge(*experts)
            rows(0, 0, 0, True)
            rows(1, 1, 0, True)
            add_b1(0, 0, True)
            rows(2, 0, 1, False)
            add_b1(1, 1, True)
            add_b2(0, 0, 0, True)
            rows(3, 1, 1, False)
            add_b1(2, 0)
            add_b2(1, 1, 0, True)
            with v.Fori(0, (T - 4) // 2) as n:
                for s in range(2):
                    rows(n * 2 + 4 + s, s, 0, False)
                    add_b1(n * 2 + 3 + s, 1 - s)
                    add_b2(n * 2 + 2 + s, s, n + 1)
            add_b1(T - 1, 1)
            add_b2(T - 2, 0, T // 2 - 1)
            add_b2(T - 1, 1, T // 2 - 1)

        @block.tensor
        def _(pe):
            def rows(i, s, half, first=False):
                pe.wait_ge(in_done[s], 16 * half + 16)
                if not first:
                    pe.wait_ge(xT_ready, i - 1)
                nc.tensor.transpose(p_x[s][:, 0:P], xin[:, s, :], kit.ident[:, :]).then_inc(x_ps, 1)

            def up(i, s, first=False):
                pe.wait_ge(xT_ready, i + 1)
                pe.wait_ge(w1_ready, i + 1)
                if not first:
                    pe.wait_ge(hb_ready, i - 1)
                for k in range(FK):
                    ins = nc.tensor.matmul(p_h[s][:, k * P:(k + 1) * P], w1[s][:, k * P:(k + 1) * P], xT[:, s, :], start=True, stop=True)
                ins.then_inc(h_ps, 1)

            def down(i, s, first=False):
                e = expert(pe, i)
                pe.wait_ge(g_ready, i + 1)
                if not first:
                    pe.wait_ge(y_ready, i - 1)
                for k in range(FK):
                    ins = nc.tensor.matmul(p_y[s][:, 0:C], hT[s][:, k, :], kit.W2[:, bass.ds(e, 1), k, :].squeeze(1),
                                           start=(k == 0), stop=(k == FK - 1))
                ins.then_inc(y_ps, 1)

            pe.wait_ge(*experts)
            rows(0, 0, 0, True)
            rows(1, 1, 0, True)
            up(0, 0, True)
            rows(2, 0, 1)
            up(1, 1, True)
            down(0, 0, True)
            rows(3, 1, 1)
            up(2, 0)
            down(1, 1, True)
            with pe.Fori(0, (T - 4) // 2) as n:
                for s in range(2):
                    rows(n * 2 + 4 + s, s, n + 2)
                    up(n * 2 + 3 + s, 1 - s)
                    down(n * 2 + 2 + s, s)
            up(T - 1, 1)
            down(T - 2, 0)
            down(T - 1, 1)


class Results:

    def __init__(self, kit, tag, sb, sem):
        self.kit, self.nc, self.rows_there = kit, kit.nc, MOES[tag].tiles * P
        self.rows, self.where = ([sb(f"{n}{i}", shape, dt) for i in range(2)] for n, shape, dt in (
            ("rows", [P, GT, TOP_K, C], FP32), ("where", [P, GT, TOP_K], I32)))
        self.staged, self.halved, self.added = sem("staged"), sem("halved"), sem("added")
        self.here = [[sem(f"here{i}{j}") for j in range(GT)] for i in range(2)]

    def stage(self, g, s):
        self.nc.vector.tensor_copy(self.where[s][:, :, :], self.kit.slot_back[:, bass.ds(g * GT, GT), :]).then_inc(self.staged, 1)

    def add(self, v, g, s, live):
        nc, X = self.nc, self.kit.X
        for k in range(TOP_K):
            for j in range(GT):
                if k == 0:
                    v.wait_ge(self.here[s][j], 16 * (g - s) + 32)
                t = bass.ds(g * GT + j, 1)
                x = X[:, t, :].squeeze(1)
                ins = nc.vector.scalar_tensor_tensor(x, self.rows[s][:, j, k, :], self.kit.gate[:, k, t], x, ALU.mult, ALU.add)
            if k == 0:
                ins.then_inc(self.halved, 1)
                v.wait_ge(self.halved, g + 1)
        ins.then_inc(self.added, 1)
        v.wait_ge(self.added, g + 1)
        if live(g + 2):
            self.stage(g + 2, s)
        self.kit.passed(v)

    def fetch(self, pool, g, s, after):
        pool.wait_ge(self.staged, g + 1)
        if after(g, 2):
            pool.wait_ge(self.added, g - 1)
        self.kit.passed(pool)
        for j in range(GT):
            for k in range(TOP_K):
                self.nc.gpsimd.indirect_dma_start(
                    out=self.rows[s][:, j, k, :], out_offset=None, in_=self.kit.expert_out[0:self.rows_there, :],
                    in_offset=bass.IndirectOffsetOnAxis(ap=self.where[s][:, j, k:k + 1], axis=0)).then_inc(self.here[s][j], 16)


def attention(kit, tag, experts):
    nc, A = kit.nc, kit.A
    SCALE = C ** -0.5
    NB = GROUP // S
    with ExitStack() as st:
        sb, ps, sem = scoped(nc, st, tag)
        w = {n: sb(n, [C, C]) for n in ("Wq", "Wk", "Wv", "Wo")}
        bias = {n: sb(n, [C, 1]) for n in ("bq", "bk", "bv")}
        bo = sb("bo", [P, C])
        cT = [sb(f"cT{i}", [C, GROUP]) for i in range(2)]
        stats, mv, var, rstd = sb("stats", [P, GT, 6]), sb("mv", [P, GT, 2]), sb("var", [P, GT]), sb("rstd", [P, GT])
        xn = [sb(f"xn{i}", [P, GT, C]) for i in range(2)]
        xnT = sb("xnT", [C, TOK])
        QT, KT, V = ([sb(f"{n}{i}", shape) for i in range(2)] for n, shape in (("QT", [C, GROUP]), ("KT", [C, GROUP]), ("V", [S, NB * C])))
        Pm, mx, su, rs = sb("Pm", [P, PAIRS, S]), sb("mx", [P, PAIRS]), sb("su", [P, PAIRS]), sb("rs", [P, PAIRS])
        PT, aT = sb("PT", [S, GROUP]), sb("aT", [C, GROUP])
        p_x, p_q, p_k, p_st, p_a, p_y = (ps(n, [P, 512]) for n in ("p_x", "p_q", "p_k", "p_st", "p_a", "p_y"))
        p_v = ps("p_v", [P, 1024])
        kv_in, rest_in, dve, var_ready, rstd_ready = (sem(n) for n in ("kv_in", "rest_in", "dve", "var_ready", "rstd_ready"))
        ctx_in = [sem(f"ctx_in{i}") for i in range(2)]
        (xn_ready, xT_ps, xnT_ready, q_ps, k_ps, v_ps, qT_ready, kT_ready, v_ready, s_ps, mx_ready, d_ready, e_ready, sums, p_ready, t_ps,
         pT_ready, a_ps, a_ready, y_ps, y_added, bo_added) = (sem(n) for n in (
             "xn_ready xT_ps xnT_ready q_ps k_ps v_ps qT_ready kT_ready v_ready s_ps mx_ready d_ready e_ready sums p_ready t_ps "
             "pT_ready a_ps a_ready y_ps y_added bo_added").split())
        X = kit.X
        results = Results(kit, experts, sb, sem)
        block = st.enter_context(nc.Block())
        group, tiles = lambda n: bass.ds(n * GROUP, GROUP), lambda n: bass.ds(n * GT, GT)

        def run(engine, step):
            pipelined(engine, (-2, NG + 2), NG, step, 2, NG - 4)

        @block.sync
        def _(sp):
            for n in ("Wk", "Wv"):
                sp.dma_start(w[n][:, :], A[f"{tag}_{n}"]).then_inc(kv_in, 16)
            for n in ("Wq", "Wo"):
                sp.dma_start(w[n][:, :], A[f"{tag}_{n}"]).then_inc(rest_in, 16)
            for n in bias:
                sp.dma_start(bias[n][:, :], A[f"{tag}_{n}"].rearrange("(c a) -> c a", a=1)).then_inc(rest_in, 16)
            sp.dma_start(bo[:, :], A[f"{tag}_bo"].rearrange("(a c) -> a c", a=1).to_broadcast([P, C])).then_inc(rest_in, 16)

            def step(n, s, live, after):
                if live(n + 1):
                    if after(n + 1, 2):
                        sp.wait_ge(v_ps, n)
                    sp.dma_start(cT[1 - s][:, :], A["ctxT"][:, group(n + 1)]).then_inc(ctx_in[1 - s], 16)
            run(sp, step)

        @block.gpsimd
        def _(pool):
            for g in range(2):
                results.fetch(pool, g, g, lambda i, k: i >= k)
            pool.wait_ge(rest_in, 96)

            def step(n, s, live, after):
                if live(n + 2):
                    inverse_root(nc, pool, var, var_ready, rstd, rstd_ready, kit.minus_half, n + 2)
                if live(n + 4):
                    results.fetch(pool, n + 4, s, after)
                if live(n + 1):
                    xg = X[:, tiles(n + 1), :]
                    pool.wait_ge(xn_ready, n + 2)
                    nc.gpsimd.tensor_tensor(xg, xg, bo[:, :].unsqueeze(1).to_broadcast([P, GT, C]), ALU.add).then_inc(bo_added, 1)
            run(pool, step)

        @block.scalar
        def _(act):
            act.wait_ge(rest_in, 96)

            def step(n, s, live, after):
                t = 1 - s
                if live(n - 1):
                    act.wait_ge(d_ready, n)
                    nc.scalar.activation(Pm[:, :, :], Pm[:, :, :], ACT.Exp, scale=SCALE).then_inc(e_ready, 1)
                if live(n):
                    act.wait_ge(v_ps, n + 1)
                    if after(n, 2):
                        act.wait_ge(a_ps, n - 1)
                    nc.scalar.activation(V[s][:, :], p_v[0:S, :], ACT.Copy).then_inc(v_ready, 1)
                if live(n + 1):
                    act.wait_ge(xT_ps, n + 2)
                    nc.scalar.activation(xnT[:, group(n + 1)], p_x[:, :], ACT.Copy).then_inc(xnT_ready, 1)
                if live(n - 1):
                    act.wait_ge(t_ps, n)
                    nc.scalar.activation(PT[:, :], p_st[0:S, :], ACT.Copy).then_inc(pT_ready, 1)
                if live(n + 1):
                    act.wait_ge(q_ps, n + 2)
                    if after(n + 1, 2):
                        act.wait_ge(s_ps, n)
                    nc.scalar.activation(QT[t][:, :], p_q[:, :], ACT.Identity, bias=bias["bq"][:, :]).then_inc(qT_ready, 1)
            run(act, step)

        @block.vector
        def _(v):
            results.stage(0, 0)
            results.stage(1, 1)
            v.sem_inc(a_ready, 1)
            v.sem_inc(y_added, 1)
            v.wait_ge(rest_in, 96)
            tt, ts = nc.vector.tensor_tensor, nc.vector.tensor_scalar

            def step(n, s, live, after):
                x = lambda j: X[:, bass.ds((n + 2) * GT + j, 1), :].squeeze(1)
                wide = lambda t: t[:, :].unsqueeze(2).to_broadcast([P, PAIRS, S])
                if live(n - 1):
                    v.wait_ge(s_ps, n)
                    s3 = p_st[:, 0:PAIRS * S].rearrange("p (j k) -> p j k", k=S)
                    nc.vector.tensor_reduce(mx[:, :], s3, AX.X, ALU.max).then_inc(mx_ready, 1)
                    v.wait_ge(mx_ready, n)
                    if after(n - 1, 1):
                        v.wait_ge(t_ps, n - 1)
                    tt(Pm[:, :, :], s3, wide(mx), ALU.subtract).then_inc(d_ready, 1)
                if live(n + 2):
                    results.add(v, n + 2, s, lambda i: live(i))
                    for j in range(GT):
                        ins = nc.vector.bn_stats(stats[:, j, :], x(j))
                    ins.then_inc(dve, 1)
                    v.wait_ge(dve, 2 * n + 5)
                    kit.passed(v)
                    for j in range(GT):
                        ins = nc.vector.bn_aggr(mv[:, j, :], stats[:, j, :])
                    ins.then_inc(dve, 1)
                    v.wait_ge(dve, 2 * n + 6)
                    ts(var[:, :], mv[:, :, 1], LN_EPS, None, ALU.add).then_inc(var_ready, 1)
                if live(n):
                    v.wait_ge(k_ps, n + 1)
                    if after(n, 2):
                        v.wait_ge(s_ps, n - 1)
                    ts(KT[s][:, :], p_k[:, :], bias["bk"][:, :], None, ALU.add).then_inc(kT_ready, 1)
                if live(n - 1):
                    v.wait_ge(e_ready, n)
                    nc.vector.tensor_reduce(su[:, :], Pm[:, :, :], AX.X, ALU.add).then_inc(sums, 1)
                    v.wait_ge(sums, 2 * n - 1)
                    nc.vector.reciprocal(rs[:, :], su[:, :]).then_inc(sums, 1)
                    v.wait_ge(sums, 2 * n)
                    tt(Pm[:, :, :], Pm[:, :, :], wide(rs), ALU.mult).then_inc(p_ready, 1)
                if live(n - 2):
                    m = n - 2
                    v.wait_ge(a_ps, m + 1)
                    v.wait_ge(y_ps, m + 1)
                    nc.vector.scalar_tensor_tensor(aT[:, :], p_a[:, :], bias["bv"][:, :], xnT[:, group(m)], ALU.add, ALU.add).then_inc(a_ready, 1)
                if live(n + 2):
                    v.wait_ge(rstd_ready, n + 3)
                    if after(n + 2, 2):
                        v.wait_ge(xT_ps, n + 1)
                    for j in range(GT):
                        ins = ts(xn[s][:, j, :], x(j), mv[:, j, 0:1], rstd[:, j:j + 1], ALU.subtract, ALU.mult)
                    ins.then_inc(xn_ready, 1)
                if live(n - 2):
                    m = n - 2
                    v.wait_ge(y_ps, m + 2)
                    v.wait_ge(bo_added, m + 1)
                    xg = X[:, tiles(m), :]
                    tt(xg, xg, p_y[:, :].rearrange("p (t c) -> p t c", c=C), ALU.add).then_inc(y_added, 1)
            run(v, step)

        @block.tensor
        def _(pe):
            pe.sem_inc(y_ps, 1)
            pe.wait_ge(rest_in, 96)
            pe.wait_ge(kv_in, 32)

            def step(n, s, live, after):
                t = 1 - s
                if live(n - 1):
                    pe.wait_ge(qT_ready, n)
                    pe.wait_ge(kT_ready, n)
                    if after(n - 1, 1):
                        pe.wait_ge(pT_ready, n - 1)
                    kit.passed(pe)
                    for b in range(NB):
                        c = slice(b * S, (b + 1) * S)
                        ins = nc.tensor.matmul(p_st[b % 2 * S:(b % 2 + 1) * S, b // 2 * S:(b // 2 + 1) * S], QT[t][:, c], KT[t][:, c],
                                               start=True, stop=True)
                    ins.then_inc(s_ps, 1)
                if live(n):
                    pe.wait_ge(ctx_in[s], 8 * (n - s) + 16)
                    if after(n, 1):
                        pe.wait_ge(kT_ready, n)
                    nc.tensor.matmul(p_k[:, :], w["Wk"][:, :], cT[s][:, :], start=True, stop=True).then_inc(k_ps, 1)
                    if after(n, 1):
                        pe.wait_ge(v_ready, n)
                    kit.passed(pe)
                    for b in range(NB):
                        ins = nc.tensor.matmul(p_v[0:S, b * C:(b + 1) * C], cT[s][:, b * S:(b + 1) * S], w["Wv"][:, :], start=True, stop=True)
                    ins.then_inc(v_ps, 1)
                if live(n - 2):
                    m = n - 2
                    pe.wait_ge(v_ready, m + 1)
                    pe.wait_ge(pT_ready, m + 1)
                    pe.wait_ge(a_ready, m + 1)
                    kit.passed(pe)
                    for b in range(NB):
                        ins = nc.tensor.matmul(p_a[:, b * S:(b + 1) * S], V[s][:, b * C:(b + 1) * C], PT[:, b * S:(b + 1) * S], start=True, stop=True)
                    ins.then_inc(a_ps, 1)
                if live(n + 1):
                    pe.wait_ge(xn_ready, n + 2)
                    if after(n + 1, 1):
                        pe.wait_ge(xnT_ready, n + 1)
                    for j in range(GT):
                        ins = nc.tensor.transpose(p_x[:, j * P:(j + 1) * P], xn[t][:, j, :], kit.ident[:, :])
                    ins.then_inc(xT_ps, 1)
                if live(n - 2):
                    m = n - 2
                    pe.wait_ge(a_ready, m + 2)
                    pe.wait_ge(y_added, m + 1)
                    for j in range(GT):
                        ins = nc.tensor.matmul(p_y[:, j * C:(j + 1) * C], aT[:, j * P:(j + 1) * P], w["Wo"][:, :], start=True, stop=True)
                    ins.then_inc(y_ps, 1)
                if live(n - 1):
                    pe.wait_ge(p_ready, n)
                    kit.passed(pe)
                    for j in range(PAIRS):
                        ins = nc.tensor.transpose(p_st[0:S, j * P:(j + 1) * P], Pm[:, j, :], kit.ident[:, :])
                    ins.then_inc(t_ps, 1)
                if live(n + 1):
                    pe.wait_ge(xnT_ready, n + 2)
                    if after(n + 1, 1):
                        pe.wait_ge(qT_ready, n + 1)
                    nc.tensor.matmul(p_q[:, :], w["Wq"][:, :], xnT[:, group(n + 1)], start=True, stop=True).then_inc(q_ps, 1)
            run(pe, step)


def mlstm(kit, tag, experts):
    nc = kit.nc
    H, DH = 8, 16
    HH = H // 2
    VW = 2 * 2 * DH + 2
    with ExitStack() as st:
        sb, _, _ = scoped(nc, st, tag)
        QT, KT = sb("QT", [C, TOK]), sb("KT", [C, TOK])
        V2 = sb("V2", [P, B, 2, VW])
        gm, M = sb("gm", [H, TOK]), sb("M", [H, TOK])
        en = sb("en", [P, TILES, 2 * HH])
        mlstm_gates(kit, tag, experts, QT, KT, V2, gm, M, en, H, DH, HH, VW)
        mlstm_attend(kit, tag, QT, KT, V2, gm, M, en, H, DH, HH, VW)


def mlstm_gates(kit, tag, experts, QT, KT, V2, gm, M, en, H, DH, HH, VW):
    nc, A = kit.nc, kit.A
    NB = GROUP // S
    FAR = -1e30
    with ExitStack() as st:
        sb, ps, sem = scoped(nc, st, tag + "_g")
        gate_w = sb("gate_w", [C, 3, P])
        ib, fb = sb("ib", [H, 1]), sb("fb", [H, 1])
        half_mask = sb("half_mask", [P, C])
        hoh, foh = sb("hoh", [H, HH]), sb("foh", [H, 2])
        c2 = [sb(f"c2_{i}", [P, NB, C]) for i in range(2)]
        stats, mv, var, rstd = sb("stats", [P, GT, 6]), sb("mv", [P, GT, 2]), sb("var", [P, GT]), sb("rstd", [P, GT])
        xn = [sb(f"xn{i}", [P, GT, C]) for i in range(2)]
        na, lf, cs, low = (sb(n, [H, GROUP]) for n in ("na", "lf", "cs", "low"))
        i_, f_ = [sb(f"i_{k}", [H, GROUP]) for k in range(2)], [sb(f"f_{k}", [H, GROUP]) for k in range(2)]
        restart, drop = sb("restart", [H, GROUP]), sb("drop", [H, GROUP])
        nm = [sb(f"nm{i}", [P, NB, 2, S]) for i in range(2)]
        head_rows = sb("head_rows", [P, HH])
        p_x = [ps(f"p_x{i}", [P, 512]) for i in range(2)]
        p_g, p_n = ps("p_g", [P, 512]), ps("p_n", [P, 512])
        keys_in, weights = sem("keys_in"), sem("weights")
        c2_in = [sem(f"c2_in{i}") for i in range(2)]
        (set_up, var_ready, rstd_ready, xn_ready, xT_ps, xnT_ready, g_ps, fi_ready, na_ready, exp_ready, l_ready, scanned,
         m_ready, nm_ready, n_ps, en_ready, v_ready, dve) = (sem(n) for n in (
             "set_up var_ready rstd_ready xn_ready xT_ps xnT_ready g_ps fi_ready na_ready exp_ready l_ready scanned "
             "m_ready nm_ready n_ps en_ready v_ready dve").split())
        N_WEIGHTS, SET_UP = 16 * 6, 12
        X = kit.X
        results = Results(kit, experts, sb, sem)
        block = st.enter_context(nc.Block())
        group = lambda n: bass.ds(n * GROUP, GROUP)

        def run(engine, step):
            pipelined(engine, (0, NG + 3), NG, step, 4, NG - 2)

        @block.sync
        def _(sp):
            col = lambda name: A[name].rearrange("(c a) -> c a", a=1)
            for dst, src in ((gate_w[:, :, :], A[f"{tag}_gate_w"]), (ib[:, :], col(f"{tag}_igate_b")), (fb[:, :], col(f"{tag}_fgate_b")),
                             (half_mask[:, :], A["half_mask16"]), (hoh[:, :], A["head_of_half"]), (foh[:, :], A["half_of_head"])):
                sp.dma_start(dst, src).then_inc(weights, 16)
            sp.dma_start(KT[:, :], A["ctxT"]).then_inc(keys_in, 16)

            def step(n, s, live, after):
                if live(n):
                    if after(n, 2):
                        sp.wait_ge(v_ready, n - 1)
                    for twice in range(2):
                        sp.dma_start(c2[s][twice * S:(twice + 1) * S, :, :],
                                     A["ctx"][group(n), :].rearrange("(b s) c -> s b c", s=S)).then_inc(c2_in[s], 16)
            run(sp, step)

        @block.gpsimd
        def _(pool):
            for g in range(2):
                results.fetch(pool, g, g, lambda i, k: i >= k)
            pool.wait_ge(weights, N_WEIGHTS)
            pool.wait_ge(set_up, SET_UP)


            def step(n, s, live, after):
                if live(n):
                    inverse_root(nc, pool, var, var_ready, rstd, rstd_ready, kit.minus_half, n)
                if live(n + 2):
                    results.fetch(pool, n + 2, s, after)
            run(pool, step)

        @block.scalar
        def _(act):
            act.wait_ge(weights, N_WEIGHTS)
            act.wait_ge(set_up, SET_UP)

            def step(n, s, live, after):
                if live(n - 2):
                    act.wait_ge(m_ready, n - 1)
                    if after(n - 2, 2):
                        act.wait_ge(n_ps, n - 3)
                    for f in range(2):
                        ins = nc.scalar.activation(nm[s][0:H, :, f, :], low[:, :].rearrange("h (b s) -> h b s", s=S), ACT.Copy,
                                                   scale=foh[:, f:f + 1])
                    ins.then_inc(nm_ready, 1)
                if live(n - 1):
                    act.wait_ge(g_ps, n)
                    if after(n - 1, 2):
                        act.wait_ge(m_ready, n - 2)
                    nc.scalar.activation(f_[1 - s][:, :], p_g[32:40, :], ACT.Identity, bias=fb[:, :])
                    nc.scalar.activation(i_[1 - s][:, :], p_g[0:H, :], ACT.Identity, bias=ib[:, :]).then_inc(fi_ready, 1)
                if live(n - 1):
                    act.wait_ge(na_ready, n)
                    nc.scalar.activation(na[:, :], na[:, :], ACT.Exp).then_inc(exp_ready, 1)
                    act.wait_ge(exp_ready, n)
                    nc.scalar.activation(na[:, :], na[:, :], ACT.Ln, bias=1.0).then_inc(l_ready, 1)
                if live(n):
                    act.wait_ge(xT_ps, n + 1)
                    nc.scalar.activation(QT[:, group(n)], p_x[s][:, :], ACT.Copy).then_inc(xnT_ready, 1)
                if live(n - 3):
                    act.wait_ge(n_ps, n - 2)
                    nc.scalar.activation(en[:, bass.ds((n - 3) * GT, GT), :].rearrange("p j h -> p (j h)"), p_n[:, 0:PAIRS * 2 * HH],
                                         ACT.Exp).then_inc(en_ready, 1)
            run(act, step)

        @block.vector
        def _(v):
            results.stage(0, 0)
            results.stage(1, 1)
            tt, ts, stt = nc.vector.tensor_tensor, nc.vector.tensor_scalar, nc.vector.scalar_tensor_tensor
            at = 0

            def setup(ins):
                nonlocal at
                at += 1
                ins.then_inc(set_up, 1)
                v.wait_ge(set_up, at)

            setup(nc.vector.memset(restart[:, :], 1.0))
            setup(nc.vector.memset(restart[:, :].rearrange("h (b s) -> h b s", s=S)[:, :, 0], 0.0))
            setup(nc.vector.memset(drop[:, :], 0.0))
            setup(nc.vector.memset(drop[:, :].rearrange("h (b s) -> h b s", s=S)[:, :, 0], FAR))
            setup(nc.vector.memset(V2[:, :, :, 4 * DH:VW], 0.0))
            setup(nc.vector.memset(V2[0:S, :, :, 4 * DH:4 * DH + 1], 1.0))
            setup(nc.vector.memset(V2[S:P, :, :, 4 * DH + 1:VW], 1.0))
            for i in range(2):
                setup(nc.vector.memset(nm[i][:, :, :, :], 0.0))
            setup(nc.vector.memset(head_rows[:, :], 0.0))
            v.wait_ge(weights, N_WEIGHTS)
            setup(nc.vector.tensor_copy(head_rows[0:H, :], hoh[:, :]))
            setup(tt(gate_w[:, 1, :], gate_w[:, 1, :], gate_w[:, 2, :], ALU.add))
            assert at == SET_UP

            def step(n, s, live, after):
                x = lambda j: X[:, bass.ds(n * GT + j, 1), :].squeeze(1)
                if live(n):
                    results.add(v, n, s, live)
                    for j in range(GT):
                        ins = nc.vector.bn_stats(stats[:, j, :], x(j))
                    ins.then_inc(dve, 1)
                    v.wait_ge(dve, 2 * n + 1)
                    kit.passed(v)
                    for j in range(GT):
                        ins = nc.vector.bn_aggr(mv[:, j, :], stats[:, j, :])
                    ins.then_inc(dve, 1)
                    v.wait_ge(dve, 2 * n + 2)
                    ts(var[:, :], mv[:, :, 1], LN_EPS, None, ALU.add).then_inc(var_ready, 1)
                    v.wait_ge(c2_in[s], 16 * (n - s) + 32)
                    hm = half_mask[:, :].rearrange("p (f i c) -> p i f c", f=2, c=2 * DH)
                    for b in range(NB):
                        ins = tt(V2[:, bass.ds(n * NB + b, 1), :, 0:4 * DH].squeeze(1).rearrange("p i (f c) -> p i f c", f=2),
                                 c2[s][:, b, :].rearrange("p (f i c) -> p i f c", f=2, c=2 * DH), hm, ALU.mult)
                    ins.then_inc(v_ready, 1)
                if live(n - 1):
                    v.wait_ge(fi_ready, n)
                    if after(n - 1, 1):
                        v.wait_ge(m_ready, n - 1)
                    stt(na[:, :], f_[1 - s][:, :], -1.0, f_[1 - s][:, :], ALU.mult, ALU.min).then_inc(na_ready, 1)
                if live(n):
                    v.wait_ge(rstd_ready, n + 1)
                    if after(n, 2):
                        v.wait_ge(xT_ps, n - 1)
                    for j in range(GT):
                        ins = ts(xn[s][:, j, :], x(j), mv[:, j, 0:1], rstd[:, j:j + 1], ALU.subtract, ALU.mult)
                    ins.then_inc(xn_ready, 1)
                if live(n - 1):
                    m = n - 1
                    v.wait_ge(l_ready, n)
                    stt(lf[:, :], f_[1 - s][:, :], 0.0, na[:, :], ALU.min, ALU.subtract).then_inc(scanned, 1)
                    v.wait_ge(scanned, 4 * m + 1)
                    nc.vector.tensor_tensor_scan(cs[:, :], restart[:, :], lf[:, :], 0.0, ALU.mult, ALU.add).then_inc(scanned, 1)
                    v.wait_ge(scanned, 4 * m + 2)
                    tt(gm[:, group(m)], i_[1 - s][:, :], cs[:, :], ALU.subtract).then_inc(scanned, 1)
                    v.wait_ge(scanned, 4 * m + 3)
                    nc.vector.tensor_tensor_scan(M[:, group(m)], drop[:, :], gm[:, group(m)], FAR, ALU.add, ALU.max).then_inc(scanned, 1)
                    v.wait_ge(scanned, 4 * m + 4)
                    if after(m, 1):
                        v.wait_ge(nm_ready, m)
                    stt(low[:, :], cs[:, :], -1.0, M[:, group(m)], ALU.mult, ALU.subtract).then_inc(m_ready, 1)
            run(v, step)

        @block.tensor
        def _(pe):
            pe.wait_ge(weights, N_WEIGHTS)
            pe.wait_ge(keys_in, 16)
            pe.wait_ge(set_up, SET_UP)

            def step(n, s, live, after):
                if live(n - 1):
                    m = n - 1
                    if after(m, 1):
                        pe.wait_ge(fi_ready, m)
                    pe.wait_ge(xnT_ready, m + 1)
                    kit.passed(pe)
                    nc.tensor.matmul(p_g[:, :], gate_w[:, 1, :], KT[:, group(m)], start=True, stop=False)
                    nc.tensor.matmul(p_g[:, :], gate_w[:, 0, :], QT[:, group(m)], start=False, stop=True).then_inc(g_ps, 1)
                if live(n):
                    pe.wait_ge(xn_ready, n + 1)
                    if after(n, 2):
                        pe.wait_ge(xnT_ready, n - 1)
                    for j in range(GT):
                        ins = nc.tensor.transpose(p_x[s][:, j * P:(j + 1) * P], xn[s][:, j, :], kit.ident[:, :])
                    ins.then_inc(xT_ps, 1)
                if live(n - 3):
                    pe.wait_ge(nm_ready, n - 2)
                    if after(n - 3, 1):
                        pe.wait_ge(en_ready, n - 3)
                    kit.passed(pe)
                    for b in range(NB):
                        ins = nc.tensor.matmul(p_n[:, b * HH:(b + 1) * HH], nm[1 - s][:, b], head_rows[:, :], start=True, stop=True)
                    ins.then_inc(n_ps, 1)
            run(pe, step)


def mlstm_attend(kit, tag, QT, KT, V2, gm, M, en, H, DH, HH, VW):
    nc, A = kit.nc, kit.A
    EPS = 1e-6
    N = 2 * HH
    with ExitStack() as st:
        sb, ps, sem = scoped(nc, st, tag + "_a")
        out_w = sb("out_w", [P, C // 2])
        head_mask = sb("head_mask", [P, HH])
        pick = sb("pick", [P, 2, S])
        hoh, foh = sb("hoh", [H, HH]), sb("foh", [H, 2])
        minus_foh = sb("minus_foh", [H, 2])
        later32, later = sb("later32", [S, S]), sb("later", [S, N, S], BF16)
        ident2 = sb("ident2", [S, 2, S], BF16)
        Qz = [sb(f"Qz{i}", [C, 2, 2, S]) for i in range(2)]
        Km = [sb(f"Km{i}", [C, 2, HH, S]) for i in range(2)]
        left = [sb(f"left{i}", [P, 2, 2, S]) for i in range(2)]
        right = [sb(f"right{i}", [P, 2, HH, S]) for i in range(2)]
        D, Cm = sb("D", [P, 2, 512]), [sb(f"Cm{i}", [P, 512]) for i in range(2)]
        CT = sb("CT", [P, 512])
        n1, n2, nrm = sb("n1", [P, N]), sb("n2", [P, N]), sb("nrm", [P, N])
        raw, sq = sb("raw", [P, N, DH]), sb("sq", [P, N, DH])
        cen, hs, hh = sb("cen", [P, 2, N, DH]), sb("hs", [P, 2, N, DH]), sb("hh", [P, 2, N, DH])
        total, hv, hr = sb("total", [P, N]), sb("hv", [P, 2, N]), sb("hr", [P, 2, N])
        minus_half, ln_eps = sb("minus_half", [P, N]), sb("ln_eps", [P, 1])
        p_d, p_q = ([ps(f"{n}{i}", [P, 512]) for i in range(2)] for n in ("p_d", "p_q"))
        p_t, p_o, p_y = (ps(n, [P, 512]) for n in ("p_t", "p_o", "p_y"))
        consts_in = sem("consts_in")
        (set_up, qz_ready, km_ready, left_ready, right_ready, d_ps, q_ps, e_ready, c_ready, t_ps, cT_ready, o_ps, o_read, dve,
         hv_ready, hr_ready, hn_ready, y_ps, y_added, sums_ready, scaled) = (sem(n) for n in (
             "set_up qz_ready km_ready left_ready right_ready d_ps q_ps e_ready c_ready t_ps cT_ready o_ps o_read dve "
             "hv_ready hr_ready hn_ready y_ps y_added sums_ready scaled").split())
        N_CONSTS = 16 * 8
        SET_UP = 15
        X = kit.X
        block = st.enter_context(nc.Block())
        pair = lambda j: bass.ds(j * P, P)

        def run(engine, step):
            pipelined(engine, (-3, TILES + 5), TILES, step, 8, TILES - 4)

        @block.sync
        def _(sp):
            for dst, src in ((head_mask[:, :], A["head_mask16"]), (pick[:, :, :].rearrange("p f s -> p (f s)"), A["ident"]),
                             (hoh[:, :], A["head_of_half"]), (foh[:, :], A["half_of_head"]),
                             (later32[:, :], A["later"]), (minus_foh[:, :], A["minus_half_of_head"])):
                sp.dma_start(dst, src).then_inc(consts_in, 16)
            for f in range(2):
                half = A[f"{tag}_out_w"][f * 64:f * 64 + 64]
                sp.dma_start(out_w[f * S:(f + 1) * S, :], half.rearrange("(a c) -> a c", a=1).to_broadcast([S, C // 2])).then_inc(consts_in, 16)
            sp.wait_ge(consts_in, N_CONSTS)

        @block.gpsimd
        def _(pool):
            pool.wait_ge(consts_in, N_CONSTS)
            pool.wait_ge(set_up, SET_UP)

            def moving(j, s, after):
                if after(j, 2):
                    pool.wait_ge(d_ps, j - 1)
                b3 = lambda t: t[:, pair(j)].rearrange("h (b s) -> h b s", s=S)
                for b in range(2):
                    ins = nc.gpsimd.tensor_tensor(right[s][0:H, b], b3(gm)[:, b].unsqueeze(1).to_broadcast([H, HH, S]),
                                                  hoh[:, :].unsqueeze(2).to_broadcast([H, HH, S]), ALU.mult)
                ins.then_inc(right_ready, 1)
                if after(j, 2):
                    pool.wait_ge(q_ps, j - 1)
                for b in range(2):
                    ins = nc.gpsimd.tensor_tensor(Km[s][:, b], b3(KT)[:, b].unsqueeze(1).to_broadcast([C, HH, S]),
                                                  head_mask[:, :].unsqueeze(2).to_broadcast([C, HH, S]), ALU.mult)
                ins.then_inc(km_ready, 1)

            def weigh(j, s, after):
                pool.wait_ge(scaled, j + 1)
                if after(j, 2):
                    pool.wait_ge(y_ps, j - 1)
                nc.gpsimd.tensor_tensor(hh[:, s].rearrange("p (b h) c -> p b (h c)", h=HH), hs[:, s].rearrange("p (b h) c -> p b (h c)", h=HH),
                   out_w[:, :].unsqueeze(1).to_broadcast([P, 2, C // 2]), ALU.mult).then_inc(hn_ready, 1)

            def step(n, s, live, after):
                if live(n + 3):
                    moving(n + 3, 1 - s, after)
                if live(n - 2):
                    pool.wait_ge(hv_ready, n - 1)
                    if after(n - 2, 2):
                        pool.wait_ge(scaled, n - 3)
                    nc.gpsimd.tensor_tensor(hr[:, s, :], hv[:, s, :], minus_half[:, :], ALU.pow).then_inc(hr_ready, 1)
                if live(n - 3):
                    weigh(n - 3, 1 - s, after)
            run(pool, step)

        @block.scalar
        def _(act):
            act.wait_ge(consts_in, N_CONSTS)
            act.wait_ge(set_up, SET_UP)

            def queries(j, s, after):
                if after(j, 2):
                    act.wait_ge(q_ps, j - 1)
                for f in range(2):
                    rows = slice(64 * f, 64 * f + 64)
                    ins = nc.scalar.activation(Qz[s][rows, :, f, :], QT[rows, pair(j)].rearrange("c (b s) -> c b s", s=S), ACT.Copy)
                ins.then_inc(qz_ready, 1)

            def minus_m(j, s, after):
                if after(j, 2):
                    act.wait_ge(d_ps, j - 1)
                for f in range(2):
                    ins = nc.scalar.activation(left[s][32:40, :, f, :], M[:, pair(j)].rearrange("h (b s) -> h b s", s=S), ACT.Copy,
                                               scale=minus_foh[:, f:f + 1])
                ins.then_inc(left_ready, 1)

            def step(n, s, live, after):
                if live(n + 1):
                    act.wait_ge(d_ps, n + 2)
                    if after(n + 1, 2):
                        act.wait_ge(c_ready, n)
                    nc.scalar.activation(D[:, 1 - s, :], p_d[1 - s][:, :], ACT.Exp).then_inc(e_ready, 1)
                if live(n - 2):
                    act.wait_ge(sums_ready, n - 1)
                    nc.scalar.activation(hv[:, s, :], hv[:, s, :], ACT.Identity, scale=1.0 / DH, bias=ln_eps[:, :]).then_inc(hv_ready, 1)
                if live(n):
                    act.wait_ge(t_ps, n + 1)
                    if after(n, 1):
                        act.wait_ge(o_ps, n)
                    nc.scalar.activation(CT[:, :], p_t[:, :], ACT.Copy).then_inc(cT_ready, 1)
                if live(n + 3):
                    minus_m(n + 3, 1 - s, after)
                    queries(n + 3, 1 - s, after)
            run(act, step)

        @block.vector
        def _(v):
            tt, ts, stt = nc.vector.tensor_tensor, nc.vector.tensor_scalar, nc.vector.scalar_tensor_tensor
            at = 0

            def setup(ins):
                nonlocal at
                at += 1
                ins.then_inc(set_up, 1)
                v.wait_ge(set_up, at)

            for i in range(2):
                setup(nc.vector.memset(left[i][:, :, :, :], 0.0))
                setup(nc.vector.memset(right[i][:, :, :, :], 0.0))
                setup(nc.vector.memset(Qz[i][:, :, :, :], 0.0))
            v.wait_ge(consts_in, N_CONSTS)
            for i in range(2):
                setup(tt(left[i][0:H], left[i][0:H], foh[:, :].unsqueeze(1).unsqueeze(3).to_broadcast([H, 2, 2, S]), ALU.add))
                setup(tt(right[i][32:40], right[i][32:40], hoh[:, :].unsqueeze(1).unsqueeze(3).to_broadcast([H, 2, HH, S]), ALU.add))
            setup(nc.vector.memset(minus_half[:, :], -0.5))
            setup(nc.vector.memset(ln_eps[:, :], LN_EPS))
            setup(ts(en[:, :, :], en[:, :, :], EPS, None, ALU.add))
            setup(nc.vector.tensor_copy(ident2[:, :, :], pick[0:S, 0, :].unsqueeze(1).to_broadcast([S, 2, S])))
            setup(nc.vector.tensor_copy(later[:, :, :], later32[:, :].unsqueeze(1).to_broadcast([S, N, S])))
            assert at == SET_UP

            def product(j, s, after):
                v.wait_ge(e_ready, j + 1)
                v.wait_ge(q_ps, j + 1)
                if after(j, 2):
                    v.wait_ge(t_ps, j - 1)
                stt(Cm[s][:, :], p_q[s][:, :], DH ** -0.5, D[:, s, :], ALU.mult, ALU.mult).then_inc(c_ready, 1)

            STEPS = 7

            def normalise(j, s, after):
                at = 0

                def own(ins):
                    nonlocal at
                    at += 1
                    ins.then_inc(dve, 1)
                    v.wait_ge(dve, STEPS * j + at)

                v.wait_ge(o_ps, j + 1)
                po = p_o[:, 0:4 * VW].rearrange("p (h c) -> p h c", c=VW)
                own(nc.vector.tensor_copy(n1[:, :].rearrange("p (h c) -> p h c", c=2), po[:, :, 4 * DH:VW]))
                own(stt(n2[:, :], n1[:, :], -1.0, n1[:, :], ALU.mult, ALU.max))
                own(stt(n2[:, :], n2[:, :], EPS, en[:, bass.ds(j, 1), :].squeeze(1), ALU.add, ALU.max))
                own(nc.vector.reciprocal(nrm[:, :], n2[:, :]))
                for f in range(2):
                    q = slice(f * S, (f + 1) * S)
                    ins = tt(raw[q].rearrange("p (h a) c -> p h a c", a=2),
                             po[q, :, f * 2 * DH:(f + 1) * 2 * DH].rearrange("p h (a c) -> p h a c", c=DH),
                             nrm[q].rearrange("p (h a) -> p h a", a=2).unsqueeze(3).to_broadcast([S, HH, 2, DH]), ALU.mult)
                ins.then_inc(o_read, 1)
                v.wait_ge(o_read, j + 1)
                own(nc.vector.tensor_reduce(total[:, :], raw[:, :, :], AX.X, ALU.add))
                own(stt(cen[:, s], total[:, :].unsqueeze(2).to_broadcast([P, N, DH]), -1.0 / DH, raw[:, :, :], ALU.mult, ALU.add))
                own(tt(sq[:, :, :], cen[:, s], cen[:, s], ALU.mult))
                assert at == STEPS
                if after(j, 2):
                    v.wait_ge(hr_ready, j - 1)
                nc.vector.tensor_reduce(hv[:, s, :], sq[:, :, :], AX.X, ALU.add).then_inc(sums_ready, 1)

            def scale(j, s, after):
                v.wait_ge(hr_ready, j + 1)
                if after(j, 2):
                    v.wait_ge(hn_ready, j - 1)
                tt(hs[:, s], cen[:, s], hr[:, s, :].unsqueeze(2).to_broadcast([P, N, DH]), ALU.mult).then_inc(scaled, 1)

            def step(n, s, live, after):
                if live(n + 1):
                    product(n + 1, 1 - s, after)
                if live(n - 3):
                    scale(n - 3, 1 - s, after)
                if live(n - 5):
                    v.wait_ge(y_ps, n - 4)
                    x = X[:, bass.ds(n - 5, 1), :].squeeze(1)
                    tt(x, x, p_y[:, 0:C], ALU.add).then_inc(y_added, 1)
                if live(n - 1):
                    normalise(n - 1, 1 - s, after)
            run(v, step)

        @block.tensor
        def _(pe):
            pe.wait_ge(set_up, SET_UP)

            def step(n, s, live, after):
                if live(n + 1):
                    j, t = n + 1, 1 - s
                    if after(j, 2):
                        pe.wait_ge(e_ready, j - 1)
                    pe.wait_ge(left_ready, j + 1)
                    pe.wait_ge(right_ready, j + 1)
                    kit.passed(pe)
                    for b in range(2):
                        nc.tensor.matmul(p_d[t][:, b * 256:(b + 1) * 256], left[t][:, b], right[t][:, b], start=(b == 0),
                                         stop=False, skip_group_check=True)
                    nc.tensor.matmul(p_d[t][:, :], ident2[:, :, :], later[:, :, :], start=False, stop=True,
                                     skip_group_check=True).then_inc(d_ps, 1)
                    pe.wait_ge(qz_ready, j + 1)
                    pe.wait_ge(km_ready, j + 1)
                    if after(j, 2):
                        pe.wait_ge(c_ready, j - 1)
                    for b in range(2):
                        ins = nc.tensor.matmul(p_q[t][:, b * 256:(b + 1) * 256], Qz[t][:, b], Km[t][:, b], start=True, stop=True)
                    ins.then_inc(q_ps, 1)
                if live(n - 1):
                    j = n - 1
                    if after(j, 1):
                        pe.wait_ge(o_read, j)
                    pe.wait_ge(cT_ready, j + 1)
                    for i in range(4):
                        ins = nc.tensor.matmul(p_o[:, i * VW:(i + 1) * VW], CT[:, i * P:(i + 1) * P],
                                               V2[:, bass.ds(2 * j + i // 2, 1), i % 2, :].squeeze(1), start=True, stop=True)
                    ins.then_inc(o_ps, 1)
                if live(n):
                    pe.wait_ge(c_ready, n + 1)
                    if after(n, 1):
                        pe.wait_ge(cT_ready, n)
                    for i in range(4):
                        ins = nc.tensor.transpose(p_t[:, i * P:(i + 1) * P], Cm[s][:, i * P:(i + 1) * P], kit.ident[:, :])
                    ins.then_inc(t_ps, 1)
                if live(n - 4):
                    j = n - 4
                    pe.wait_ge(hn_ready, j + 1)
                    if after(j, 1):
                        pe.wait_ge(y_added, j)
                    kit.passed(pe)
                    for b in range(2):
                        for f in range(2):
                            ins = nc.tensor.matmul(p_y[b * S:(b + 1) * S, f * 64:f * 64 + 64], pick[:, f, :],
                                                   hh[:, s, b * HH:(b + 1) * HH, :], start=True, stop=True)
                    ins.then_inc(y_ps, 1)
            run(pe, step)


def quantised_ffn(kit, tag, out):
    nc = kit.nc
    TAPS = 3
    ROUND = 1.5 * 2.0 ** 23
    with ExitStack() as st:
        sb, _, _ = scoped(nc, st, tag)
        xT = sb("xT", [C, TOK])
        w1t, w2q = sb("w1t", [C, TAPS, FF]), sb("w2q", [P, FK, C], BF16)
        wmean = sb("wmean", [P, 2])
        identb = sb("identb", [P, P], BF16)
        bias_parts, bias_rows = sb("bias_parts", [P, FF], BF16), sb("bias_rows", [P, P], BF16)
        quantise_tokens(kit, tag, xT, w1t, w2q, wmean, identb, bias_rows, bias_parts, TAPS, ROUND)
        quantised_products(kit, tag, out, xT, w1t, w2q, wmean, identb, bias_rows, bias_parts, TAPS, ROUND)


def quantise_tokens(kit, tag, xT, w1t, w2q, wmean, identb, bias_rows, bias_parts, TAPS, ROUND):
    nc, A = kit.nc, kit.A
    with ExitStack() as st:
        sb, ps, sem = scoped(nc, st, tag + "_q")
        w1, w2 = sb("w1", [C, FF]), sb("w2", [P, FK, C])
        taps = sb("taps", [P, TAPS, FF])
        conv_b, part_rows = sb("conv_b", [P, FF]), sb("part_rows", [P, P])
        rest = [conv_b, sb("rest1", [P, FF]), sb("rest2", [P, FF])]
        part = [sb(f"part{i}", [P, FF], BF16) for i in range(3)]
        split = sem("split")
        wsum, wscale, wq = sb("wsum", [P, 2]), sb("wscale", [P, 2]), sb("wq", [P, FF])
        stats, mv, var, rstd = sb("stats", [P, GT, 6]), sb("mv", [P, GT, 2]), sb("var", [P, GT]), sb("rstd", [P, GT])
        xn, xq = [sb(f"xn{i}", [P, GT, C]) for i in range(2)], [sb(f"xq{i}", [P, GT, C]) for i in range(2)]
        amax = sb("amax", [P, GT])
        aback, ascale = [sb(f"aback{i}", [P, GT]) for i in range(2)], [sb(f"ascale{i}", [P, GT]) for i in range(2)]
        p_x, p_w = [ps(f"p_x{i}", [P, 512]) for i in range(2)], ps("p_w", [P, 512])
        weights, w_ps, set_up, dve = sem("weights"), sem("w_ps"), sem("set_up"), sem("dve")
        var_ready, rstd_ready, xn_ready, max_ready, rounded, xq_ready, xT_ps, xT_ready = (
            sem(n) for n in "var_ready rstd_ready xn_ready max_ready rounded xq_ready xT_ps xT_ready".split())
        N_WEIGHTS = 16 * 7
        X = kit.X
        block = st.enter_context(nc.Block())

        def run(engine, step):
            pipelined(engine, (0, NG + 1), NG, step, 2, NG)

        @block.sync
        def _(sp):
            for dst, src in ((w1[:, :], A[f"{tag}_w1"]), (w2[:, :, :], A[f"{tag}_w2"])):
                sp.dma_start(dst, src).then_inc(weights, 16)
            for k in range(TAPS):
                sp.dma_start(taps[:, k, :], A[f"{tag}_conv_w"][k:k + 1, :].to_broadcast([P, FF])).then_inc(weights, 16)
            sp.dma_start(conv_b[:, :], A[f"{tag}_conv_b"].rearrange("(a c) -> a c", a=1).to_broadcast([P, FF])).then_inc(weights, 16)
            sp.dma_start(part_rows[:, :], A["part_rows"]).then_inc(weights, 16)
            sp.wait_ge(weights, N_WEIGHTS)

        @block.gpsimd
        def _(pool):
            def step(n, s, live, after):
                if live(n):
                    inverse_root(nc, pool, var, var_ready, rstd, rstd_ready, kit.minus_half, n)
            run(pool, step)

            pool.wait_ge(weights, N_WEIGHTS)
            at = 0

            def own(ins):
                nonlocal at
                at += 1
                ins.then_inc(split, 1)
                pool.wait_ge(split, at)

            own(nc.gpsimd.memset(bias_parts[:, :], 0.0))
            own(nc.gpsimd.tensor_copy(bias_rows[:, :], part_rows[:, :]))
            for k in range(3):
                own(nc.gpsimd.tensor_copy(part[k][:, :], rest[k][:, :]))
                own(nc.gpsimd.tensor_copy(bias_parts[32 * k:32 * k + 1, :], part[k][32 * k:32 * k + 1, :]))
                if k < 2:
                    own(nc.gpsimd.tensor_tensor(rest[k + 1][:, :], rest[k][:, :], part[k][:, :], ALU.subtract))

        @block.vector
        def _(v):
            tt, ts = nc.vector.tensor_tensor, nc.vector.tensor_scalar
            DVE_STEPS = 5
            wide = lambda t: t[:, :].unsqueeze(2).to_broadcast([P, GT, C])

            def step(n, s, live, after):
                x = lambda j: X[:, bass.ds(n * GT + j, 1), :].squeeze(1)
                if live(n):
                    for j in range(GT):
                        ins = nc.vector.bn_stats(stats[:, j, :], x(j))
                    ins.then_inc(dve, 1)
                    v.wait_ge(dve, DVE_STEPS * n + 1)
                    kit.passed(v)
                    for j in range(GT):
                        ins = nc.vector.bn_aggr(mv[:, j, :], stats[:, j, :])
                    ins.then_inc(dve, 1)
                    v.wait_ge(dve, DVE_STEPS * n + 2)
                    ts(var[:, :], mv[:, :, 1], LN_EPS, None, ALU.add).then_inc(var_ready, 1)
                if live(n - 1):
                    t = 1 - s
                    v.wait_ge(max_ready, n)
                    tt(xn[t][:, :, :], xn[t][:, :, :], wide(ascale[t]), ALU.mult).then_inc(xn_ready, 1)
                    v.wait_ge(xn_ready, n)
                    ts(xn[t][:, :, :], xn[t][:, :, :], ROUND, ROUND, ALU.add, ALU.subtract).then_inc(rounded, 1)
                if live(n):
                    v.wait_ge(rstd_ready, n + 1)
                    if after(n, 2):
                        v.wait_ge(xq_ready, n - 1)
                    for j in range(GT):
                        ins = ts(xn[s][:, j, :], x(j), mv[:, j, 0:1], rstd[:, j:j + 1], ALU.subtract, ALU.mult)
                    ins.then_inc(dve, 1)
                    v.wait_ge(dve, DVE_STEPS * n + 3)
                    nc.vector.tensor_reduce(amax[:, :], xn[s][:, :, :], AX.X, ALU.max, apply_absolute_value=True).then_inc(dve, 1)
                    v.wait_ge(dve, DVE_STEPS * n + 4)
                    ts(aback[s][:, :], amax[:, :], 1e-5, 1.0 / 127.0, ALU.max, ALU.mult).then_inc(dve, 1)
                    v.wait_ge(dve, DVE_STEPS * n + 5)
                    nc.vector.reciprocal(ascale[s][:, :], aback[s][:, :]).then_inc(max_ready, 1)
            run(v, step)

            at = 0

            def setup(ins):
                nonlocal at
                at += 1
                ins.then_inc(set_up, 1)
                v.wait_ge(set_up, at)

            v.wait_ge(weights, N_WEIGHTS)
            both = (w1[:, :], w2[:, :, :].rearrange("p k c -> p (k c)"))
            for n in range(2):
                setup(nc.vector.tensor_reduce(wsum[:, n:n + 1], both[n], AX.X, ALU.add, apply_absolute_value=True))
            setup(nc.vector.tensor_copy(identb[:, :], kit.ident[:, :]))
            v.wait_ge(w_ps, 1)
            setup(ts(wmean[:, :], p_w[:, 0:2], 1.0 / (C * FF), 1e-5, ALU.mult, ALU.max))
            setup(nc.vector.reciprocal(wscale[:, :], wmean[:, :]))

            def ternary(n):
                setup(ts(wq[:, :], both[n], wscale[:, n:n + 1], ROUND, ALU.mult, ALU.add))
                setup(ts(wq[:, :], wq[:, :], ROUND, None, ALU.subtract))
                setup(ts(wq[:, :], wq[:, :], -1.0, 1.0, ALU.max, ALU.min))

            ternary(1)
            setup(nc.vector.tensor_copy(w2q[:, :, :].rearrange("p k c -> p (k c)"), wq[:, :]))
            ternary(0)
            setup(ts(wq[:, :], wq[:, :], wmean[:, 0:1], None, ALU.mult))
            for k in range(TAPS):
                setup(tt(w1t[:, k, :], wq[:, :], taps[:, k, :], ALU.mult))

        @block.scalar
        def _(act):
            def step(n, s, live, after):
                if live(n - 1):
                    t = 1 - s
                    act.wait_ge(rounded, n)
                    if after(n - 1, 2):
                        act.wait_ge(xT_ps, n - 2)
                    for j in range(GT):
                        ins = nc.scalar.activation(xq[t][:, j, :], xn[t][:, j, :], ACT.Copy, scale=aback[t][:, j:j + 1])
                    ins.then_inc(xq_ready, 1)
                    act.wait_ge(xT_ps, n)
                    nc.scalar.activation(xT[:, bass.ds((n - 1) * GROUP, GROUP)], p_x[t][:, :], ACT.Copy).then_inc(xT_ready, 1)
            run(act, step)

        @block.tensor
        def _(pe):
            def step(n, s, live, after):
                if live(n - 1):
                    t = 1 - s
                    pe.wait_ge(xq_ready, n)
                    if after(n - 1, 2):
                        pe.wait_ge(xT_ready, n - 2)
                    for j in range(GT):
                        ins = nc.tensor.transpose(p_x[t][:, j * P:(j + 1) * P], xq[t][:, j, :], kit.ident[:, :])
                    ins.then_inc(xT_ps, 1)
            run(pe, step)
            pe.wait_ge(set_up, 2)
            nc.tensor.matmul(p_w[:, 0:2], kit.ones[:, :], wsum[:, :], start=True, stop=True).then_inc(w_ps, 1)


def quantised_products(kit, tag, out, xT, w1t, w2q, wmean, identb, bias_rows, bias_parts, TAPS, ROUND):
    nc = kit.nc
    with ExitStack() as st:
        sb, ps, sem = scoped(nc, st, tag + "_m")
        xs = [sb(f"xs{i}", [C, TAPS, P]) for i in range(2)]
        h = [sb(f"h{i}", [P, FF]) for i in range(2)]
        hmax, hback, hscale = sb("hmax", [P, 2]), sb("hback", [P, 2]), sb("hscale", [P, 2])
        y_scale = sb("y_scale", [P, TILES])
        minus_round = sb("minus_round", [P, 1])
        hq, hT = sb("hq", [P, 2, FF], BF16), sb("hT", [P, 2, FF], BF16)
        p_h = [ps(f"p_h{i}", [P, FF]) for i in range(2)]
        p_t = [ps(f"p_t{i}", [P, 2 * FF], BF16) for i in range(2)]
        p_y = [ps(f"p_y{i}", [P, 512]) for i in range(2)]
        set_up, dve, max_ready, stored = sem("set_up"), sem("dve"), sem("max_ready"), sem("stored")
        xs_ready, h_ps, s_ready, scaled, hq_ready, hT_ps, hT_ready, y_ps, y_added = (
            sem(n) for n in "xs_ready h_ps s_ready scaled hq_ready hT_ps hT_ready y_ps y_added".split())
        X = kit.X
        block = st.enter_context(nc.Block())

        def run(engine, step):
            pipelined(engine, (-3, TILES + 2), TILES, step, 4, TILES - 4)

        @block.sync
        def _(sp):
            def step(n, s, live, after):
                if live(n - 2):
                    j = n - 2
                    sp.wait_ge(y_added, j + 1)
                    sp.dma_start(out[bass.ds(j * P, P), :], X[:, bass.ds(j, 1), :].squeeze(1)).then_inc(stored, 16)
            run(sp, step)
            sp.wait_ge(stored, 16 * TILES)

        @block.gpsimd
        def _(pool):
            pool.wait_ge(set_up, 3)

            def shift(j, s, after):
                if after(j, 2):
                    pool.wait_ge(h_ps, j - 1)
                t3 = lambda t: t.rearrange("c (b s) -> c b s", s=S)
                src = t3(xT[:, bass.ds(j * P, P)])
                nc.gpsimd.tensor_copy(t3(xs[s][:, 1, :]), src)
                nc.gpsimd.tensor_copy(t3(xs[s][:, 0, :])[:, :, 1:S], src[:, :, 0:S - 1])
                nc.gpsimd.tensor_copy(t3(xs[s][:, 2, :])[:, :, 0:S - 1], src[:, :, 1:S]).then_inc(xs_ready, 1)

            def step(n, s, live, after):
                if live(n + 3):
                    shift(n + 3, 1 - s, after)
            run(pool, step)

        @block.vector
        def _(v):
            ts, stt = nc.vector.tensor_scalar, nc.vector.scalar_tensor_tensor
            for i in range(2):
                nc.vector.memset(xs[i][:, :, :], 0.0).then_inc(set_up, 1)
            nc.vector.memset(minus_round[:, :], -ROUND).then_inc(set_up, 1)
            DVE_STEPS = 2

            def quantise(j, s, after):
                one = lambda t: t[:, s:s + 1]
                v.wait_ge(s_ready, j + 1)
                nc.vector.tensor_reduce(one(hmax), h[s][:, :], AX.X, ALU.max, apply_absolute_value=True).then_inc(max_ready, 1)
                v.wait_ge(max_ready, j + 1)
                ts(one(hback), one(hmax), 1e-5, 1.0 / 127.0, ALU.max, ALU.mult).then_inc(dve, 1)
                v.wait_ge(dve, DVE_STEPS * j + 1)
                nc.vector.reciprocal(one(hscale), one(hback)).then_inc(dve, 1)
                ts(y_scale[:, bass.ds(j, 1)], one(hback), wmean[:, 1:2], None, ALU.mult)
                v.wait_ge(dve, DVE_STEPS * j + 2)
                ts(h[s][:, :], h[s][:, :], one(hscale), ROUND, ALU.mult, ALU.add).then_inc(scaled, 1)

            def step(n, s, live, after):
                if live(n - 2):
                    j = n - 2
                    v.wait_ge(y_ps, j + 1)
                    v.wait_ge(scaled, j + 1)
                    x = X[:, bass.ds(j, 1), :].squeeze(1)
                    stt(x, p_y[s][:, 0:C], y_scale[:, bass.ds(j, 1)], x, ALU.mult, ALU.add).then_inc(y_added, 1)
                if live(n + 1):
                    quantise(n + 1, 1 - s, after)
            run(v, step)

        @block.scalar
        def _(act):
            act.wait_ge(set_up, 3)

            def step(n, s, live, after):
                if live(n + 2):
                    act.wait_ge(h_ps, n + 3)
                    if after(n + 2, 2):
                        act.wait_ge(hq_ready, n + 1)
                    nc.scalar.activation(h[s][:, :], p_h[s][:, :], ACT.Silu).then_inc(s_ready, 1)
                if live(n):
                    act.wait_ge(hT_ps, n + 1)
                    if after(n, 2):
                        act.wait_ge(y_ps, n - 1)
                    nc.scalar.activation(hT[:, s, :], p_t[s][:, 0:FF], ACT.Copy).then_inc(hT_ready, 1)
                if live(n + 1):
                    act.wait_ge(scaled, n + 2)
                    if after(n + 1, 2):
                        act.wait_ge(hT_ps, n)
                    nc.scalar.activation(hq[:, 1 - s, :], h[1 - s][:, :], ACT.Identity, bias=minus_round[:, :]).then_inc(hq_ready, 1)
            run(act, step)

        @block.tensor
        def _(pe):
            def step(n, s, live, after):
                if live(n + 2):
                    j = n + 2
                    pe.wait_ge(xs_ready, j + 1)
                    if after(j, 2):
                        pe.wait_ge(s_ready, j - 1)
                    nc.tensor.matmul(p_h[s][:, :], bias_rows[:, :], bias_parts[:, :], start=True, stop=False)
                    for k in range(TAPS):
                        ins = nc.tensor.matmul(p_h[s][:, :], xs[s][:, k, :], w1t[:, k, :], start=False, stop=(k == TAPS - 1))
                    ins.then_inc(h_ps, 1)
                if live(n - 1):
                    j, t = n - 1, 1 - s
                    pe.wait_ge(hT_ready, j + 1)
                    if after(j, 2):
                        pe.wait_ge(y_added, j - 1)
                    for k in range(FK):
                        ins = nc.tensor.matmul(p_y[t][:, 0:C], hT[:, t, k * P:(k + 1) * P], w2q[:, k, :], start=(k == 0), stop=(k == FK - 1))
                    ins.then_inc(y_ps, 1)
                if live(n):
                    pe.wait_ge(hq_ready, n + 1)
                    if after(n, 2):
                        pe.wait_ge(hT_ready, n - 1)
                    for k in range(FK):
                        ins = nc.tensor.transpose(p_t[s][:, k * P:(k + 1) * P], hq[:, s, k * P:(k + 1) * P], identb[:, :])
                    ins.then_inc(hT_ps, 1)
            run(pe, step)


def build(nc, A, out, phases=range(8)):
    with ExitStack() as ctx:
        kit = Kit(nc, A, ctx)
        load_x(kit)
        steps = [lambda: mha(kit, "L0_xattn"), lambda: moe(kit, "L0_ffn"), lambda: attention(kit, "L1_xattn", "L0_ffn"),
                 lambda: moe(kit, "L1_ffn"), lambda: mlstm(kit, "L2_xattn", "L1_ffn"), lambda: moe(kit, "L2_ffn"), lambda: mha(kit, "L3_xattn", "L2_ffn"),
                 lambda: quantised_ffn(kit, "L3_ffn", out)]
        for n in phases:
            steps[n]()


def arrays_for(inputs):
    a = {k: np.asarray(v) for k, v in inputs.items()}
    r = {}
    r["x"] = np.ascontiguousarray(a["x"].reshape(TOK, C))
    r["ctx"] = np.ascontiguousarray(a["ctx_1024"].reshape(TOK, C))
    r["ctxT"] = np.ascontiguousarray(a["ctx_1024"].reshape(TOK, C).T)
    r["ident"] = np.eye(P, dtype=np.float32)
    r["head_mask"] = (np.arange(P)[:, None] // 8 % 8 == np.arange(8)[None, :]).astype(np.float32)
    r["half_mask8"] = (np.arange(P)[:, None] // 64 == np.arange(C)[None, :] // 8 % 2).astype(np.float32)
    r["not_earlier"] = -np.tril(np.ones((P, P), np.float32))
    r["ones"] = np.ones((P, P), np.float32)
    r["token"] = np.arange(TOK, dtype=np.float32).reshape(TILES, P).T.copy()
    r["iota"] = np.arange(128, dtype=np.float32)[None, :]

    def up(w):
        return np.ascontiguousarray(w.transpose(1, 0, 2))

    def down(w):
        return np.ascontiguousarray(w.reshape(w.shape[0], FK, P, C).transpose(2, 0, 1, 3))

    r["L0_ffn_w1"] = up(a["L0_ffn_expert_w1"].transpose(0, 2, 1))
    r["L0_ffn_w2"] = down(a["L0_ffn_expert_w2"].transpose(0, 2, 1))
    bias = lambda b: np.ascontiguousarray(b.reshape(-1, FK, P).transpose(2, 0, 1))
    r["L0_ffn_b1"], r["L0_ffn_b2"] = bias(a["L0_ffn_expert_b1"]), a["L0_ffn_expert_b2"]
    r["L1_ffn_w1"], r["L1_ffn_w2"] = up(a["L1_ffn_w1"]), down(a["L1_ffn_w2"])
    r["L1_ffn_b1"], r["L1_ffn_b2"] = bias(a["L1_ffn_b1"]), a["L1_ffn_b2"]
    with_fallback = lambda n: np.concatenate([a[f"L2_ffn_{n}"], a[f"L2_ffn_f{n.lower()}"][None]])
    r["L2_ffn_w1"], r["L2_ffn_w2"] = up(with_fallback("W1")), down(with_fallback("W2"))
    r["L2_ffn_b1"], r["L2_ffn_b2"] = bias(with_fallback("b1")), with_fallback("b2")
    r["L0_ffn_router_w"] = np.ascontiguousarray(a["L0_ffn_router_w"].T)
    r["L1_ffn_router_w"] = np.ascontiguousarray(a["L1_ffn_router_w"].T)
    r["L2_ffn_router_w"] = np.ascontiguousarray(a["L2_ffn_Wr"].T)
    r["L1_ffn_router_b"] = a["L1_ffn_router_b"]
    r["L0_ffn_router_b"] = r["L2_ffn_router_b"] = np.zeros(8, np.float32)
    r["fold"] = np.tile(np.eye(S, dtype=np.float32), (2, 1))
    for n in ("q", "k", "v", "o"):
        for layer in ("L0", "L1", "L3"):
            w = a[f"{layer}_xattn_W{n}"]
            r[f"{layer}_xattn_W{n}"] = w if layer == "L3" else np.ascontiguousarray(w.T)
            r[f"{layer}_xattn_b{n}"] = a[f"{layer}_xattn_b{n}"]
    gate_w = np.zeros((C, 3, P), np.float32)
    gate_w[:, :, 0:8] = a["L2_xattn_igate_w"].reshape(8, 3, C).transpose(2, 1, 0)
    gate_w[:, :, 32:40] = a["L2_xattn_fgate_w"].reshape(8, 3, C).transpose(2, 1, 0)
    r["L2_xattn_gate_w"] = gate_w
    r["L2_xattn_igate_b"], r["L2_xattn_fgate_b"], r["L2_xattn_out_w"] = (
        a[f"L2_xattn_{n}"] for n in ("igate_b", "fgate_b", "out_w"))
    heads = np.arange(8)
    r["head_mask16"] = (np.arange(P)[:, None] // 16 % 4 == np.arange(4)[None, :]).astype(np.float32)
    r["half_mask16"] = (np.arange(P)[:, None] // 64 == np.arange(C)[None, :] // 16 % 2).astype(np.float32)
    r["head_of_half"] = (heads[:, None] % 4 == np.arange(4)[None, :]).astype(np.float32)
    r["half_of_head"] = (heads[:, None] // 4 == np.arange(2)[None, :]).astype(np.float32)
    r["minus_half_of_head"] = -r["half_of_head"]
    r["later"] = np.where(np.arange(S)[:, None] < np.arange(S)[None, :], np.float32(-2.0 ** 100), np.float32(0))
    r["L3_ffn_w1"] = np.ascontiguousarray(a["L3_ffn_w1"].T)
    r["L3_ffn_w2"] = np.ascontiguousarray(a["L3_ffn_w2"].T.reshape(FK, P, C).transpose(1, 0, 2))
    r["L3_ffn_conv_w"] = np.ascontiguousarray(a["L3_ffn_conv_w"][:, 0, :].T)
    r["L3_ffn_conv_b"] = a["L3_ffn_conv_b"]
    r["part_rows"] = np.zeros((P, P), np.float32)
    r["part_rows"][0:3 * 32:32] = 1.0
    return r


def kernel(**inputs):
    import concourse.bacc as bacc
    from concourse.bass_utils import run_bass_kernel_spmd

    nc = bacc.Bacc("TRN2", target_bir_lowering=False, num_devices=1)
    arrays, A = {}, {}
    for name, a in arrays_for(inputs).items():
        arrays[f"in_{name}_dram"] = a
        A[name] = nc.dram_tensor(f"in_{name}_dram", a.shape, mybir.dt.from_np(a.dtype), kind="ExternalInput").ap()
    out = nc.dram_tensor("out_0_dram", (TOK, C), FP32, kind="ExternalOutput").ap()
    build(nc, A, out)
    result = run_bass_kernel_spmd(nc, [arrays], core_ids=[0])
    return result.results[0]["out_0_dram"].reshape(B, S, C)
```
